# Optimizing a Trainium2 kernel written in Bass

```python
import numpy as np
import jax
import jax.numpy as jnp

def _softmax(x, axis=-1):
    return jax.nn.softmax(x, axis=axis)

def _gelu(x):
    return jax.nn.gelu(x, approximate=True)

def _silu(x):
    return jax.nn.silu(x)

def _sigmoid(x):
    return jax.nn.sigmoid(x)

def _layernorm(x, axis=-1, eps=1e-05):
    m = jnp.mean(x, axis=axis, keepdims=True)
    v = jnp.var(x, axis=axis, keepdims=True)
    return (x - m) / jnp.sqrt(v + eps)

def _scatter_add(tgt, idx, src, axis=0):
    return tgt.at[idx].add(src)

def _segment_sum(src, seg, n):
    return jax.ops.segment_sum(src, seg, n)
kernel_name = 'mk_prb_d1_jaxref_r8_b359a5'

def setup_inputs(seed: int=0):
    np.random.seed(seed)
    _w = jnp.asarray

    def _L0_attn_setup():
        import math
        import jax, jax.numpy as jnp
        import numpy as np
        D_MODEL = 128
        D_STATE = 64
        D_CONV = 4
        HEADDIM = 64
        EXPAND = 2
        NGROUPS = 1
        CHUNK = 64
        LORA = 48
        THETA_CLIP = math.pi / 2
        D_INNER = EXPAND * D_MODEL
        NHEADS = D_INNER // HEADDIM
        NBLK = D_STATE // 2
        CONV_DIM = D_INNER + 2 * NGROUPS * D_STATE
        D_IN_PROJ = 2 * D_INNER + 2 * NGROUPS * D_STATE + NHEADS
        BATCH, SEQ = (2, 256)
        RMS_EPS = 1e-05

        def _forward(x, in_proj_w, conv_w, conv_b, dt_bias, lambda_base, theta_base, theta_w1, theta_w2, viscosity_eta, D, norm_w, out_proj_w):
            Bsz, L, _ = x.shape
            zxbcdt = x @ in_proj_w.T
            z = zxbcdt[..., :D_INNER]
            xBC = zxbcdt[..., D_INNER:D_INNER + CONV_DIM]
            dt = jax.nn.softplus(zxbcdt[..., -NHEADS:] + dt_bias)
            xp = jnp.pad(xBC, ((0, 0), (D_CONV - 1, 0), (0, 0)))
            conv = conv_b
            for k in range(D_CONV):
                conv = conv + xp[:, k:k + L, :] * conv_w[:, k]
            xBC = jax.nn.silu(conv)
            x_ssm = xBC[..., :D_INNER].reshape(Bsz, L, NHEADS, HEADDIM)
            Bg = xBC[..., D_INNER:D_INNER + NGROUPS * D_STATE].reshape(Bsz, L, NGROUPS, D_STATE)
            Cg = xBC[..., D_INNER + NGROUPS * D_STATE:].reshape(Bsz, L, NGROUPS, D_STATE)
            rep = NHEADS // NGROUPS
            Bh = jnp.repeat(Bg, rep, axis=2)
            Ch = jnp.repeat(Cg, rep, axis=2)
            B_c = jax.lax.complex(Bh[..., 0::2], Bh[..., 1::2])
            C_c = jax.lax.complex(Ch[..., 0::2], Ch[..., 1::2])
            lora = jnp.tanh(x @ theta_w1) @ theta_w2
            theta = jnp.clip(theta_base[None, None] + lora.reshape(Bsz, L, NHEADS, NBLK), -THETA_CLIP, THETA_CLIP)
            lambda_eff = lambda_base[None, None] + viscosity_eta[None, None] * theta ** 2
            log_z = jax.lax.complex(-lambda_eff * dt[..., None], theta * dt[..., None])
            x_disc = x_ssm * dt[..., None]
            Nc = L // CHUNK

            def chunkify(a):
                return a.reshape(Bsz, Nc, CHUNK, *a.shape[2:]).swapaxes(0, 1)
            mask = jnp.tril(jnp.ones((CHUNK, CHUNK), bool))[None, :, :, None, None]
            state0 = jnp.zeros((Bsz, NHEADS, HEADDIM, NBLK), jnp.complex64)

            def step(state, inp):
                lz, bc, cc, xc = inp
                cumlog = jnp.cumsum(lz, axis=1)
                diff = cumlog[:, :, None] - cumlog[:, None, :]
                real = jnp.where(mask, diff.real, -60.0)
                A = jnp.where(mask, jnp.exp(jax.lax.complex(real, diff.imag)), 0.0)
                scaled_B = A * bc[:, :, None]
                S_intra = jnp.einsum('btshk,bshp->bthpk', scaled_B, xc.astype(jnp.complex64))
                S_total = jnp.exp(cumlog)[:, :, :, None, :] * state[:, None] + S_intra
                y = jnp.einsum('bthk,bthpk->bthp', cc, S_total).real
                return (S_total[:, -1], y)
            _, ys = jax.lax.scan(step, state0, (chunkify(log_z), chunkify(B_c), chunkify(C_c), chunkify(x_disc)))
            y = ys.swapaxes(0, 1).reshape(Bsz, L, NHEADS, HEADDIM)
            y = y + x_ssm * D[None, None, :, None]
            y = y.reshape(Bsz, L, D_INNER)
            g = y * jax.nn.silu(z)
            g = g * jax.lax.rsqrt(jnp.mean(g * g, axis=-1, keepdims=True) + RMS_EPS) * norm_w
            return g @ out_proj_w.T
        key = jax.random.key(seed)
        ks = jax.random.split(key, 12)
        x = jax.random.normal(ks[0], (BATCH, SEQ, D_MODEL), jnp.float32)
        in_proj_w = jax.random.normal(ks[1], (D_IN_PROJ, D_MODEL), jnp.float32) * 0.02
        conv_w = jax.random.normal(ks[2], (CONV_DIM, D_CONV), jnp.float32) * 0.2
        conv_b = jnp.zeros((CONV_DIM,), jnp.float32)
        dt = jnp.exp(jax.random.uniform(ks[3], (NHEADS,)) * (math.log(0.1) - math.log(0.001)) + math.log(0.001))
        dt = jnp.maximum(dt, 0.0001)
        dt_bias = dt + jnp.log(-jnp.expm1(-dt))
        lambda_base = jax.random.uniform(ks[4], (NHEADS, NBLK), minval=1.0, maxval=16.0)
        theta_base = jax.random.uniform(ks[5], (NHEADS, NBLK), minval=-math.pi / 16, maxval=math.pi / 16)
        theta_w1 = jax.random.normal(ks[6], (D_MODEL, LORA), jnp.float32) * 0.01
        theta_w2 = jax.random.uniform(ks[7], (LORA, NHEADS * NBLK), minval=-0.01, maxval=0.01)
        viscosity_eta = jax.random.normal(ks[8], (NHEADS, NBLK), jnp.float32) * 0.01
        D = jnp.ones((NHEADS,), jnp.float32)
        norm_w = jnp.ones((D_INNER,), jnp.float32)
        out_proj_w = jax.random.normal(ks[9], (D_MODEL, D_INNER), jnp.float32) * 0.02
        return dict(x=x, in_proj_w=in_proj_w, conv_w=conv_w, conv_b=conv_b, dt_bias=dt_bias, lambda_base=lambda_base, theta_base=theta_base, theta_w1=theta_w1, theta_w2=theta_w2, viscosity_eta=viscosity_eta, D=D, norm_w=norm_w, out_proj_w=out_proj_w)
    _L0_attn_in = _L0_attn_setup()

    def _L0_ffn_setup():
        import jax, jax.numpy as jnp
        import numpy as np
        import math
        D_IN = 128
        FEATURES = (512, 512, 128)
        BATCH, SEQ = (8, 256)

        def _conn_dense(kernel_bool, x):
            w = jnp.where(kernel_bool, jnp.float32(1.0), jnp.float32(-1.0))
            return x @ w
        key = jax.random.key(seed)
        kx, kk0, kk1, kk2 = jax.random.split(key, 4)
        x = jax.random.normal(kx, (BATCH, SEQ, D_IN), dtype=jnp.float32)
        k0 = jax.random.randint(kk0, (2 * D_IN, FEATURES[0]), 0, 2).astype(jnp.bool_)
        k1 = jax.random.randint(kk1, (FEATURES[0], FEATURES[1]), 0, 2).astype(jnp.bool_)
        k2 = jax.random.randint(kk2, (FEATURES[1], FEATURES[2]), 0, 2).astype(jnp.bool_)
        s0 = jnp.asarray(1.0 / math.sqrt(2 * D_IN), dtype=jnp.float32)
        s1 = jnp.asarray(1.0 / math.sqrt(FEATURES[0]), dtype=jnp.float32)
        s2 = jnp.asarray(1.0 / math.sqrt(FEATURES[1]), dtype=jnp.float32)
        return {'x': x, 'k0': k0, 'k1': k1, 'k2': k2, 's0': s0, 's1': s1, 's2': s2}
    _L0_ffn_in = _L0_ffn_setup()
    _d = {'L0_attn_x': _L0_attn_in['x'], 'L0_attn_in_proj_w': _L0_attn_in['in_proj_w'], 'L0_attn_conv_w': _L0_attn_in['conv_w'], 'L0_attn_conv_b': _L0_attn_in['conv_b'], 'L0_attn_dt_bias': _L0_attn_in['dt_bias'], 'L0_attn_lambda_base': _L0_attn_in['lambda_base'], 'L0_attn_theta_base': _L0_attn_in['theta_base'], 'L0_attn_theta_w1': _L0_attn_in['theta_w1'], 'L0_attn_theta_w2': _L0_attn_in['theta_w2'], 'L0_attn_viscosity_eta': _L0_attn_in['viscosity_eta'], 'L0_attn_D': _L0_attn_in['D'], 'L0_attn_norm_w': _L0_attn_in['norm_w'], 'L0_attn_out_proj_w': _L0_attn_in['out_proj_w'], 'L0_ffn_k0': _L0_ffn_in['k0'], 'L0_ffn_k1': _L0_ffn_in['k1'], 'L0_ffn_k2': _L0_ffn_in['k2'], 'L0_ffn_s0': _L0_ffn_in['s0'], 'L0_ffn_s1': _L0_ffn_in['s1'], 'L0_ffn_s2': _L0_ffn_in['s2']}
    _x0 = _d['L0_attn_x']
    _d['L0_attn_x'] = jax.random.normal(jax.random.fold_in(jax.random.key(seed), 1), (8, 512, 128), dtype=_x0.dtype)
    del _x0
    return _d

def reference(L0_attn_x, L0_attn_in_proj_w, L0_attn_conv_w, L0_attn_conv_b, L0_attn_dt_bias, L0_attn_lambda_base, L0_attn_theta_base, L0_attn_theta_w1, L0_attn_theta_w2, L0_attn_viscosity_eta, L0_attn_D, L0_attn_norm_w, L0_attn_out_proj_w, L0_ffn_k0, L0_ffn_k1, L0_ffn_k2, L0_ffn_s0, L0_ffn_s1, L0_ffn_s2):

    def _L0_attn_ref(x, in_proj_w, conv_w, conv_b, dt_bias, lambda_base, theta_base, theta_w1, theta_w2, viscosity_eta, D, norm_w, out_proj_w):
        import math
        import jax, jax.numpy as jnp
        import numpy as np
        D_MODEL = 128
        D_STATE = 64
        D_CONV = 4
        HEADDIM = 64
        EXPAND = 2
        NGROUPS = 1
        CHUNK = 64
        LORA = 48
        THETA_CLIP = math.pi / 2
        D_INNER = EXPAND * D_MODEL
        NHEADS = D_INNER // HEADDIM
        NBLK = D_STATE // 2
        CONV_DIM = D_INNER + 2 * NGROUPS * D_STATE
        D_IN_PROJ = 2 * D_INNER + 2 * NGROUPS * D_STATE + NHEADS
        BATCH, SEQ = (2, 256)
        RMS_EPS = 1e-05

        def _forward(x, in_proj_w, conv_w, conv_b, dt_bias, lambda_base, theta_base, theta_w1, theta_w2, viscosity_eta, D, norm_w, out_proj_w):
            Bsz, L, _ = x.shape
            zxbcdt = x @ in_proj_w.T
            z = zxbcdt[..., :D_INNER]
            xBC = zxbcdt[..., D_INNER:D_INNER + CONV_DIM]
            dt = jax.nn.softplus(zxbcdt[..., -NHEADS:] + dt_bias)
            xp = jnp.pad(xBC, ((0, 0), (D_CONV - 1, 0), (0, 0)))
            conv = conv_b
            for k in range(D_CONV):
                conv = conv + xp[:, k:k + L, :] * conv_w[:, k]
            xBC = jax.nn.silu(conv)
            x_ssm = xBC[..., :D_INNER].reshape(Bsz, L, NHEADS, HEADDIM)
            Bg = xBC[..., D_INNER:D_INNER + NGROUPS * D_STATE].reshape(Bsz, L, NGROUPS, D_STATE)
            Cg = xBC[..., D_INNER + NGROUPS * D_STATE:].reshape(Bsz, L, NGROUPS, D_STATE)
            rep = NHEADS // NGROUPS
            Bh = jnp.repeat(Bg, rep, axis=2)
            Ch = jnp.repeat(Cg, rep, axis=2)
            B_c = jax.lax.complex(Bh[..., 0::2], Bh[..., 1::2])
            C_c = jax.lax.complex(Ch[..., 0::2], Ch[..., 1::2])
            lora = jnp.tanh(x @ theta_w1) @ theta_w2
            theta = jnp.clip(theta_base[None, None] + lora.reshape(Bsz, L, NHEADS, NBLK), -THETA_CLIP, THETA_CLIP)
            lambda_eff = lambda_base[None, None] + viscosity_eta[None, None] * theta ** 2
            log_z = jax.lax.complex(-lambda_eff * dt[..., None], theta * dt[..., None])
            x_disc = x_ssm * dt[..., None]
            Nc = L // CHUNK

            def chunkify(a):
                return a.reshape(Bsz, Nc, CHUNK, *a.shape[2:]).swapaxes(0, 1)
            mask = jnp.tril(jnp.ones((CHUNK, CHUNK), bool))[None, :, :, None, None]
            state0 = jnp.zeros((Bsz, NHEADS, HEADDIM, NBLK), jnp.complex64)

            def step(state, inp):
                lz, bc, cc, xc = inp
                cumlog = jnp.cumsum(lz, axis=1)
                diff = cumlog[:, :, None] - cumlog[:, None, :]
                real = jnp.where(mask, diff.real, -60.0)
                A = jnp.where(mask, jnp.exp(jax.lax.complex(real, diff.imag)), 0.0)
                scaled_B = A * bc[:, :, None]
                S_intra = jnp.einsum('btshk,bshp->bthpk', scaled_B, xc.astype(jnp.complex64))
                S_total = jnp.exp(cumlog)[:, :, :, None, :] * state[:, None] + S_intra
                y = jnp.einsum('bthk,bthpk->bthp', cc, S_total).real
                return (S_total[:, -1], y)
            _, ys = jax.lax.scan(step, state0, (chunkify(log_z), chunkify(B_c), chunkify(C_c), chunkify(x_disc)))
            y = ys.swapaxes(0, 1).reshape(Bsz, L, NHEADS, HEADDIM)
            y = y + x_ssm * D[None, None, :, None]
            y = y.reshape(Bsz, L, D_INNER)
            g = y * jax.nn.silu(z)
            g = g * jax.lax.rsqrt(jnp.mean(g * g, axis=-1, keepdims=True) + RMS_EPS) * norm_w
            return g @ out_proj_w.T
        return _forward(x, in_proj_w, conv_w, conv_b, dt_bias, lambda_base, theta_base, theta_w1, theta_w2, viscosity_eta, D, norm_w, out_proj_w)

    def _L0_ffn_ref(x, k0, k1, k2, s0, s1, s2):
        import jax, jax.numpy as jnp
        import numpy as np
        import math
        D_IN = 128
        FEATURES = (512, 512, 128)
        BATCH, SEQ = (8, 256)

        def _conn_dense(kernel_bool, x):
            w = jnp.where(kernel_bool, jnp.float32(1.0), jnp.float32(-1.0))
            return x @ w
        h = jnp.concatenate([x, -x], axis=-1)
        h = s0 * _conn_dense(k0, h)
        h = jax.nn.relu(h) * 2
        h = s1 * _conn_dense(k1, h)
        h = jax.nn.relu(h) * 2
        h = s2 * _conn_dense(k2, h)
        return h
    x = L0_attn_x
    xn = _layernorm(x, axis=-1)
    x = x + _L0_attn_ref(xn, L0_attn_in_proj_w, L0_attn_conv_w, L0_attn_conv_b, L0_attn_dt_bias, L0_attn_lambda_base, L0_attn_theta_base, L0_attn_theta_w1, L0_attn_theta_w2, L0_attn_viscosity_eta, L0_attn_D, L0_attn_norm_w, L0_attn_out_proj_w) + _L0_ffn_ref(xn, L0_ffn_k0, L0_ffn_k1, L0_ffn_k2, L0_ffn_s0, L0_ffn_s1, L0_ffn_s2)
    return x

_drawn_inputs = setup_inputs


def setup_inputs(seed=0):
    import zlib

    import numpy as np

    out = dict(_drawn_inputs(seed))
    spreads = {'L0_attn_conv_b': (0.0, 0.1), 'L0_attn_D': (1.0, 0.6), 'L0_attn_norm_w': (1.0, 0.597)}
    factors = {'L0_attn_dt_bias': 64.0,
     'L0_attn_lambda_base': 8.0,
     'L0_attn_theta_base': 8.0,
     'L0_attn_theta_w1': 8.0,
     'L0_attn_theta_w2': 8.0,
     'L0_attn_viscosity_eta': 8.0}
    for name, (base, spread) in spreads.items():
        noise = np.random.default_rng([zlib.crc32(name.encode()), seed]).standard_normal(out[name].shape)
        drawn = base * np.exp(spread * noise) if base else spread * noise
        out[name] = jnp.asarray(drawn.astype(out[name].dtype))
    for name, factor in factors.items():
        out[name] = (out[name] * factor).astype(out[name].dtype)
    return out
```

```python
import math
from contextlib import ExitStack

import numpy as np

import concourse.bass as bass
from concourse import mybir

ALU = mybir.AluOpType
ACT = mybir.ActivationFunctionType
AX_X = mybir.AxisListType.X
F32 = mybir.dt.float32
F16 = mybir.dt.float16
U8 = mybir.dt.uint8
I32 = mybir.dt.int32

SEQS, T, D = 8, 512, 128
INNER, HEADS, HEAD, BLK = 256, 4, 64, 32
STATE = 2 * BLK
TAPS = 4
LORA = 48
CH = 128
NCH = T // CH
MLP = 512
MT = MLP // 128
EPS = 1e-5
CLIP = math.pi / 2
XSCALE = 16.0
SUB = 64
NSUB = T // SUB
LEVELS = [1, 2, 4, 8, 16, 32]
SAFE = 80.0
MEAN = 1 / (2 * math.sqrt(INNER))
ROUND = 1.5 * 2.0 ** 23
SETUP = 47
TURN = 6.2831850
LOG1P_TERMS = 9


def view(t, part, parts, offset, dims):
    pitch = t[:].ap[0][0]
    return bass.AP(t, part * pitch + offset, [[pitch, parts], *dims])


CONST_PARTS = {}


def constants():
    p = np.arange(128)
    parts = {}
    parts["ident"] = np.eye(128)
    s_, t_ = p[:, None], p[None, :]
    parts["causal"] = (s_ <= t_) * 1.0
    parts["restart"] = np.tile((np.arange(T) % SUB != 0) * 1.0, (128, 1))
    parts["ones"] = np.ones((128, T))
    bre, bim, cre, cim = 0, 1, STATE, STATE + 1
    for name, rows in (("bcol", (bre, bim, bre, bim)), ("ccol", (cre, cim, cim, cre)),
                       ("bre", (bre,) * 4), ("bim", (bim,) * 4), ("cre", (cre,) * 4), ("cim", (cim,) * 4)):
        sel = np.zeros((128, 128))
        for col in range(128):
            sel[rows[col // BLK] + 2 * (col % BLK), col] = 0.5
        parts[name] = sel
    for name, signs in (("cbre", (1, -1, 0, 0)), ("cbim", (0, 0, 1, 1))):
        parts[name] = np.array([[signs[r // BLK] * (r % BLK == col % BLK) for col in range(128)] for r in range(128)])
    parts["heads"] = (p[:, None] // BLK == np.arange(INNER)[None, :] // HEAD) * 1.0
    for m in LEVELS:
        t = np.array([a + m + i for a in range(0, CH, 2 * m) for i in range(m)])
        parts[f"level{m}"] = ((p[:, None] // (2 * m) == t[None, :] // (2 * m)) & (p[:, None] % (2 * m) < m)) * 1.0
    at = 0
    for name, a in parts.items():
        CONST_PARTS[name] = (at, at + a.shape[1])
        at += a.shape[1]
    return np.concatenate(list(parts.values()), 1).astype(np.float32)


CONSTANTS = constants()


class Signal:

    def __init__(self, ctx, nc, name, steps):
        self.sem = ctx.enter_context(nc.semaphore(name))
        self.steps = steps

    def at(self, b, step):
        return b * self.steps + step

    def done(self, b):
        return b * self.steps + self.steps


def build(nc, mode, a, consts, out):
    fast = mode == "fast"
    ctx = ExitStack()
    with ctx:
        def sb(name, shape, dt=F32):
            return ctx.enter_context(nc.sbuf_tensor(name, shape, dt))

        def sem(name):
            return ctx.enter_context(nc.semaphore(name))

        def signal(name, steps):
            return Signal(ctx, nc, name, steps)

        bank = [ctx.enter_context(nc.psum_tensor(f"bank{i}", [128, 512], F32)) for i in range(8)]

        const = sb("const", [128, CONSTANTS.shape[1]])

        def c_(name):
            lo, hi = CONST_PARTS[name]
            return const[:, lo:hi]

        ident = c_("ident")
        win = sb("win", [128, 5, D])
        wdt = sb("wdt", [HEADS, D])
        wout = sb("wout", [128, INNER])
        cw = sb("cw", [128, 3, TAPS])
        cb_row = sb("cb_row", [1, INNER])
        cb_col = sb("cb_col", [128, 1])
        dtb = sb("dtb", [128, HEADS])
        skip = sb("skip", [128, HEADS])
        lam = sb("lam", [128, 1])
        base = sb("base", [128, 1])
        eta = sb("eta", [128, 1])
        normw = sb("normw", [128, 2])
        tw1 = sb("tw1", [128, LORA])
        tw2 = sb("tw2", [LORA, 128])
        k0u = sb("k0u", [128, 2, MLP], U8)
        k1u = sb("k1u", [128, MT, MLP], U8)
        k2u = sb("k2u", [128, MT, D], U8)
        s012 = sb("s012", [128, 3])
        XW = sb("XW", [128, TAPS, INNER])
        BCW = sb("BCW", [128, TAPS, 128])
        ZW = sb("ZW", [128, INNER])
        OW = sb("OW", [128, 2, D])
        DTW = sb("DTW", [128, HEADS])
        w0d = sb("w0d", [128, MLP])
        W0 = sb("W0", [128, MLP], F16)
        W1 = sb("W1", [128, MT, MLP], F16)
        W2 = sb("W2", [128, MT, D], F16)
        sign = sb("sign", [128, 3])
        negs = sb("negs", [128, 3])
        abss = sb("abss", [128, 3])
        w1s = sb("w1s", [128, 2])
        w0s = sb("w0s", [128, 1])
        sffn = sb("sffn", [128, 1])
        neglam = sb("neglam", [128, 1])
        negeta = sb("negeta", [128, 1])
        hcb = sb("hcb", [128, 1])
        hskip = sb("hskip", [128, HEADS])
        halfpi = sb("halfpi", [128, 1])
        minus_half = sb("minus_half", [128, NCH])
        eps4 = sb("eps4", [128, NCH])
        carrier = sb("carrier", [128, 2])
        ones = sb("ones", [1, 128])

        xtok = [sb(f"xtok{p}", [128, NCH, D]) for p in range(2)]
        osb = [sb(f"osb{p}", [128, NCH, D]) for p in range(2)]
        st6 = sb("st6", [128, NCH, 6])
        mv = sb("mv", [128, NCH, 2])
        vare = sb("vare", [128, NCH])
        rstd = sb("rstd", [128, NCH])
        xn = sb("xn", [128, NCH, D])
        PAD = TAPS - 1
        xnT = sb("xnT", [128, PAD + T])
        xh = sb("xh", [128, T], F16)
        xl = sb("xl", [128, T], F16)
        th1 = sb("th1", [LORA, T])
        x2 = sb("x2", [128, NCH, INNER])
        thx = sb("thx", [128, NCH, INNER])
        z2 = sb("z2", [128, NCH, INNER])
        thz = sb("thz", [128, NCH, INNER])
        bcp = sb("bcp", [128, T])
        thb = sb("thb", [128, T])
        bc2 = sb("bc2", [128, T])
        dv = sb("dv", [128, NCH, HEADS])
        dneg = sb("dneg", [128, NCH, HEADS])
        de = sb("de", [128, NCH, HEADS])
        ds = sb("ds", [128, NCH, HEADS])
        dq = sb("dq", [128, NCH, HEADS])
        dacc = sb("dacc", [128, NCH, HEADS])
        dt = sb("dt", [128, NCH, HEADS])
        hdt = sb("hdt", [128, NCH, HEADS])
        dtb32 = sb("dtb32", [128, NCH, HEADS, BLK])
        xd = sb("xd", [128, NCH, INNER])
        theta = sb("theta", [128, T])
        sq = sb("sq", [128, T])
        nl = sb("nl", [128, T])
        lz = sb("lz", [128, T])
        ph = sb("ph", [128, T])
        cum3 = sb("cum3", [128, 3, T])
        phl = sb("phl", [128, T])
        pend = sb("pend", [128, NSUB])
        pint = sb("pint", [128, NSUB])
        poff = sb("poff", [128, NSUB])
        pabs = sb("pabs", [128, T])
        Xre = sb("Xre", [128, 2, T])
        Xim = sb("Xim", [128, 2, T])
        pcs, psn = Xre[:, 0, :], Xim[:, 0, :]
        bcol = sb("bcol", [128, T])
        prod = sb("prod", [128, T])
        be = sb("be", [128, 2, NSUB])
        ec = sb("ec", [128, T])
        es = sb("es", [128, T])
        tmpa = sb("tmpa", [128, T])
        tmpb = sb("tmpb", [128, T])
        E = sb("E", [128, T])
        E2 = sb("E2", [128, T])
        aend = sb("aend", [128, NSUB])
        Kre = sb("Kre", [128, T])
        Kim = sb("Kim", [128, T])
        Qre = sb("Qre", [128, T])
        Qim = sb("Qim", [128, T])
        Bre = sb("Bre", [128, T])
        Bim = sb("Bim", [128, T])
        Ure = sb("Ure", [128, T])
        Uim = sb("Uim", [128, T])
        GT = sb("GT", [128, HEADS, NCH, CH])
        scaled = GT[:].rearrange("p h c t -> p (h c) t")
        KT = sb("KT", [128, NCH, 2, 128])
        NST = NCH - 1 if fast else NSUB - 1
        Sst = [sb(f"S{c}", [128, 2, INNER]) for c in range(3)]
        stmp = sb("stmp", [128, 2, INNER])
        dx = sb("dx", [128, NCH, INNER])
        y1 = sb("y1", [128, NCH, INNER])
        g2 = sb("g2", [128, NCH, INNER])
        gsq = sb("gsq", [128, INNER])
        ssq = sb("ssq", [128, NCH])
        msq = sb("msq", [128, NCH])
        rms = sb("rms", [128, NCH])
        gT = sb("gT", [128, 2, T])
        o1 = sb("o1", [128, NCH, D])
        h0h = sb("h0h", [128, MT, T], F16)
        h0l = sb("h0l", [128, MT, T], F16)
        h1h = sb("h1h", [128, MT, T], F16)
        h1l = sb("h1l", [128, MT, T], F16)
        if not fast:
            diff, arg = tmpa, tmpb
            Wre, Wim = Ure, Uim

        weights = sem("weights_loaded")
        x_in = [sem(f"x_loaded{p}") for p in range(2)]
        o_out = [sem(f"out_stored{p}") for p in range(2)]
        set_dve = sem("setup_vector")
        set_pe = sem("setup_transposes")
        set_act = sem("setup_copies")
        set_pool = sem("setup_pool")
        s_ln = signal("layernorm", 3 * NCH + 2)
        s_xl = signal("xn_low_half", 1)
        s_dt = signal("dt_steps", 11 + LOG1P_TERMS)
        s_silu = signal("silu", 5)
        s_xd = signal("x_times_dt", 1)
        s_ph = signal("phases", 15)
        s_bc = signal("products_of_B_and_C", 3)
        s_tail = signal("K_exponents", 1)
        s_kq = signal("decayed", 4 + 12 + 6)
        s_g = signal("G_in_sbuf", HEADS if fast else HEADS + (HEADS + 1) * len(LEVELS))
        s_lvarg = signal("level_exponents", 1 if fast else len(LEVELS))
        s_lvmul = signal("level_products", 2 if fast else 2 * len(LEVELS))
        s_st = signal("states", NST if fast else 2 * NST)
        s_gate = signal("gated", 4)
        s_fin = signal("final", 2 * NCH)
        s_h0l = signal("h0_low_half", MT)
        s_h1l = signal("h1_low_half", MT)
        s_rstd = signal("rstd", 1)
        s_dx = signal("skip_term", 1)
        s_rms = signal("rms", 1)
        a_xnT = signal("xnT_copied", 2)
        a_tanh = signal("tanhs", 7)
        a_dte = signal("dt_exp", 1)
        a_sq = signal("theta_squared", 1)
        a_trig = signal("sin_cos", 2)
        a_exp = signal("decay_exps", 3)
        a_lv = signal("level_exps", 1 if fast else len(LEVELS))
        a_bc = signal("B_copied", 1)
        a_kt = signal("KT_copied", 2)
        a_ssq = signal("squares", NCH)
        a_gT = signal("gT_copied", 2)
        a_h0 = signal("h0_high_half", MT)
        a_h1 = signal("h1_high_half", MT)
        t_T = signal("xn_transposed", 1)
        t_dt = signal("dt_projected", 1)
        t_l1 = signal("lora1", 1)
        t_x = signal("x_projected", 1)
        t_bc = signal("bc_projected", 1)
        t_z = signal("z_projected", 1)
        t_l2 = signal("lora2", 1)
        t_dtr = signal("dt_spread", 1)
        t_bcc = signal("bc_in_columns", 1)
        t_sel = signal("bc_spread", 1)
        t_h0 = signal("mlp0", MT)
        t_h1 = signal("mlp1", MT)
        t_mo = signal("mlp_out", 1)
        t_g = signal("G_products", 1 if fast else 1 + len(LEVELS))
        t_kt = signal("K_transposed", 1)
        t_s = signal("state_products", NST)
        t_y = signal("y_products", 2)
        t_gT = signal("g_transposed", 1)
        t_o = signal("out_projected", 1)

        x_dram = a["x"].rearrange("b (c p) d -> b p c d", p=128)
        out_dram = out.rearrange("b (c p) d -> b p c d", p=128)

        def col(ap1d, n=128):
            return ap1d.rearrange("(p o) -> p o", o=1)

        def row_all(ap1d, n):
            return bass.AP(ap1d.tensor, ap1d.offset, [[0, 128], [1, n]])

        loads = [
            (const[:], consts),
            (win[:], a["in_proj_w"][0:640, :].rearrange("(t p) d -> p t d", p=128)),
            (wdt[:], a["in_proj_w"][640:644, :]),
            (wout[:], a["out_proj_w"]),
            (cw[:], a["conv_w"].rearrange("(t p) k -> p t k", p=128)),
            (cb_row[:], a["conv_b"][0:INNER].rearrange("(o c) -> o c", o=1)),
            (cb_col[:], col(a["conv_b"][INNER:INNER + 128])),
            (dtb[:], row_all(a["dt_bias"], HEADS)),
            (skip[:], row_all(a["D"], HEADS)),
            (lam[:], a["lambda_base"].rearrange("h (k o) -> (h k) o", o=1)),
            (base[:], a["theta_base"].rearrange("h (k o) -> (h k) o", o=1)),
            (eta[:], a["viscosity_eta"].rearrange("h (k o) -> (h k) o", o=1)),
            (normw[:], a["norm_w"].rearrange("(t p) -> p t", p=128)),
            (tw1[:], a["theta_w1"]),
            (tw2[:], a["theta_w2"]),
            (k0u[:], a["k0"].rearrange("(t p) f -> p t f", p=128)),
            (k1u[:], a["k1"].rearrange("(t p) f -> p t f", p=128)),
            (k2u[:], a["k2"].rearrange("(t p) f -> p t f", p=128)),
            (s012[:, 0:1], row_all(a["s0"], 1)),
            (s012[:, 1:2], row_all(a["s1"], 1)),
            (s012[:, 2:3], row_all(a["s2"], 1)),
        ]
        block = ctx.enter_context(nc.Block())

        @block.sync
        def _(sp):
            with nc.allow_non_contiguous_dma("small columns of weights"):
                for p in range(2):
                    sp.dma_start(xtok[p][:], x_dram[p]).then_inc(x_in[p], 16)
                for dst, src in loads:
                    sp.dma_start(dst, src).then_inc(weights, 16)

                def store(b, p):
                    sp.wait_ge(s_fin.sem, s_fin.done(b))
                    sp.dma_start(out_dram[b], osb[p][:]).then_inc(o_out[p], 16)

                with sp.Fori(0, SEQS // 2 - 1) as i:
                    for p in range(2):
                        b = 2 * i + p
                        store(b, p)
                        sp.dma_start(xtok[p][:], x_dram[b + 2]).then_inc(x_in[p], 16)
                for p in range(2):
                    store(SEQS - 2 + p, p)
                for p in range(2):
                    sp.wait_ge(o_out[p], 16 * (SEQS // 2) + 1)

        @block.vector
        def _(v):
            nd = [0]

            def setup(ins):
                nd[0] += 1
                ins.then_inc(set_dve, 1)
                v.wait_ge(set_dve, nd[0])

            V = nc.vector
            for p in range(2):
                V.memset(carrier[:, p:p + 1], 0.0).then_inc(o_out[p], 1)
            setup(V.memset(xnT[:, 0:PAD], 0.0))
            setup(V.memset(minus_half[:], -0.5))
            setup(V.memset(halfpi[:], math.pi / 2))
            setup(V.memset(ones[:], 1.0))
            setup(V.memset(eps4[:], EPS))
            setup(V.memset(poff[:], 0.0))
            v.wait_ge(weights, 16 * len(loads))
            for k in range(TAPS):
                for t in range(3):
                    setup(V.tensor_scalar(scaled[:, 3 * k + t, :], win[:, 2 + t, :], cw[:, t, k:k + 1], None, ALU.mult))
            setup(V.tensor_scalar(sign[:], s012[:], 0.0, None, ALU.is_gt))
            setup(V.tensor_scalar(negs[:], s012[:], 0.0, None, ALU.is_lt))
            setup(V.tensor_tensor(sign[:], sign[:], negs[:], ALU.subtract))
            setup(V.tensor_tensor(abss[:], sign[:], s012[:], ALU.mult))
            setup(V.tensor_scalar(w0s[:], sign[:, 0:1], 2.0 / XSCALE, None, ALU.mult))
            setup(V.tensor_scalar(w1s[:, 0:1], sign[:, 1:2], 0.5, None, ALU.mult))
            setup(V.tensor_scalar(w1s[:, 1:2], sign[:, 1:2], -0.25, None, ALU.mult))
            setup(V.tensor_tensor(sffn[:], abss[:, 0:1], abss[:, 1:2], ALU.mult))
            setup(V.tensor_scalar(sffn[:], sffn[:], s012[:, 2:3], 16.0, ALU.mult, ALU.mult))
            setup(V.tensor_tensor(w0d[:], k0u[:, 0, :], k0u[:, 1, :], ALU.subtract))
            setup(V.tensor_scalar(W0[:], w0d[:], w0s[:, 0:1], None, ALU.mult))
            setup(V.tensor_scalar(W1[:], k1u[:], w1s[:, 0:1], w1s[:, 1:2], ALU.mult, ALU.add))
            setup(V.tensor_scalar(W2[:], k2u[:], 2.0, -1.0, ALU.mult, ALU.add))
            setup(V.tensor_scalar(neglam[:], lam[:], -1.0, None, ALU.mult))
            setup(V.tensor_scalar(negeta[:], eta[:], -1.0, None, ALU.mult))
            setup(V.tensor_scalar(hcb[:], cb_col[:], 0.5, None, ALU.mult))
            setup(V.tensor_scalar(hskip[:], skip[:], 0.5, None, ALU.mult))
            v.wait_ge(set_pe, 1)
            for k in range(TAPS):
                setup(V.tensor_copy(XW[:, k, :], bank[k][:, 0:INNER]))
                setup(V.tensor_copy(BCW[:, k, :], bank[k][:, INNER:INNER + 128]))
            setup(V.tensor_copy(ZW[:], bank[4][:, 0:INNER]))
            for h in range(2):
                setup(V.tensor_scalar(OW[:, h, :], bank[4][:, 256 + 128 * h:384 + 128 * h], normw[:, h:h + 1], 0.5,
                                      ALU.mult, ALU.mult))
            setup(V.tensor_copy(DTW[:], bank[5][:, 0:HEADS]))

            assert nd[0] == SETUP, nd

            def chain(signal_, b):
                n = [0]

                def step(ins, linked=True):
                    n[0] += 1
                    ins.then_inc(signal_.sem, 1)
                    assert n[0] <= signal_.steps
                    if linked:
                        v.wait_ge(signal_.sem, signal_.at(b, n[0]))
                step.count = n
                return step

            def layernorm(b, p, i):
                v.wait_ge(x_in[p], 16 * i + 16)
                step = chain(s_ln, b)
                for c in range(NCH):
                    step(V.bn_stats(st6[:, c, :], xtok[p][:, c, :]), linked=False)
                v.wait_ge(s_ln.sem, s_ln.at(b, NCH))
                step(V.memset(carrier[:, 0:1], 0.0), linked=False)
                for c in range(NCH):
                    step(V.bn_aggr(mv[:, c, :], st6[:, c, :]), linked=c == NCH - 1)
                step(V.tensor_scalar(vare[:], mv[:, :, 1], EPS, None, ALU.add))
                v.wait_ge(s_rstd.sem, s_rstd.done(b))
                for c in range(NCH):
                    step(V.tensor_scalar(xn[:, c, :], xtok[p][:, c, :], mv[:, c, 0:1], rstd[:, c:c + 1],
                                         ALU.subtract, ALU.mult))

            def xn_low(b):
                v.wait_ge(a_xnT.sem, a_xnT.done(b))
                step = chain(s_xl, b)
                step(V.scalar_tensor_tensor(xl[:], bank[0][:], XSCALE, xh[:], ALU.mult, ALU.subtract))

            def dt_steps(b):
                v.wait_ge(t_dt.sem, t_dt.done(b))
                step = chain(s_dt, b)
                ps = bank[1][:, 0:NCH * HEADS].rearrange("p (c h) -> p c h", h=HEADS)
                bias = view(dtb, 0, 128, 0, [[0, NCH], [1, HEADS]])
                step(V.tensor_tensor(dv[:], ps, bias, ALU.add))
                step(V.scalar_tensor_tensor(dneg[:], dv[:], -1.0, dv[:], ALU.mult, ALU.min))
                v.wait_ge(a_dte.sem, a_dte.done(b))
                step(V.tensor_scalar(ds[:], de[:], 2.0, None, ALU.add))
                step(V.reciprocal(dq[:], ds[:]))
                step(V.tensor_tensor(ds[:], de[:], dq[:], ALU.mult))
                step(V.tensor_tensor(dq[:], ds[:], ds[:], ALU.mult))
                n = LOG1P_TERMS
                step(V.tensor_scalar(dacc[:], dq[:], 1.0 / (2 * n + 1), None, ALU.mult))
                for j in range(n - 1, 0, -1):
                    step(V.scalar_tensor_tensor(dacc[:], dacc[:], 1.0 / (2 * j + 1), dq[:], ALU.add, ALU.mult))
                step(V.scalar_tensor_tensor(dacc[:], dacc[:], 1.0, ds[:], ALU.add, ALU.mult))
                step(V.tensor_scalar(dv[:], dv[:], 0.0, None, ALU.max))
                step(V.scalar_tensor_tensor(dt[:], dacc[:], 2.0, dv[:], ALU.mult, ALU.add))
                step(V.tensor_scalar(hdt[:], dt[:], 0.5, None, ALU.mult))
                step(V.tensor_copy(dtb32[:], view(dt, 0, 128, 0, [[1, NCH * HEADS], [0, BLK]])))
                return step

            def silus(b):
                step = chain(s_silu, b)
                for half in range(2):
                    v.wait_ge(a_tanh.sem, a_tanh.at(b, 2 + half))
                    step(V.scalar_tensor_tensor(x2[:, 2 * half:2 * half + 2, :], thx[:, 2 * half:2 * half + 2, :], 1.0,
                                                bank[2 + half][:], ALU.add, ALU.mult))
                v.wait_ge(a_tanh.sem, a_tanh.at(b, 5))
                step(V.scalar_tensor_tensor(bc2[:], thb[:], 1.0, bcp[:], ALU.add, ALU.mult))
                for half in range(2):
                    v.wait_ge(a_tanh.sem, a_tanh.at(b, 6 + half))
                    step(V.scalar_tensor_tensor(z2[:, 2 * half:2 * half + 2, :], thz[:, 2 * half:2 * half + 2, :], 1.0,
                                                bank[4 + half][:], ALU.add, ALU.mult))

            def x_times_dt(b):
                step = chain(s_xd, b)
                step(V.tensor_tensor(xd[:].rearrange("p c (h e) -> p (c h) e", h=HEADS),
                                     x2[:].rearrange("p c (h e) -> p (c h) e", h=HEADS),
                                     view(hdt, 0, 128, 0, [[1, NCH * HEADS], [0, HEAD]]), ALU.mult))

            def phases(b):
                step = chain(s_ph, b)
                v.wait_ge(t_l2.sem, t_l2.done(b))
                step(V.tensor_scalar(theta[:], bank[1][:], base[:, 0:1], -CLIP, ALU.add, ALU.max))
                step(V.tensor_scalar(theta[:], theta[:], CLIP, None, ALU.min))
                v.wait_ge(a_sq.sem, a_sq.done(b))
                step(V.tensor_scalar(nl[:], sq[:], negeta[:, 0:1], neglam[:, 0:1], ALU.mult, ALU.add))
                v.wait_ge(t_dtr.sem, t_dtr.done(b))
                step(V.tensor_tensor(lz[:], nl[:], bank[0][:], ALU.mult))
                step(V.scalar_tensor_tensor(ph[:], theta[:], 1.0 / (2 * math.pi), bank[0][:], ALU.mult, ALU.mult))
                step(V.tensor_tensor_scan(cum3[:, 0, :], c_("ones" if fast else "restart"), lz[:], 0.0, ALU.mult, ALU.add))
                step(V.tensor_tensor_scan(phl[:], c_("restart"), ph[:], 0.0, ALU.mult, ALU.add))
                step(V.tensor_scalar(cum3[:, 1, :], cum3[:, 0, :], -1.0, None, ALU.mult))
                step(V.tensor_copy(cum3[:, 2, :], cum3[:, 0, :]))
                ends = view(phl, 0, 128, SUB - 1, [[SUB, NSUB]])
                step(V.tensor_scalar(pint[:], ends, ROUND, -ROUND, ALU.add, ALU.add))
                step(V.tensor_tensor(pend[:], ends, pint[:], ALU.subtract))
                step(V.tensor_tensor_scan(poff[:, 1:NSUB], c_("ones")[:, 1:NSUB], pend[:, 0:NSUB - 1], 0.0, ALU.mult, ALU.add))
                step(V.tensor_tensor(phl[:].rearrange("p (c t) -> p c t", t=SUB), phl[:].rearrange("p (c t) -> p c t", t=SUB),
                                     view(poff, 0, 128, 0, [[1, NSUB], [0, SUB]]), ALU.add))
                step(V.tensor_scalar(ph[:], phl[:], ROUND, -ROUND, ALU.add, ALU.add))
                step(V.tensor_tensor(phl[:], phl[:], ph[:], ALU.subtract))
                assert step.count[0] == 15, step.count

            def b_and_c(b):
                step = chain(s_bc, b)
                v.wait_ge(a_bc.sem, a_bc.done(b))
                step(V.tensor_tensor(prod[:], bcol[:], bank[3][:], ALU.mult))
                v.wait_ge(t_sel.sem, t_sel.done(b))
                step(V.tensor_copy(be[:, 0, :], bank[7][:, 0:NSUB]))
                step(V.tensor_copy(be[:, 1, :], bank[7][:, NSUB:2 * NSUB]))

            def k_exponents(b):
                step = chain(s_tail, b)
                if fast:
                    step(V.nop())
                else:
                    step(V.tensor_tensor(diff[:].rearrange("p (c t) -> p c t", t=SUB),
                                         view(cum3, 0, 128, SUB - 1, [[SUB, NSUB], [0, SUB]]),
                                         cum3[:, 1, :].rearrange("p (c t) -> p c t", t=SUB), ALU.add))

            def decayed(b):
                step = chain(s_kq, b)
                v.wait_ge(a_trig.sem, a_trig.done(b))
                v.wait_ge(a_exp.sem, a_exp.done(b))
                step(V.tensor_tensor(Kre[:], pcs, E[:], ALU.mult))
                step(V.tensor_tensor(Kim[:], psn, E[:], ALU.mult))
                step(V.tensor_tensor(ec[:], pcs, E2[:], ALU.mult))
                step(V.tensor_tensor(es[:], psn, E2[:], ALU.mult))
                cbre, cbim, cre, cim = (bank[q][:] for q in (4, 5, 2, 3))
                uc, us = (ec[:], es[:]) if fast else (pcs, psn)
                ure, uim = (Ure[:], Uim[:]) if fast else (Xre[:, 1, :], Xim[:, 1, :])
                for dst, (p1, f1), (p2, f2), op in (
                    (ure, (cbre, uc), (cbim, us), ALU.subtract),
                    (uim, (cbre, us), (cbim, uc), ALU.add),
                    (Qre[:], (cre, ec[:]), (cim, es[:]), ALU.subtract),
                    (Qim[:], (cre, es[:]), (cim, ec[:]), ALU.add),
                ):
                    step(V.tensor_tensor(tmpa[:], p1, f1, ALU.mult))
                    step(V.tensor_tensor(tmpb[:], p2, f2, ALU.mult))
                    step(V.tensor_tensor(dst, tmpa[:], tmpb[:], op))

                def subs(t):
                    return t[:].rearrange("p (c t) -> p c t", t=SUB)

                br = view(be, 0, 128, 0, [[1, NSUB], [0, SUB]])
                bi = view(be, 0, 128, NSUB, [[1, NSUB], [0, SUB]])
                for dst, (p1, f1), (p2, f2), op in (
                    (Bre, (Kre, br), (Kim, bi), ALU.add),
                    (Bim, (Kim, br), (Kre, bi), ALU.subtract),
                ):
                    step(V.tensor_tensor(subs(tmpa), subs(p1), f1, ALU.mult))
                    step(V.tensor_tensor(subs(tmpb), subs(p2), f2, ALU.mult))
                    step(V.tensor_tensor(dst[:], tmpa[:], tmpb[:], op))

            def g_base(b, mask):
                step = g_step[0] = chain(s_g, b)
                v.wait_ge(t_g.sem, t_g.at(b, 1))
                m0 = CONST_PARTS[mask][0]
                for h in range(HEADS):
                    step(V.tensor_tensor(GT[:, h, :, :], bank[2 + h][:].rearrange("p (c t) -> p c t", t=CH),
                                         view(const, 0, 128, m0, [[0, NCH], [1, CH]]), ALU.mult))

            g_step = [None]

            def level_arg(b, n, m, step):
                nb = T // (2 * m)
                step(V.tensor_tensor(view(arg, 0, 128, 0, [[2 * m, nb], [m, 2], [1, m]]),
                                     view(cum3, 0, 128, T, [[2 * m, nb], [T + m, 2], [1, m]]),
                                     view(cum3, 0, 128, m - 1, [[2 * m, nb], [T, 2], [0, m]]), ALU.add))

            def level_mul(b, n, m, step):
                nb = T // (2 * m)
                v.wait_ge(a_lv.sem, a_lv.at(b, n + 1))
                e = view(E, 0, 128, 0, [[2 * m, nb], [m, 2], [1, m]])
                for dst, src in ((Wre, Xre), (Wim, Xim)):
                    step(V.tensor_tensor(view(dst, 0, 128, 0, [[2 * m, nb], [m, 2], [1, m]]),
                                         view(src, 0, 128, 0, [[2 * m, nb], [T + m, 2], [1, m]]), e, ALU.mult), linked=dst is Wre)

            def level_take(b, n, m, step):
                v.wait_ge(t_g.sem, t_g.at(b, 2 + n))
                step(V.memset(carrier[:, 1:2], 0.0), linked=False)
                m0 = CONST_PARTS[f"level{m}"][0]
                nb = CH // (2 * m)
                for h in range(HEADS):
                    dst = view(GT, 0, 128, h * T + m, [[CH, NCH], [2 * m, nb], [1, m]])
                    mask = view(const, 0, 128, m0, [[0, NCH], [1, CH // 2]]).bitcast(I32)
                    src = bank[2 + h][:, 0:T // 2].rearrange("p (c t) -> p c t", t=CH // 2)
                    step(V.copy_predicated(dst, mask, src), linked=h == HEADS - 1)

            def states(b):
                step = chain(s_st, b)
                heads = view(const, 0, 128, CONST_PARTS["heads"][0], [[0, 2], [1, INNER]])
                for c in range(NST):
                    v.wait_ge(t_s.sem, t_s.at(b, c + 1))
                    new, old = Sst[c % 3], Sst[(c - 1) % 3]
                    ps = bank[6][:].rearrange("p (r e) -> p r e", r=2)
                    if fast:
                        step(V.tensor_tensor(new[:], ps, heads, ALU.mult))
                    elif c:
                        step(V.tensor_tensor(stmp[:], ps, heads, ALU.mult))
                        step(V.scalar_tensor_tensor(new[:], old[:], aend[:, c:c + 1], stmp[:], ALU.mult, ALU.add))
                    else:
                        step(V.memset(stmp[:], 0.0))
                        step(V.tensor_tensor(new[:], ps, heads, ALU.mult))

            def gated(b):
                step = chain(s_gate, b)
                v.wait_ge(s_dx.sem, s_dx.done(b))
                for half in range(2):
                    v.wait_ge(t_y.sem, t_y.at(b, half + 1))
                    w = slice(2 * half, 2 * half + 2)
                    step(V.tensor_tensor(y1[:, w, :], dx[:, w, :], bank[half][:].rearrange("p (c e) -> p c e", e=INNER), ALU.add))
                    step(V.tensor_tensor(g2[:, w, :], y1[:, w, :], z2[:, w, :], ALU.mult))

            def mean_square(b):
                v.wait_ge(a_ssq.sem, a_ssq.done(b))

            def low_half(sig, high, lo, ready, b):
                step = chain(sig, b)
                for f in range(MT):
                    v.wait_ge(ready.sem, ready.at(b, f + 1))
                    step(V.scalar_tensor_tensor(lo[:, f, :], bank[6 + f % 2][:], 0.0, high[:, f, :], ALU.max, ALU.subtract))

            def final(b, p, i):
                step = chain(s_fin, b)
                v.wait_ge(t_mo.sem, t_mo.done(b))
                v.wait_ge(o_out[p], 16 * i + 1)
                for c in range(NCH):
                    step(V.scalar_tensor_tensor(o1[:, c, :], bank[7][:, 128 * c:128 * c + 128], sffn[:, 0:1],
                                                xtok[p][:, c, :], ALU.mult, ALU.add))
                v.wait_ge(t_o.sem, t_o.done(b))
                v.wait_ge(s_rms.sem, s_rms.done(b))
                for c in range(NCH):
                    step(V.scalar_tensor_tensor(osb[p][:, c, :], bank[4][:, 128 * c:128 * c + 128], rms[:, c:c + 1],
                                                o1[:, c, :], ALU.mult, ALU.add))

            with v.Fori(0, SEQS // 2) as i:
                for p in range(2):
                    b = 2 * i + p
                    layernorm(b, p, i)
                    xn_low(b)
                    dt_steps(b)
                    silus(b)
                    x_times_dt(b)
                    phases(b)
                    k_exponents(b)
                    b_and_c(b)
                    low_half(s_h0l, h0h, h0l, a_h0, b)
                    low_half(s_h1l, h1h, h1l, a_h1, b)
                    decayed(b)
                    if fast:
                        g_base(b, "causal")
                    else:
                        g_base(b, "ident")
                        sa, sm = chain(s_lvarg, b), chain(s_lvmul, b)
                        for n, m in enumerate(LEVELS):
                            level_arg(b, n, m, sa)
                            level_mul(b, n, m, sm)
                            level_take(b, n, m, g_step[0])
                    states(b)
                    gated(b)
                    final(b, p, i)

        @block.scalar
        def _(act):
            A = nc.scalar
            act.wait_ge(weights, 16 * len(loads))
            act.wait_ge(set_dve, 6)

            def step(sig, ins):
                ins.then_inc(sig.sem, 1)

            def mlp_high(sig, ready, hi, b):
                for f in range(MT):
                    act.wait_ge(ready.sem, ready.at(b, f + 1))
                    step(sig, A.activation(hi[:, f, :], bank[6 + f % 2][:], ACT.Relu))

            def tanhs(b):
                act.wait_ge(t_l1.sem, t_l1.done(b))
                step(a_tanh, A.activation(th1[:], bank[0][0:LORA, :], ACT.Tanh))
                for half in range(2):
                    act.wait_ge(t_x.sem, t_x.done(b))
                    step(a_tanh, A.activation(thx[:, 2 * half:2 * half + 2, :], bank[2 + half][:], ACT.Tanh, scale=0.5))
                act.wait_ge(t_bc.sem, t_bc.done(b))
                step(a_tanh, A.activation(bcp[:], bank[6][:], ACT.Identity, bias=cb_col[:, 0:1]))
                step(a_tanh, A.activation(thb[:], bank[6][:], ACT.Tanh, bias=hcb[:, 0:1], scale=0.5))
                act.wait_ge(t_z.sem, t_z.done(b))
                for half in range(2):
                    step(a_tanh, A.activation(thz[:, 2 * half:2 * half + 2, :], bank[4 + half][:], ACT.Tanh, scale=0.5))

            with act.Fori(0, SEQS // 2) as i:
                for p in range(2):
                    b = 2 * i + p
                    act.wait_ge(t_T.sem, t_T.done(b))
                    step(a_xnT, A.copy(xnT[:, PAD:PAD + T], bank[0][:]))
                    step(a_xnT, A.activation(xh[:], bank[0][:], ACT.Copy, scale=XSCALE))
                    act.wait_ge(s_dt.sem, s_dt.at(b, 2))
                    step(a_dte, A.activation(de[:], dneg[:], ACT.Exp))
                    tanhs(b)
                    act.wait_ge(s_ph.sem, s_ph.at(b, 2))
                    step(a_sq, A.activation(sq[:], theta[:], ACT.Square))
                    act.wait_ge(s_ph.sem, s_ph.done(b))
                    act.wait_ge(t_bcc.sem, t_bcc.done(b))
                    step(a_bc, A.copy(bcol[:], bank[2][:]))
                    A.activation(pabs[:], phl[:], ACT.Abs).then_inc(set_act, 1)
                    step(a_trig, A.activation(psn, phl[:], ACT.Sin, scale=TURN))
                    act.wait_ge(set_act, b + 1)
                    step(a_trig, A.activation(pcs, pabs[:], ACT.Sin, scale=-TURN, bias=halfpi[:, 0:1]))
                    mlp_high(a_h0, t_h0, h0h, b)
                    mlp_high(a_h1, t_h1, h1h, b)
                    if fast:
                        step(a_exp, A.activation(E[:], cum3[:, 1, :], ACT.Exp))
                    else:
                        act.wait_ge(s_tail.sem, s_tail.done(b))
                        step(a_exp, A.activation(E[:], diff[:], ACT.Exp))
                    step(a_exp, A.activation(E2[:], cum3[:, 0, :], ACT.Exp))
                    step(a_exp, A.activation(aend[:], view(cum3, 0, 128, SUB - 1, [[SUB, NSUB]]), ACT.Exp))
                    act.wait_ge(t_kt.sem, t_kt.done(b))
                    kt = [[KT[:, 0:2, :, :], bank[6][:]], [KT[:, 2:4, :, :], bank[7][:]]]
                    if not fast:
                        act.wait_ge(s_kq.sem, s_kq.done(b))
                        for n in range(len(LEVELS)):
                            act.wait_ge(s_lvarg.sem, s_lvarg.at(b, n + 1))
                            step(a_lv, A.activation(E[:], arg[:], ACT.Exp))
                    for dst, src in kt:
                        step(a_kt, A.copy(dst, src))
                    for c in range(NCH):
                        act.wait_ge(s_gate.sem, s_gate.at(b, 2 * (c // 2) + 2))
                        act.wait_ge(a_ssq.sem, a_ssq.at(b, c))
                        step(a_ssq, A.activation(gsq[:], g2[:, c, :], ACT.Square, scale=MEAN, accum_out=ssq[:, c:c + 1]))
                    act.wait_ge(t_gT.sem, t_gT.done(b))
                    for h in range(2):
                        step(a_gT, A.copy(gT[:, h, :], bank[2 + h][:]))

        @block.gpsimd
        def _(g):
            P = nc.gpsimd
            g.wait_ge(set_dve, 40)
            g.wait_ge(weights, 16 * len(loads))
            with g.Fori(0, SEQS // 2) as i:
                for p in range(2):
                    b = 2 * i + p
                    g.wait_ge(s_ln.sem, s_ln.at(b, 2 * NCH + 2))
                    P.tensor_tensor(rstd[:], vare[:], minus_half[:], ALU.pow).then_inc(s_rstd.sem, 1)
                    g.wait_ge(s_silu.sem, s_silu.at(b, 2))
                    P.tensor_tensor(dx[:].rearrange("p c (h e) -> p c h e", h=HEADS),
                                    x2[:].rearrange("p c (h e) -> p c h e", h=HEADS),
                                    view(hskip, 0, 128, 0, [[0, NCH], [1, HEADS], [0, HEAD]]), ALU.mult).then_inc(s_dx.sem, 1)
                    g.wait_ge(a_ssq.sem, a_ssq.done(b))
                    P.tensor_tensor(msq[:], ssq[:], eps4[:], ALU.add).then_inc(set_pool, 1)
                    g.wait_ge(set_pool, b + 1)
                    P.tensor_tensor(rms[:], msq[:], minus_half[:], ALU.pow).then_inc(s_rms.sem, 1)

        @block.tensor
        def _(pe):
            M = nc.tensor
            pe.wait_ge(weights, 16 * len(loads))
            pe.wait_ge(set_dve, 6 + 3 * TAPS)
            for k in range(TAPS):
                for t in range(3):
                    M.transpose(bank[k][:, 128 * t:128 * t + 128], scaled[:, 3 * k + t, :], ident)
            for t in range(2):
                M.transpose(bank[4][:, 128 * t:128 * t + 128], win[:, t, :], ident)
                M.transpose(bank[4][:, 256 + 128 * t:384 + 128 * t], wout[:, 128 * t:128 * t + 128], ident)
            M.transpose(bank[5][:, 0:HEADS], wdt[:], ident[0:HEADS, 0:HEADS]).then_inc(set_pe, 1)
            pe.wait_ge(set_dve, SETUP)

            def tok(c, k=PAD):
                return xnT[:, k + CH * c:k + CH * c + CH]

            def projections(b):
                pe.wait_ge(s_ln.sem, s_ln.done(b))
                for c in range(NCH):
                    last = M.transpose(bank[0][:, CH * c:CH * c + CH], xn[:, c, :], ident)
                last.then_inc(t_T.sem, 1)
                pe.wait_ge(a_xnT.sem, a_xnT.at(b, 1))
                for c in range(NCH):
                    last = M.matmul(bank[1][:, HEADS * c:HEADS * c + HEADS], tok(c), DTW[:], start=True, stop=True)
                last.then_inc(t_dt.sem, 1)
                pe.wait_ge(s_xl.sem, s_xl.done(b))
                M.matmul(bank[0][0:LORA, :], tw1[:], xnT[:, PAD:PAD + T], start=True, stop=True).then_inc(t_l1.sem, 1)
                for c in range(NCH):
                    dst = bank[2 + c // 2][:, INNER * (c % 2):INNER * (c % 2) + INNER]
                    for k in range(TAPS):
                        M.matmul(dst, tok(c, k), XW[:, k, :], start=(k == 0), stop=False)
                    last = M.matmul(dst, ones[:], cb_row[:], start=False, stop=True)
                last.then_inc(t_x.sem, 1)
                for k in range(TAPS):
                    last = M.matmul(bank[6][:], BCW[:, k, :], xnT[:, k:k + T], start=(k == 0), stop=(k == TAPS - 1))
                last.then_inc(t_bc.sem, 1)
                for c in range(NCH):
                    last = M.matmul(bank[4 + c // 2][:, INNER * (c % 2):INNER * (c % 2) + INNER], tok(c), ZW[:],
                                    start=True, stop=True)
                last.then_inc(t_z.sem, 1)
                pe.wait_ge(a_tanh.sem, a_tanh.at(b, 1))
                pe.wait_ge(s_dt.sem, s_dt.done(b))
                M.matmul(bank[1][:], tw2[:], th1[:], start=True, stop=True).then_inc(t_l2.sem, 1)
                for c in range(NCH):
                    last = M.matmul(bank[0][:, CH * c:CH * c + CH], dtb32[:, c, :, :].rearrange("p h k -> p (h k)"), ident,
                                    start=True, stop=True)
                last.then_inc(t_dtr.sem, 1)
                pe.wait_ge(s_silu.sem, s_silu.done(b))
                M.matmul(bank[2][:], c_("bcol"), bc2[:], start=True, stop=True)
                M.matmul(bank[3][:], c_("ccol"), bc2[:], start=True, stop=True).then_inc(t_bcc.sem, 1)
                pe.wait_ge(s_bc.sem, s_bc.at(b, 1))
                last_tokens = view(bc2, 0, 128, SUB - 1, [[SUB, NSUB]])
                M.matmul(bank[7][:, 0:NSUB], c_("bre"), last_tokens, start=True, stop=True)
                M.matmul(bank[7][:, NSUB:2 * NSUB], c_("bim"), last_tokens, start=True, stop=True)
                M.matmul(bank[2][:], c_("cre"), bc2[:], start=True, stop=True)
                M.matmul(bank[3][:], c_("cim"), bc2[:], start=True, stop=True)
                M.matmul(bank[4][:], c_("cbre"), prod[:], start=True, stop=True)
                M.matmul(bank[5][:], c_("cbim"), prod[:], start=True, stop=True).then_inc(t_sel.sem, 1)

            def mlp(b):
                for f in range(MT):
                    if f < 2:
                        pe.wait_ge(s_bc.sem, s_bc.done(b))
                    else:
                        pe.wait_ge(s_h0l.sem, s_h0l.at(b, f - 1))
                    w = W0[:, 128 * f:128 * f + 128]
                    M.matmul(bank[6 + f % 2][:], w, xh[:], start=True, stop=False)
                    M.matmul(bank[6 + f % 2][:], w, xl[:], start=False, stop=True).then_inc(t_h0.sem, 1)
                for f in range(MT):
                    pe.wait_ge(s_h0l.sem, s_h0l.done(b))
                    if f >= 2:
                        pe.wait_ge(s_h1l.sem, s_h1l.at(b, f - 1))
                    for k in range(MT):
                        w = W1[:, k, 128 * f:128 * f + 128]
                        M.matmul(bank[6 + f % 2][:], w, h0h[:, k, :], start=(k == 0), stop=False)
                        last = M.matmul(bank[6 + f % 2][:], w, h0l[:, k, :], start=False, stop=(k == MT - 1))
                    last.then_inc(t_h1.sem, 1)

            def mlp_out(b):
                pe.wait_ge(s_h1l.sem, s_h1l.done(b))
                for c in range(NCH):
                    for k in range(MT):
                        for n, h in enumerate((h1h, h1l)):
                            last = M.matmul(bank[7][:, D * c:D * c + D], h[:, k, CH * c:CH * c + CH], W2[:, k, :],
                                            start=(k == 0 and n == 0), stop=(k == MT - 1 and n == 1))
                last.then_inc(t_mo.sem, 1)

            def g_products(b, left, right, off, step_, n_blk, m, then=True):
                for c in range(NCH):
                    for r in range(2):
                        for h in range(HEADS):
                            lt, rt = left[r], right[r]
                            width = n_blk * m
                            rhs = view(rt[0], 32 * h, 32, rt[1] + CH * c + off, [[step_, n_blk], [1, m]])
                            last = M.matmul(bank[2 + h][:, width * c:width * c + width],
                                            view(lt[0], 32 * h, 32, lt[1] + CH * c, [[1, CH]]), rhs,
                                            start=(r == 0), stop=(r == 1), skip_group_check=True)
                if then:
                    last.then_inc(t_g.sem, 1)

            def g_across(b):
                for c in range(NCH):
                    for r, (k, q) in enumerate(((Bre, Qre), (Bim, Qim))):
                        for h in range(HEADS):
                            last = M.matmul(bank[2 + h][0:SUB, CH * c + SUB:CH * c + CH],
                                            view(k, 32 * h, 32, CH * c, [[1, SUB]]),
                                            view(q, 32 * h, 32, CH * c + SUB, [[1, SUB]]),
                                            start=(r == 0), stop=(r == 1), skip_group_check=True)
                last.then_inc(t_g.sem, 1)

            def k_transposed(b):
                pe.wait_ge(s_kq.sem, s_kq.done(b))
                for c in range(NCH):
                    for r, k in enumerate((Bre, Bim)):
                        n = 2 * c + r
                        last = M.transpose(bank[6 + n // 4][:, 128 * (n % 4):128 * (n % 4) + 128], k[:, CH * c:CH * c + CH], ident)
                last.then_inc(t_kt.sem, 1)

            def states_and_y(b):
                pe.wait_ge(a_kt.sem, a_kt.done(b))
                pe.wait_ge(s_g.sem, s_g.done(b))
                for c in range(NCH):
                    bankc, at = bank[c // 2], INNER * (c % 2)
                    halves = ((0, CH),) if fast else ((0, SUB), (SUB, SUB))
                    for n, (lo, size) in enumerate(halves):
                        j = len(halves) * c + n
                        if j < NST:
                            if j:
                                pe.wait_ge(s_st.sem, s_st.at(b, j if fast else 2 * j))
                            for r in range(2):
                                last = M.matmul(bank[6][:, INNER * r:INNER * r + INNER], view(KT, lo, size, 256 * c + 128 * r, [[1, 128]]),
                                                view(xd, lo, size, INNER * c, [[1, INNER]]),
                                                start=(not fast or (j == 0 and r == 0)), stop=True, skip_group_check=True)
                            last.then_inc(t_s.sem, 1)
                        if j:
                            pe.wait_ge(s_st.sem, s_st.at(b, j if fast else 2 * j))
                            for r, q in enumerate((Qre, Qim)):
                                M.matmul(bankc[lo:lo + size, at:at + INNER], q[:, CH * c + lo:CH * c + lo + size], Sst[(j - 1) % 3][:, r, :],
                                         start=(r == 0), stop=False, skip_group_check=True)
                        for h in range(HEADS):
                            last = M.matmul(bankc[lo:lo + size, at + HEAD * h:at + HEAD * h + HEAD],
                                            GT[:, h, c, lo:lo + size], xd[:, c, HEAD * h:HEAD * h + HEAD],
                                            start=(j == 0), stop=True, skip_group_check=True)
                    if c % 2:
                        last.then_inc(t_y.sem, 1)

            def out_projection(b):
                pe.wait_ge(s_gate.sem, s_gate.done(b))
                for h in range(2):
                    for c in range(NCH):
                        last = M.transpose(bank[2 + h][:, CH * c:CH * c + CH], g2[:, c, 128 * h:128 * h + 128], ident)
                last.then_inc(t_gT.sem, 1)
                pe.wait_ge(a_gT.sem, a_gT.done(b))
                for c in range(NCH):
                    for h in range(2):
                        last = M.matmul(bank[4][:, D * c:D * c + D], gT[:, h, CH * c:CH * c + CH], OW[:, h, :],
                                        start=(h == 0), stop=(h == 1))
                last.then_inc(t_o.sem, 1)

            with pe.Fori(0, SEQS // 2) as i:
                for p in range(2):
                    b = 2 * i + p
                    projections(b)
                    mlp(b)
                    k_transposed(b)
                    if fast:
                        g_products(b, ((Kre, 0), (Kim, 0)), ((Ure, 0), (Uim, 0)), 0, CH, 1, CH, then=False)
                        g_across(b)
                    else:
                        g_products(b, ((Xre, 0), (Xim, 0)), ((Xre, T), (Xim, T)), 0, CH, 1, CH)
                        for n, m in enumerate(LEVELS):
                            pe.wait_ge(s_lvmul.sem, s_lvmul.at(b, 2 * n + 2))
                            pe.wait_ge(s_g.sem, s_g.at(b, HEADS + (HEADS + 1) * n))
                            g_products(b, ((Wre, 0), (Wim, 0)), ((Wre, 0), (Wim, 0)), m, 2 * m, CH // (2 * m), m)
                    states_and_y(b)
                    mlp_out(b)
                    out_projection(b)


_NAMES = ["x", "in_proj_w", "conv_w", "conv_b", "dt_bias", "lambda_base", "theta_base", "theta_w1", "theta_w2",
          "viscosity_eta", "D", "norm_w", "out_proj_w"]
_FFN = ["k0", "k1", "k2", "s0", "s1", "s2"]


def kernel(**inputs):
    import numpy as _np
    import concourse.bacc as _bacc
    from concourse import mybir as _mybir
    from concourse.bass_utils import run_bass_kernel_spmd as _run

    nc = _bacc.Bacc("TRN2", target_bir_lowering=False, num_devices=1)
    arrays, args = {}, {}
    for name in _NAMES + _FFN:
        full = ("L0_ffn_" if name in _FFN else "L0_attn_") + name
        arr = _np.ascontiguousarray(inputs[full])
        arr = arr.reshape(arr.shape or (1,))
        arrays[f"in_{name}"] = arr
        args[name] = nc.dram_tensor(f"in_{name}", arr.shape, _mybir.dt.from_np(arr.dtype), kind="ExternalInput").ap()
    arrays["constants"] = CONSTANTS
    consts = nc.dram_tensor("constants", CONSTANTS.shape, F32, kind="ExternalInput").ap()
    out = nc.dram_tensor("out", (SEQS, T, D), F32, kind="ExternalOutput").ap()
    build(nc, MODE, args, consts, out)
    r = _run(nc, [arrays], core_ids=[0])
    return r.results[0]["out"]


MODE = "general"
```

```python
import math
from contextlib import ExitStack

import numpy as np

import concourse.bass as bass
from concourse import mybir

ALU = mybir.AluOpType
ACT = mybir.ActivationFunctionType
AX_X = mybir.AxisListType.X
F32 = mybir.dt.float32
F16 = mybir.dt.float16
U8 = mybir.dt.uint8
I32 = mybir.dt.int32

SEQS, T, D = 8, 512, 128
INNER, HEADS, HEAD, BLK = 256, 4, 64, 32
STATE = 2 * BLK
TAPS = 4
LORA = 48
CH = 128
NCH = T // CH
MLP = 512
MT = MLP // 128
EPS = 1e-5
CLIP = math.pi / 2
XSCALE = 16.0
SUB = 64
NSUB = T // SUB
LEVELS = [1, 2, 4, 8, 16, 32]
SAFE = 40.0
SPREAD = 0.999 * SAFE ** 2
MEAN = 1 / (2 * math.sqrt(INNER))
ROUND = 1.5 * 2.0 ** 23
SETUP = 48
TURN = 6.2831850
PHASE_STEPS = 10
LOG1P_TERMS = 9


def view(t, part, parts, offset, dims):
    pitch = t[:].ap[0][0]
    return bass.AP(t, part * pitch + offset, [[pitch, parts], *dims])


CONST_PARTS = {}


def constants():
    p = np.arange(128)
    parts = {}
    parts["ident"] = np.eye(128)
    s_, t_ = p[:, None], p[None, :]
    parts["causal"] = (s_ <= t_) * 1.0
    parts["restart"] = np.tile((np.arange(T) % SUB != 0) * 1.0, (128, 1))
    parts["ones"] = np.ones((128, T))
    bre, bim, cre, cim = 0, 1, STATE, STATE + 1
    for name, rows in (("bcol", (bre, bim, bre, bim)), ("ccol", (cre, cim, cim, cre)),
                       ("bre", (bre,) * 4), ("bim", (bim,) * 4), ("cre", (cre,) * 4), ("cim", (cim,) * 4)):
        sel = np.zeros((128, 128))
        for col in range(128):
            sel[rows[col // BLK] + 2 * (col % BLK), col] = 0.5
        parts[name] = sel
    for name, signs in (("cbre", (1, -1, 0, 0)), ("cbim", (0, 0, 1, 1))):
        parts[name] = np.array([[signs[r // BLK] * (r % BLK == col % BLK) for col in range(128)] for r in range(128)])
    parts["heads"] = (p[:, None] // BLK == np.arange(INNER)[None, :] // HEAD) * 1.0
    for m in LEVELS:
        t = np.array([a + m + i for a in range(0, CH, 2 * m) for i in range(m)])
        parts[f"level{m}"] = ((p[:, None] // (2 * m) == t[None, :] // (2 * m)) & (p[:, None] % (2 * m) < m)) * 1.0
    at = 0
    for name, a in parts.items():
        CONST_PARTS[name] = (at, at + a.shape[1])
        at += a.shape[1]
    return np.concatenate(list(parts.values()), 1).astype(np.float32)


CONSTANTS = constants()


class Signal:

    def __init__(self, ctx, nc, name, steps):
        self.sem = ctx.enter_context(nc.semaphore(name))
        self.steps = steps

    def at(self, n, step):
        return n * self.steps + step

    def done(self, n):
        return n * self.steps + self.steps


class Level(Signal):

    def at(self, n, step):
        return (n - SEQS) * self.steps + step

    def done(self, n):
        return (n - SEQS) * self.steps + self.steps


def build(nc, a, consts, out):
    ctx = ExitStack()
    with ctx:
        def sb(name, shape, dt=F32):
            return ctx.enter_context(nc.sbuf_tensor(name, shape, dt))

        def sem(name):
            return ctx.enter_context(nc.semaphore(name))

        def signal(name, steps):
            return Signal(ctx, nc, name, steps)

        bank = [ctx.enter_context(nc.psum_tensor(f"bank{i}", [128, 512], F32)) for i in range(8)]

        const = sb("const", [128, CONSTANTS.shape[1]])

        def c_(name):
            lo, hi = CONST_PARTS[name]
            return const[:, lo:hi]

        ident = c_("ident")
        win = sb("win", [128, 5, D])
        wdt = sb("wdt", [HEADS, D])
        wout = sb("wout", [128, INNER])
        cw = sb("cw", [128, 3, TAPS])
        cb_row = sb("cb_row", [1, INNER])
        cb_col = sb("cb_col", [128, 1])
        dtb = sb("dtb", [128, HEADS])
        skip = sb("skip", [128, HEADS])
        lam = sb("lam", [128, 1])
        base = sb("base", [128, 1])
        eta = sb("eta", [128, 1])
        normw = sb("normw", [128, 2])
        tw1 = sb("tw1", [128, LORA])
        tw2 = sb("tw2", [LORA, 128])
        k0u = sb("k0u", [128, 2, MLP], U8)
        k1u = sb("k1u", [128, MT, MLP], U8)
        k2u = sb("k2u", [128, MT, D], U8)
        s012 = sb("s012", [128, 3])
        XW = sb("XW", [128, TAPS, INNER])
        BCW = sb("BCW", [128, TAPS, 128])
        ZW = sb("ZW", [128, INNER])
        OW = sb("OW", [128, 2, D])
        DTW = sb("DTW", [128, HEADS])
        w0d = sb("w0d", [128, MLP])
        W0 = sb("W0", [128, MLP], F16)
        W1 = sb("W1", [128, MT, MLP], F16)
        W2 = sb("W2", [128, MT, D], F16)
        sign = sb("sign", [128, 3])
        negs = sb("negs", [128, 3])
        abss = sb("abss", [128, 3])
        w1s = sb("w1s", [128, 2])
        w0s = sb("w0s", [128, 1])
        sffn = sb("sffn", [128, 1])
        neglam = sb("neglam", [128, 1])
        negeta = sb("negeta", [128, 1])
        hcb = sb("hcb", [128, 1])
        hskip = sb("hskip", [128, HEADS])
        halfpi = sb("halfpi", [128, 1])
        minus_half = sb("minus_half", [128, NCH])
        eps4 = sb("eps4", [128, NCH])
        carrier = sb("carrier", [128, 2])
        ones = sb("ones", [1, 128])

        xtok = [sb(f"xtok{p}", [128, NCH, D]) for p in range(2)]
        osb = [sb(f"osb{p}", [128, NCH, D]) for p in range(2)]
        st6 = sb("st6", [128, NCH, 6])
        mv = sb("mv", [128, NCH, 2])
        vare = sb("vare", [128, NCH])
        rstd = sb("rstd", [128, NCH])
        xn = sb("xn", [128, NCH, D])
        PAD = TAPS - 1
        xnT = sb("xnT", [128, PAD + T])
        xh = sb("xh", [128, T], F16)
        xl = sb("xl", [128, T], F16)
        th1 = sb("th1", [LORA, T])
        x2 = sb("x2", [128, NCH, INNER])
        thx = sb("thx", [128, NCH, INNER])
        z2 = sb("z2", [128, NCH, INNER])
        thz = sb("thz", [128, NCH, INNER])
        bcp = sb("bcp", [128, T])
        thb = sb("thb", [128, T])
        bc2 = sb("bc2", [128, T])
        dv = sb("dv", [128, NCH, HEADS])
        dneg = sb("dneg", [128, NCH, HEADS])
        de = sb("de", [128, NCH, HEADS])
        ds = sb("ds", [128, NCH, HEADS])
        dq = sb("dq", [128, NCH, HEADS])
        dacc = sb("dacc", [128, NCH, HEADS])
        dt = sb("dt", [128, NCH, HEADS])
        hdt = sb("hdt", [128, NCH, HEADS])
        dtb32 = sb("dtb32", [128, NCH, HEADS, BLK])
        xd = sb("xd", [128, NCH, INNER])
        theta = sb("theta", [128, T])
        sq = sb("sq", [128, T])
        nl = sb("nl", [128, T])
        lz = sb("lz", [128, T])
        ph = sb("ph", [128, T])
        cum3 = sb("cum3", [128, 3, T])
        phl = sb("phl", [128, T])
        pend = sb("pend", [128, NSUB])
        pint = sb("pint", [128, NSUB])
        poff = sb("poff", [128, NSUB])
        pabs = sb("pabs", [128, T])
        Xre = sb("Xre", [128, 2, T])
        Xim = sb("Xim", [128, 2, T])
        pcs, psn = Xre[:, 0, :], Xim[:, 0, :]
        bcol = sb("bcol", [128, T])
        prod = sb("prod", [128, T])
        be = sb("be", [128, 2, NSUB])
        ec = sb("ec", [128, T])
        es = sb("es", [128, T])
        btmp = [sb(f"btmp{k}", [128, T]) for k in range(2)]
        tmpa = sb("tmpa", [128, T])
        tmpb = sb("tmpb", [128, T])
        E = sb("E", [128, T])
        E2 = sb("E2", [128, T])
        aend = sb("aend", [128, NSUB])
        Kre = sb("Kre", [128, T])
        Kim = sb("Kim", [128, T])
        Qre = sb("Qre", [128, T])
        Qim = sb("Qim", [128, T])
        Bre = sb("Bre", [128, T])
        Bim = sb("Bim", [128, T])
        Ure = sb("Ure", [128, T])
        Uim = sb("Uim", [128, T])
        GT = sb("GT", [128, HEADS, NCH, CH])
        scaled = GT[:].rearrange("p h c t -> p (h c) t")
        KT = sb("KT", [128, NCH, 2, 128])
        Sst = [sb(f"S{c}", [128, 2, INNER]) for c in range(3)]
        stmp = sb("stmp", [128, 2, INNER])
        dx = sb("dx", [128, NCH, INNER])
        y1 = sb("y1", [128, NCH, INNER])
        g2 = sb("g2", [128, NCH, INNER])
        gsq = sb("gsq", [128, INNER])
        ssq = sb("ssq", [128, NCH])
        msq = sb("msq", [128, NCH])
        rms = sb("rms", [128, NCH])
        gT = sb("gT", [128, 2, T])
        o1 = sb("o1", [128, NCH, D])
        h0h = sb("h0h", [128, MT, T], F16)
        h0l = sb("h0l", [128, MT, T], F16)
        h1h = sb("h1h", [128, MT, T], F16)
        h1l = sb("h1l", [128, MT, T], F16)
        diff, arg = tmpa, tmpb
        Wre, Wim = Ure, Uim
        tmpc = sb("tmpc", [128, T])
        tmpd = sb("tmpd", [128, T])
        spread = sb("spread", [128, 1])
        beyond = sb("beyond", [128, 1])
        most = sb("most", [128, 1])
        top = sb("top", [1, 1])
        above = sb("above", [1, 1])
        again = sb("again", [1, 1], I32)

        weights = sem("weights_loaded")
        x_in = [sem(f"x_loaded{p}") for p in range(2)]
        o_out = [sem(f"out_stored{p}") for p in range(2)]
        set_dve = sem("setup_vector")
        set_pe = sem("setup_transposes")
        set_act = sem("setup_copies")
        flag_ready = sem("flag_ready")
        flag_top = sem("flag_top")
        NL = len(LEVELS)
        NST = {True: NCH - 1, False: NSUB - 1}
        s_ln = signal("layernorm", 3 * NCH + 2)
        s_xl = signal("xn_low_half", 1)
        s_dt = signal("dt_steps", 11 + LOG1P_TERMS)
        s_silu = signal("silu", 5)
        s_xd = signal("x_times_dt", 1)
        s_ph = signal("phases", 15)
        s_bc = signal("products_of_B_and_C", 2)
        s_tail = Level(ctx, nc, "K_exponents", 1)
        s_kq = signal("decayed", 4 + 12)
        s_g = {True: signal("G_in_sbuf", HEADS), False: Level(ctx, nc, "G_in_sbuf_general", HEADS * (1 + 2 * NL))}
        s_lvarg = Level(ctx, nc, "level_exponents", NL)
        s_lvmul = Level(ctx, nc, "level_products", 2 * NL)
        s_st = {True: signal("states", NST[True]), False: Level(ctx, nc, "states_general", 2 * NST[False])}
        s_most = signal("largest_exponents", 1)
        s_gate = signal("gated", 4)
        s_fin = signal("final", NCH)
        s_h0l = signal("h0_low_half", MT)
        s_h1l = signal("h1_low_half", MT)
        s_rstd = signal("rstd", 1)
        s_dx = signal("skip_term", 1)
        s_rms = signal("rms", 1)
        s_msq = signal("mean_squares", 1)
        s_bk = signal("B_K", 6)
        a_xnT = signal("xnT_copied", 2)
        a_tanh = signal("tanhs", 7)
        a_dte = signal("dt_exp", 1)
        a_sq = signal("theta_squared", 1)
        a_trig = signal("sin_cos", 2)
        a_exp = signal("decay_exps", 4)
        a_lv = Level(ctx, nc, "level_exps", NL)
        a_bc = signal("B_copied", 1)
        a_kt = signal("KT_copied", 2)
        s_mo = signal("mlp_added", 1)
        a_ssq = signal("squares", NCH)
        a_gT = signal("gT_copied", 2)
        a_h0 = signal("h0_high_half", MT)
        a_h1 = signal("h1_high_half", MT)
        a_abs = signal("phase_abs", 1)
        t_T = signal("xn_transposed", 1)
        t_dt = signal("dt_projected", 1)
        t_l1 = signal("lora1", 1)
        t_x = signal("x_projected", 1)
        t_bc = signal("bc_projected", 1)
        t_z = signal("z_projected", 1)
        t_l2 = signal("lora2", 1)
        t_dtr = signal("dt_spread", 1)
        t_bcc = signal("bc_in_columns", 1)
        t_be = signal("b_at_ends", 1)
        t_sel = signal("bc_spread", 1)
        t_h0 = signal("mlp0", MT)
        t_h1 = signal("mlp1", MT)
        t_mo = signal("mlp_out", 1)
        t_g = {True: signal("G_products", HEADS), False: Level(ctx, nc, "G_products_general", HEADS * (1 + NL))}
        t_kt = signal("K_transposed", 2)
        t_s = {True: signal("state_products", NST[True]), False: Level(ctx, nc, "state_products_general", NST[False])}
        t_y = signal("y_products", 2)
        t_gT = signal("g_transposed", 1)
        t_o = signal("out_projected", 1)

        x_dram = a["x"].rearrange("b (c p) d -> b p c d", p=128)
        out_dram = out.rearrange("b (c p) d -> b p c d", p=128)

        def col(ap1d, n=128):
            return ap1d.rearrange("(p o) -> p o", o=1)

        def row_all(ap1d, n):
            return bass.AP(ap1d.tensor, ap1d.offset, [[0, 128], [1, n]])

        loads = [
            (const[:], consts),
            (win[:], a["in_proj_w"][0:640, :].rearrange("(t p) d -> p t d", p=128)),
            (wdt[:], a["in_proj_w"][640:644, :]),
            (wout[:], a["out_proj_w"]),
            (cw[:], a["conv_w"].rearrange("(t p) k -> p t k", p=128)),
            (cb_row[:], a["conv_b"][0:INNER].rearrange("(o c) -> o c", o=1)),
            (cb_col[:], col(a["conv_b"][INNER:INNER + 128])),
            (dtb[:], row_all(a["dt_bias"], HEADS)),
            (skip[:], row_all(a["D"], HEADS)),
            (lam[:], a["lambda_base"].rearrange("h (k o) -> (h k) o", o=1)),
            (base[:], a["theta_base"].rearrange("h (k o) -> (h k) o", o=1)),
            (eta[:], a["viscosity_eta"].rearrange("h (k o) -> (h k) o", o=1)),
            (normw[:], a["norm_w"].rearrange("(t p) -> p t", p=128)),
            (tw1[:], a["theta_w1"]),
            (tw2[:], a["theta_w2"]),
            (k0u[:], a["k0"].rearrange("(t p) f -> p t f", p=128)),
            (k1u[:], a["k1"].rearrange("(t p) f -> p t f", p=128)),
            (k2u[:], a["k2"].rearrange("(t p) f -> p t f", p=128)),
            (s012[:, 0:1], row_all(a["s0"], 1)),
            (s012[:, 1:2], row_all(a["s1"], 1)),
            (s012[:, 2:3], row_all(a["s2"], 1)),
        ]
        block = ctx.enter_context(nc.Block())

        def general_needed(eng):
            eng.wait_ge(flag_ready, 1)
            return eng.value_load(again[0:1, 0:1], min_val=0, max_val=1)

        @block.sync
        def _(sp):
            def load(n, b, p):
                if not (isinstance(n, int) and n < 2):
                    sp.wait_ge(s_mo.sem, s_mo.done(n - 2))
                sp.dma_start(xtok[p][:], x_dram[b]).then_inc(x_in[p], 16)

            def store(n, b, p):
                sp.wait_ge(s_fin.sem, s_fin.done(n))
                sp.dma_start(out_dram[b], osb[p][:]).then_inc(o_out[p], 16)

            with nc.allow_non_contiguous_dma("small columns of weights"):
                for p in range(2):
                    load(p, p, p)
                for dst, src in loads:
                    sp.dma_start(dst, src).then_inc(weights, 16)
                with sp.Fori(0, SEQS // 2 - 1) as i:
                    for p in range(2):
                        load(2 * i + p + 2, 2 * i + p + 2, p)
                        store(2 * i + p, 2 * i + p, p)
                for p in range(2):
                    store(SEQS - 2 + p, SEQS - 2 + p, p)
                for p in range(2):
                    sp.wait_ge(o_out[p], 16 * (SEQS // 2) + 1)
                if True:
                    flag = general_needed(sp)
                    with nc.If(flag > 0):
                        with sp.Fori(0, SEQS // 2) as i:
                            for p in range(2):
                                load(SEQS + 2 * i + p, 2 * i + p, p)
                                store(SEQS + 2 * i + p, 2 * i + p, p)
                        for p in range(2):
                            sp.wait_ge(o_out[p], 16 * SEQS + 1)
                        sp.nop()
                    with nc.Else():
                        sp.nop()
                    sp.nop()

        @block.vector
        def _(v):
            nd = [0]

            def setup(ins):
                nd[0] += 1
                ins.then_inc(set_dve, 1)
                v.wait_ge(set_dve, nd[0])

            V = nc.vector
            for p in range(2):
                V.memset(carrier[:, p:p + 1], 0.0).then_inc(o_out[p], 1)
            V.memset(most[:], 0.0).then_inc(s_most.sem, 1)
            setup(V.memset(xnT[:, 0:PAD], 0.0))
            setup(V.memset(minus_half[:], -0.5))
            setup(V.memset(halfpi[:], math.pi / 2))
            setup(V.memset(ones[:], 1.0))
            setup(V.memset(eps4[:], EPS))
            setup(V.memset(spread[:], -SPREAD))
            setup(V.memset(poff[:], 0.0))
            v.wait_ge(weights, 16 * len(loads))
            for k in range(TAPS):
                for t in range(3):
                    setup(V.tensor_scalar(scaled[:, 3 * k + t, :], win[:, 2 + t, :], cw[:, t, k:k + 1], None, ALU.mult))
            setup(V.tensor_scalar(sign[:], s012[:], 0.0, None, ALU.is_gt))
            setup(V.tensor_scalar(negs[:], s012[:], 0.0, None, ALU.is_lt))
            setup(V.tensor_tensor(sign[:], sign[:], negs[:], ALU.subtract))
            setup(V.tensor_tensor(abss[:], sign[:], s012[:], ALU.mult))
            setup(V.tensor_scalar(w0s[:], sign[:, 0:1], 2.0 / XSCALE, None, ALU.mult))
            setup(V.tensor_scalar(w1s[:, 0:1], sign[:, 1:2], 0.5, None, ALU.mult))
            setup(V.tensor_scalar(w1s[:, 1:2], sign[:, 1:2], -0.25, None, ALU.mult))
            setup(V.tensor_tensor(sffn[:], abss[:, 0:1], abss[:, 1:2], ALU.mult))
            setup(V.tensor_scalar(sffn[:], sffn[:], s012[:, 2:3], 16.0, ALU.mult, ALU.mult))
            setup(V.tensor_tensor(w0d[:], k0u[:, 0, :], k0u[:, 1, :], ALU.subtract))
            setup(V.tensor_scalar(W0[:], w0d[:], w0s[:, 0:1], None, ALU.mult))
            setup(V.tensor_scalar(W1[:], k1u[:], w1s[:, 0:1], w1s[:, 1:2], ALU.mult, ALU.add))
            setup(V.tensor_scalar(W2[:], k2u[:], 2.0, -1.0, ALU.mult, ALU.add))
            setup(V.tensor_scalar(neglam[:], lam[:], -1.0, None, ALU.mult))
            setup(V.tensor_scalar(negeta[:], eta[:], -1.0, None, ALU.mult))
            setup(V.tensor_scalar(hcb[:], cb_col[:], 0.5, None, ALU.mult))
            setup(V.tensor_scalar(hskip[:], skip[:], 0.5, None, ALU.mult))
            v.wait_ge(set_pe, 1)
            for k in range(TAPS):
                setup(V.tensor_copy(XW[:, k, :], bank[k][:, 0:INNER]))
                setup(V.tensor_copy(BCW[:, k, :], bank[k][:, INNER:INNER + 128]))
            setup(V.tensor_copy(ZW[:], bank[4][:, 0:INNER]))
            for h in range(2):
                setup(V.tensor_scalar(OW[:, h, :], bank[4][:, 256 + 128 * h:384 + 128 * h], normw[:, h:h + 1], 0.5,
                                      ALU.mult, ALU.mult))
            setup(V.tensor_copy(DTW[:], bank[5][:, 0:HEADS]))

            assert nd[0] == SETUP, nd

            def chain(signal_, n):
                count = [0]

                def step(ins, linked=True, by=1):
                    count[0] += by
                    ins.then_inc(signal_.sem, by)
                    assert count[0] <= signal_.steps
                    if linked:
                        v.wait_ge(signal_.sem, signal_.at(n, count[0]))

                def link(at=None):
                    v.wait_ge(signal_.sem, signal_.at(n, count[0] if at is None else at))

                step.count, step.link = count, link
                return step

            def layernorm(n, p, loaded):
                v.wait_ge(x_in[p], loaded)
                step = chain(s_ln, n)
                for c in range(NCH):
                    step(V.bn_stats(st6[:, c, :], xtok[p][:, c, :]), linked=False)
                step.link()
                step(V.memset(carrier[:, 0:1], 0.0), linked=False)
                for c in range(NCH):
                    step(V.bn_aggr(mv[:, c, :], st6[:, c, :]), linked=c == NCH - 1)
                step(V.tensor_scalar(vare[:], mv[:, :, 1], EPS, None, ALU.add), linked=False)

            def normalised(n, p):
                step = chain(s_ln, n)
                step.count[0] = 2 * NCH + 2
                v.wait_ge(s_rstd.sem, s_rstd.done(n))
                for c in range(NCH):
                    step(V.tensor_scalar(xn[:, c, :], xtok[p][:, c, :], mv[:, c, 0:1], rstd[:, c:c + 1],
                                         ALU.subtract, ALU.mult), linked=False)

            def xn_low(n):
                v.wait_ge(a_xnT.sem, a_xnT.done(n))
                step = chain(s_xl, n)
                step(V.scalar_tensor_tensor(xl[:], bank[0][:], XSCALE, xh[:], ALU.mult, ALU.subtract), linked=False)

            def dt_steps(n):
                v.wait_ge(t_dt.sem, t_dt.done(n))
                step = chain(s_dt, n)
                ps = bank[1][:, 0:NCH * HEADS].rearrange("p (c h) -> p c h", h=HEADS)
                bias = view(dtb, 0, 128, 0, [[0, NCH], [1, HEADS]])
                step(V.tensor_tensor(dv[:], ps, bias, ALU.add))
                step(V.scalar_tensor_tensor(dneg[:], dv[:], -1.0, dv[:], ALU.mult, ALU.min))
                v.wait_ge(a_dte.sem, a_dte.done(n))
                step(V.tensor_scalar(ds[:], de[:], 2.0, None, ALU.add))
                step(V.reciprocal(dq[:], ds[:]))
                step(V.tensor_tensor(ds[:], de[:], dq[:], ALU.mult))
                step(V.tensor_tensor(dq[:], ds[:], ds[:], ALU.mult))
                terms = LOG1P_TERMS
                step(V.tensor_scalar(dacc[:], dq[:], 1.0 / (2 * terms + 1), None, ALU.mult))
                for j in range(terms - 1, 0, -1):
                    step(V.scalar_tensor_tensor(dacc[:], dacc[:], 1.0 / (2 * j + 1), dq[:], ALU.add, ALU.mult))
                step(V.scalar_tensor_tensor(dacc[:], dacc[:], 1.0, ds[:], ALU.add, ALU.mult))
                step(V.tensor_scalar(dv[:], dv[:], 0.0, None, ALU.max))
                step(V.scalar_tensor_tensor(dt[:], dacc[:], 2.0, dv[:], ALU.mult, ALU.add))
                step(V.tensor_scalar(hdt[:], dt[:], 0.5, None, ALU.mult), linked=False)
                step(V.tensor_copy(dtb32[:], view(dt, 0, 128, 0, [[1, NCH * HEADS], [0, BLK]])))

            def silu_x(n):
                for half in range(2):
                    v.wait_ge(a_tanh.sem, a_tanh.at(n, 2 + half))
                    if half == 0:
                        wait_past(s_dx, n)
                    V.scalar_tensor_tensor(x2[:, 2 * half:2 * half + 2, :], thx[:, 2 * half:2 * half + 2, :], 1.0,
                                           bank[2 + half][:], ALU.add, ALU.mult).then_inc(s_silu.sem, 1)

            def silu_bc(n):
                v.wait_ge(a_tanh.sem, a_tanh.at(n, 5))
                V.scalar_tensor_tensor(bc2[:], thb[:], 1.0, bcp[:], ALU.add, ALU.mult).then_inc(s_silu.sem, 1)

            def silu_z(n):
                for half in range(2):
                    v.wait_ge(a_tanh.sem, a_tanh.at(n, 6 + half))
                    V.scalar_tensor_tensor(z2[:, 2 * half:2 * half + 2, :], thz[:, 2 * half:2 * half + 2, :], 1.0,
                                           bank[2 + half][:], ALU.add, ALU.mult).then_inc(s_silu.sem, 1)

            def wait_past(sig, n):
                if not (isinstance(n, int) and n == 0):
                    v.wait_ge(sig.sem, sig.at(n, 0))

            def x_times_dt(n):
                v.wait_ge(s_silu.sem, s_silu.at(n, 2))
                V.tensor_tensor(xd[:].rearrange("p c (h e) -> p (c h) e", h=HEADS),
                                x2[:].rearrange("p c (h e) -> p (c h) e", h=HEADS),
                                view(hdt, 0, 128, 0, [[1, NCH * HEADS], [0, HEAD]]), ALU.mult).then_inc(s_xd.sem, 1)

            def phases(n, fast):
                step = chain(s_ph, n)
                v.wait_ge(t_l2.sem, t_l2.done(n))
                step(V.tensor_scalar(theta[:], bank[1][:], base[:, 0:1], -CLIP, ALU.add, ALU.max))
                step(V.tensor_scalar(theta[:], theta[:], CLIP, None, ALU.min))
                v.wait_ge(t_dtr.sem, t_dtr.done(n))
                step(V.scalar_tensor_tensor(ph[:], theta[:], 1.0 / (2 * math.pi), bank[0][:], ALU.mult, ALU.mult))
                step(V.tensor_tensor_scan(phl[:], c_("restart"), ph[:], 0.0, ALU.mult, ALU.add))
                ends = view(phl, 0, 128, SUB - 1, [[SUB, NSUB]])
                step(V.tensor_scalar(pint[:], ends, ROUND, -ROUND, ALU.add, ALU.add))
                step(V.tensor_tensor(pend[:], ends, pint[:], ALU.subtract))
                step(V.tensor_tensor_scan(poff[:, 1:NSUB], c_("ones")[:, 1:NSUB], pend[:, 0:NSUB - 1], 0.0, ALU.mult, ALU.add))
                step(V.tensor_tensor(phl[:].rearrange("p (c t) -> p c t", t=SUB), phl[:].rearrange("p (c t) -> p c t", t=SUB),
                                     view(poff, 0, 128, 0, [[1, NSUB], [0, SUB]]), ALU.add))
                step(V.tensor_scalar(ph[:], phl[:], ROUND, -ROUND, ALU.add, ALU.add))
                step(V.tensor_tensor(phl[:], phl[:], ph[:], ALU.subtract))
                assert step.count[0] == PHASE_STEPS
                v.wait_ge(a_sq.sem, a_sq.done(n))
                step(V.tensor_scalar(nl[:], sq[:], negeta[:, 0:1], neglam[:, 0:1], ALU.mult, ALU.add))
                step(V.tensor_tensor(lz[:], nl[:], bank[0][:], ALU.mult))
                if fast:
                    step(V.tensor_tensor_scan(cum3[:, 1, :], c_("ones"), lz[:], 0.0, ALU.mult, ALU.add))
                    step(V.tensor_scalar(cum3[:, 0, :], cum3[:, 1, :], SAFE, -SAFE, ALU.min, ALU.max), by=2)
                else:
                    step(V.tensor_tensor_scan(cum3[:, 0, :], c_("restart"), lz[:], 0.0, ALU.mult, ALU.add))
                    step(V.tensor_scalar(cum3[:, 1, :], cum3[:, 0, :], -1.0, None, ALU.mult))
                    step(V.tensor_copy(cum3[:, 2, :], cum3[:, 0, :]))
                assert step.count[0] == s_ph.steps, step.count

            def b_and_c(n):
                v.wait_ge(t_be.sem, t_be.done(n))
                V.tensor_copy(be[:], bank[1][:, 0:2 * NSUB].rearrange("p (r c) -> p r c", r=2)).then_inc(s_bc.sem, 1)
                v.wait_ge(a_bc.sem, a_bc.done(n))
                V.tensor_tensor(prod[:], bcol[:], bank[3][:], ALU.mult).then_inc(s_bc.sem, 1)

            def k_exponents(n):
                V.tensor_tensor(diff[:].rearrange("p (c t) -> p c t", t=SUB),
                                view(cum3, 0, 128, SUB - 1, [[SUB, NSUB], [0, SUB]]),
                                cum3[:, 1, :].rearrange("p (c t) -> p c t", t=SUB), ALU.add).then_inc(s_tail.sem, 1)

            def decayed(n, fast, part):
                step = chain(s_kq, n)
                uc, us = (ec, es) if fast else (Xre, Xim)
                ure, uim = (Ure[:], Uim[:]) if fast else (Xre[:, 1, :], Xim[:, 1, :])
                if part == 0:
                    v.wait_ge(a_trig.sem, a_trig.done(n))
                    v.wait_ge(a_exp.sem, a_exp.at(n, 1))
                    step(V.tensor_tensor(Kre[:], pcs, E[:], ALU.mult), linked=False)
                    step(V.tensor_tensor(Kim[:], psn, E[:], ALU.mult), linked=False)
                elif part == 1:
                    step.count[0] = 2
                    v.wait_ge(a_exp.sem, a_exp.done(n))
                    step(V.tensor_tensor(ec[:], pcs, E2[:], ALU.mult), linked=False)
                    step(V.tensor_tensor(es[:], psn, E2[:], ALU.mult))
                else:
                    step.count[0] = 3 * part - 2
                    if part == 2:
                        v.wait_ge(t_sel.sem, t_sel.done(n))
                    cbre, cbim, cre, cim = (bank[q][:] for q in (0, 1, 2, 3))
                    uc, us = (ec[:], es[:]) if fast else (pcs, psn)
                    dst, (p1, f1), (p2, f2), op = (
                        (ure, (cbre, uc), (cbim, us), ALU.subtract),
                        (uim, (cbre, us), (cbim, uc), ALU.add),
                        (Qre[:], (cre, ec[:]), (cim, es[:]), ALU.subtract),
                        (Qim[:], (cre, es[:]), (cim, ec[:]), ALU.add),
                    )[part - 2]
                    t1, t2 = (tmpa, tmpb) if part % 2 else (tmpc, tmpd)
                    step(V.tensor_tensor(t1[:], p1, f1, ALU.mult), linked=False)
                    step(V.tensor_tensor(t2[:], p2, f2, ALU.mult))
                    step(V.tensor_tensor(dst, t1[:], t2[:], op), linked=part == 5)

            def largest(n):
                v.wait_ge(a_exp.sem, a_exp.done(n))
                v.wait_ge(s_most.sem, s_most.at(n, 1))
                V.tensor_tensor(most[:], most[:], beyond[:], ALU.max).then_inc(s_most.sem, 1)

            def g_base(n, fast, h):
                mask = CONST_PARTS["causal" if fast else "ident"][0]
                v.wait_ge(t_g[fast].sem, t_g[fast].at(n, h + 1))
                if h == 0:
                    wait_past(t_y, n)
                V.tensor_tensor(GT[:, h, :, :], bank[4 + h % 2][:].rearrange("p (c t) -> p c t", t=CH),
                                view(const, 0, 128, mask, [[0, NCH], [1, CH]]), ALU.mult).then_inc(s_g[fast].sem, 1)

            def level_arg(n, k, m):
                nb = T // (2 * m)
                V.tensor_tensor(view(arg, 0, 128, 0, [[2 * m, nb], [m, 2], [1, m]]),
                                view(cum3, 0, 128, T, [[2 * m, nb], [T + m, 2], [1, m]]),
                                view(cum3, 0, 128, m - 1, [[2 * m, nb], [T, 2], [0, m]]), ALU.add).then_inc(s_lvarg.sem, 1)

            def level_mul(n, k, m):
                nb = T // (2 * m)
                v.wait_ge(a_lv.sem, a_lv.at(n, k + 1))
                e = view(E, 0, 128, 0, [[2 * m, nb], [m, 2], [1, m]])
                for dst, src in ((Wre, Xre), (Wim, Xim)):
                    V.tensor_tensor(view(dst, 0, 128, 0, [[2 * m, nb], [m, 2], [1, m]]),
                                    view(src, 0, 128, 0, [[2 * m, nb], [T + m, 2], [1, m]]), e, ALU.mult).then_inc(s_lvmul.sem, 1)

            def level_take(n, k, m, step):
                m0 = CONST_PARTS[f"level{m}"][0]
                nb = CH // (2 * m)
                for h in range(HEADS):
                    v.wait_ge(t_g[False].sem, t_g[False].at(n, HEADS * (1 + k) + h + 1))
                    step(V.memset(carrier[:, 1:2], 0.0), linked=False)
                    dst = view(GT, 0, 128, h * T + m, [[CH, NCH], [2 * m, nb], [1, m]])
                    mask = view(const, 0, 128, m0, [[0, NCH], [1, CH // 2]]).bitcast(I32)
                    src = bank[4 + h % 2][:, 0:T // 2].rearrange("p (c t) -> p c t", t=CH // 2)
                    step(V.copy_predicated(dst, mask, src))

            def state(n, fast, c):
                step = chain(s_st[fast], n)
                heads = view(const, 0, 128, CONST_PARTS["heads"][0], [[0, 2], [1, INNER]])
                v.wait_ge(t_s[fast].sem, t_s[fast].at(n, c + 1))
                new, old = Sst[c % 3], Sst[(c - 1) % 3]
                ps = bank[4][:].rearrange("p (r e) -> p r e", r=2)
                if fast:
                    step.count[0] = c
                    step(V.tensor_tensor(new[:], ps, heads, ALU.mult), linked=False)
                    return
                step.count[0] = 2 * c
                if c:
                    step(V.tensor_tensor(stmp[:], ps, heads, ALU.mult))
                    step(V.scalar_tensor_tensor(new[:], old[:], aend[:, c:c + 1], stmp[:], ALU.mult, ALU.add))
                else:
                    step(V.tensor_tensor(new[:], ps, heads, ALU.mult), by=2)

            def gated(n):
                step = chain(s_gate, n)
                v.wait_ge(s_dx.sem, s_dx.done(n))
                for half in range(2):
                    v.wait_ge(t_y.sem, t_y.at(n, half + 1))
                    w = slice(2 * half, 2 * half + 2)
                    step(V.tensor_tensor(y1[:, w, :], dx[:, w, :], bank[6 + half][:].rearrange("p (c e) -> p c e", e=INNER), ALU.add))
                    step(V.tensor_tensor(g2[:, w, :], y1[:, w, :], z2[:, w, :], ALU.mult), linked=False)

            def low_half(sig, high, lo, ready, n, f):
                v.wait_ge(ready.sem, ready.at(n, f + 1))
                V.scalar_tensor_tensor(lo[:, f, :], bank[4 + f % 2][:], 0.0, high[:, f, :], ALU.max, ALU.subtract).then_inc(sig.sem, 1)

            def add_mlp(n, p):
                v.wait_ge(t_mo.sem, t_mo.done(n))
                V.scalar_tensor_tensor(o1[:].rearrange("p c d -> p (c d)"), bank[7][:], sffn[:, 0:1],
                                       xtok[p][:].rearrange("p c d -> p (c d)"), ALU.mult, ALU.add).then_inc(s_mo.sem, 1)

            def final(n, p, stored):
                v.wait_ge(o_out[p], stored)
                v.wait_ge(t_o.sem, t_o.done(n))
                v.wait_ge(s_rms.sem, s_rms.done(n))
                v.wait_ge(s_mo.sem, s_mo.done(n))
                for c in range(NCH):
                    V.scalar_tensor_tensor(osb[p][:, c, :], bank[6][:, 128 * c:128 * c + 128], rms[:, c:c + 1],
                                           o1[:, c, :], ALU.mult, ALU.add).then_inc(s_fin.sem, 1)

            def front(n, p, fast, ahead=None):
                for f in range(MT):
                    low_half(s_h0l, h0h, h0l, a_h0, n, f)
                if fast:
                    decayed(n, fast, 0)
                    decayed(n, fast, 1)
                for f in range(MT):
                    low_half(s_h1l, h1h, h1l, a_h1, n, f)
                    if fast:
                        decayed(n, fast, 2 + f)
                if not fast:
                    for part in range(6):
                        decayed(n, fast, part)

            def pipelined(n, p, pq, loaded, stored, has_back, has_front, next_loaded):
                if has_back:
                    g_base(n - 1, True, 0)
                    g_base(n - 1, True, 1)
                if has_front:
                    xn_low(n)
                    dt_steps(n)
                if has_back:
                    g_base(n - 1, True, 2)
                    g_base(n - 1, True, 3)
                    state(n - 1, True, 0)
                if has_front:
                    silu_x(n)
                if has_back:
                    state(n - 1, True, 1)
                if has_front:
                    silu_bc(n)
                if has_back:
                    state(n - 1, True, 2)
                    gated(n - 1)
                if has_front:
                    silu_z(n)
                    phases(n, True)
                    x_times_dt(n)
                    b_and_c(n)
                if has_back:
                    final(n - 1, pq, stored)
                if has_front:
                    front(n, p, True)
                    add_mlp(n, p)
                    largest(n)
                if next_loaded is not None:
                    layernorm(n + 1, 1 - p, next_loaded)
                    normalised(n + 1, 1 - p)

            layernorm(0, 0, 16)
            normalised(0, 0)
            pipelined(0, 0, 1, 16, None, False, True, 16)
            with v.Fori(0, SEQS // 2 - 1) as i:
                pipelined(2 * i + 1, 1, 0, None, 16 * i + 1, True, True, 16 * i + 32)
                pipelined(2 * i + 2, 0, 1, None, 16 * i + 1, True, True, 16 * i + 32)
            last = SEQS // 2 - 1
            pipelined(SEQS - 1, 1, 0, None, 16 * last + 1, True, True, None)
            pipelined(SEQS, 0, 1, None, 16 * last + 1, True, False, None)

            v.wait_ge(set_pe, 2)
            V.tensor_reduce(top[:], bank[0][0:1, 0:128], AX_X, ALU.max).then_inc(flag_top, 1)
            v.wait_ge(flag_top, 1)
            V.tensor_scalar(above[:], top[:], 0.0, None, ALU.is_gt).then_inc(flag_top, 1)
            v.wait_ge(flag_top, 2)
            V.tensor_copy(again[:], above[:]).then_inc(flag_ready, 1)
            flag = general_needed(v)
            with nc.If(flag > 0):
                with v.Fori(0, SEQS // 2) as i:
                    for p in range(2):
                        n = SEQS + 2 * i + p
                        layernorm(n, p, 16 * i + 16 * (SEQS // 2) + 16)
                        normalised(n, p)
                        xn_low(n)
                        dt_steps(n)
                        silu_x(n)
                        silu_bc(n)
                        silu_z(n)
                        phases(n, False)
                        x_times_dt(n)
                        k_exponents(n)
                        b_and_c(n)
                        front(n, p, False)
                        add_mlp(n, p)
                        for h in range(HEADS):
                            g_base(n, False, h)
                        step = chain(s_g[False], n)
                        step.count[0] = HEADS
                        step.link()
                        for k, m in enumerate(LEVELS):
                            level_arg(n, k, m)
                            level_mul(n, k, m)
                            level_take(n, k, m, step)
                        for c in range(NST[False]):
                            state(n, False, c)
                        gated(n)
                        final(n, p, 16 * i + 16 * (SEQS // 2) + 1)
                v.nop()
            with nc.Else():
                v.nop()
            v.nop()

        @block.scalar
        def _(act):
            A = nc.scalar
            act.wait_ge(weights, 16 * len(loads))
            act.wait_ge(set_dve, 7)

            def step(sig, ins, by=1):
                ins.then_inc(sig.sem, by)

            def xn_t(n):
                act.wait_ge(t_T.sem, t_T.done(n))
                step(a_xnT, A.copy(xnT[:, PAD:PAD + T], bank[0][:]))
                step(a_xnT, A.activation(xh[:], bank[0][:], ACT.Copy, scale=XSCALE))

            def dt_exp(n):
                act.wait_ge(s_dt.sem, s_dt.at(n, 2))
                step(a_dte, A.activation(de[:], dneg[:], ACT.Exp))

            def tanh_lora(n):
                act.wait_ge(t_l1.sem, t_l1.done(n))
                step(a_tanh, A.activation(th1[:], bank[0][0:LORA, :], ACT.Tanh))

            def tanh_x(n):
                act.wait_ge(t_x.sem, t_x.done(n))
                for half in range(2):
                    step(a_tanh, A.activation(thx[:, 2 * half:2 * half + 2, :], bank[2 + half][:], ACT.Tanh, scale=0.5))

            def tanh_bc(n):
                act.wait_ge(t_bc.sem, t_bc.done(n))
                step(a_tanh, A.activation(bcp[:], bank[0][:], ACT.Identity, bias=cb_col[:, 0:1]))
                step(a_tanh, A.activation(thb[:], bank[0][:], ACT.Tanh, bias=hcb[:, 0:1], scale=0.5))

            def tanh_z(n):
                act.wait_ge(t_z.sem, t_z.done(n))
                for half in range(2):
                    step(a_tanh, A.activation(thz[:, 2 * half:2 * half + 2, :], bank[2 + half][:], ACT.Tanh, scale=0.5))

            def theta_square(n):
                act.wait_ge(s_ph.sem, s_ph.at(n, 2))
                step(a_sq, A.activation(sq[:], theta[:], ACT.Square))

            def b_columns(n):
                act.wait_ge(t_bcc.sem, t_bcc.done(n))
                step(a_bc, A.copy(bcol[:], bank[2][:]))

            def trig(n):
                act.wait_ge(s_ph.sem, s_ph.at(n, PHASE_STEPS))
                step(a_abs, A.activation(pabs[:], phl[:], ACT.Abs))
                step(a_trig, A.activation(psn, phl[:], ACT.Sin, scale=TURN))
                act.wait_ge(a_abs.sem, a_abs.done(n))
                step(a_trig, A.activation(pcs, pabs[:], ACT.Sin, scale=-TURN, bias=halfpi[:, 0:1]))

            def decays(n, fast):
                if fast:
                    act.wait_ge(s_ph.sem, s_ph.done(n))
                    step(a_exp, A.activation(E[:], cum3[:, 0, :], ACT.Exp, scale=-1.0))
                else:
                    act.wait_ge(s_tail.sem, s_tail.done(n))
                    step(a_exp, A.activation(E[:], diff[:], ACT.Exp))
                step(a_exp, A.activation(E2[:], cum3[:, 0, :], ACT.Exp))
                if fast:
                    step(a_exp, A.activation(sq[:], cum3[:, 0, :], ACT.Square))
                    act.wait_ge(a_exp.sem, a_exp.at(n, 3))
                    step(a_exp, A.activation(sq[:], sq[:], ACT.Relu, bias=spread[:, 0:1], accum_out=beyond[:]))
                else:
                    step(a_exp, A.activation(aend[:], view(cum3, 0, 128, SUB - 1, [[SUB, NSUB]]), ACT.Exp), by=2)

            def level_exps(n):
                act.wait_ge(s_kq.sem, s_kq.done(n))
                for k in range(NL):
                    act.wait_ge(s_lvarg.sem, s_lvarg.at(n, k + 1))
                    step(a_lv, A.activation(E[:], arg[:], ACT.Exp))

            def mlp_high(sig, ready, hi, n):
                for f in range(MT):
                    act.wait_ge(ready.sem, ready.at(n, f + 1))
                    step(sig, A.activation(hi[:, f, :], bank[4 + f % 2][:], ACT.Relu))

            def kt_copies(n):
                for half in range(2):
                    act.wait_ge(t_kt.sem, t_kt.at(n, half + 1))
                    step(a_kt, A.copy(KT[:, 2 * half:2 * half + 2, :, :], bank[6 + half][:]))

            def squares(n):
                for c in range(NCH):
                    act.wait_ge(s_gate.sem, s_gate.at(n, 2 * (c // 2) + 2))
                    if c:
                        act.wait_ge(a_ssq.sem, a_ssq.at(n, c))
                    step(a_ssq, A.activation(gsq[:], g2[:, c, :], ACT.Square, scale=MEAN, accum_out=ssq[:, c:c + 1]))

            def g_transposed(n):
                act.wait_ge(t_gT.sem, t_gT.done(n))
                for h in range(2):
                    step(a_gT, A.copy(gT[:, h, :], bank[4 + h][:]))

            def pipelined(n, has_back, has_front):
                if has_front:
                    xn_t(n)
                if has_back:
                    kt_copies(n - 1)
                if has_front:
                    dt_exp(n)
                    tanh_lora(n)
                    tanh_x(n)
                    tanh_bc(n)
                if has_back:
                    squares(n - 1)
                if has_front:
                    tanh_z(n)
                if has_back:
                    g_transposed(n - 1)
                if has_front:
                    theta_square(n)
                    b_columns(n)
                    trig(n)
                    decays(n, True)
                    mlp_high(a_h0, t_h0, h0h, n)
                    mlp_high(a_h1, t_h1, h1h, n)

            pipelined(0, False, True)
            with act.Fori(0, SEQS // 2 - 1) as i:
                pipelined(2 * i + 1, True, True)
                pipelined(2 * i + 2, True, True)
            pipelined(SEQS - 1, True, True)
            pipelined(SEQS, True, False)

            flag = general_needed(act)
            with nc.If(flag > 0):
                with act.Fori(0, SEQS // 2) as i:
                    for p in range(2):
                        n = SEQS + 2 * i + p
                        xn_t(n)
                        dt_exp(n)
                        tanh_lora(n)
                        tanh_x(n)
                        tanh_bc(n)
                        tanh_z(n)
                        theta_square(n)
                        b_columns(n)
                        trig(n)
                        decays(n, False)
                        mlp_high(a_h0, t_h0, h0h, n)
                        mlp_high(a_h1, t_h1, h1h, n)
                        kt_copies(n)
                        level_exps(n)
                        squares(n)
                        g_transposed(n)
                act.nop()
            with nc.Else():
                act.nop()
            act.nop()

        @block.gpsimd
        def _(g):
            P = nc.gpsimd
            g.wait_ge(set_dve, SETUP)
            g.wait_ge(weights, 16 * len(loads))

            def rstds(n):
                g.wait_ge(s_ln.sem, s_ln.at(n, 2 * NCH + 2))
                P.tensor_tensor(rstd[:], vare[:], minus_half[:], ALU.pow).then_inc(s_rstd.sem, 1)

            def skip_term(n):
                if not (isinstance(n, int) and n == 0):
                    g.wait_ge(s_gate.sem, s_gate.at(n, 0))
                g.wait_ge(s_silu.sem, s_silu.at(n, 2))
                P.tensor_tensor(dx[:].rearrange("p c (h e) -> p c h e", h=HEADS),
                                x2[:].rearrange("p c (h e) -> p c h e", h=HEADS),
                                view(hskip, 0, 128, 0, [[0, NCH], [1, HEADS], [0, HEAD]]), ALU.mult).then_inc(s_dx.sem, 1)

            def rms_of(n):
                g.wait_ge(a_ssq.sem, a_ssq.done(n))
                P.tensor_tensor(msq[:], ssq[:], eps4[:], ALU.add).then_inc(s_msq.sem, 1)
                g.wait_ge(s_msq.sem, s_msq.done(n))
                P.tensor_tensor(rms[:], msq[:], minus_half[:], ALU.pow).then_inc(s_rms.sem, 1)

            def b_and_k(n):
                def subs(t):
                    return t[:].rearrange("p (c t) -> p c t", t=SUB)

                br = view(be, 0, 128, 0, [[1, NSUB], [0, SUB]])
                bi = view(be, 0, 128, NSUB, [[1, NSUB], [0, SUB]])
                g.wait_ge(s_bc.sem, s_bc.at(n, 1))
                g.wait_ge(s_kq.sem, s_kq.at(n, 2))
                for k, (dst, (p1, f1), (p2, f2), op) in enumerate((
                    (Bre, (Kre, br), (Kim, bi), ALU.add),
                    (Bim, (Kim, br), (Kre, bi), ALU.subtract),
                )):
                    P.tensor_tensor(subs(btmp[0]), subs(p1), f1, ALU.mult).then_inc(s_bk.sem, 1)
                    P.tensor_tensor(subs(btmp[1]), subs(p2), f2, ALU.mult).then_inc(s_bk.sem, 1)
                    g.wait_ge(s_bk.sem, s_bk.at(n, 3 * k + 2))
                    P.tensor_tensor(dst[:], btmp[0][:], btmp[1][:], op).then_inc(s_bk.sem, 1)
                    if k == 0:
                        g.wait_ge(s_bk.sem, s_bk.at(n, 3))

            def pipelined(n, has_back, has_front, has_next):
                if has_back:
                    rms_of(n - 1)
                if has_front:
                    skip_term(n)
                    b_and_k(n)
                if has_next:
                    rstds(n + 1)

            rstds(0)
            pipelined(0, False, True, True)
            with g.Fori(0, SEQS // 2 - 1) as i:
                pipelined(2 * i + 1, True, True, True)
                pipelined(2 * i + 2, True, True, True)
            pipelined(SEQS - 1, True, True, False)
            pipelined(SEQS, True, False, False)

            flag = general_needed(g)
            with nc.If(flag > 0):
                with g.Fori(0, SEQS // 2) as i:
                    for p in range(2):
                        n = SEQS + 2 * i + p
                        rstds(n)
                        skip_term(n)
                        b_and_k(n)
                        rms_of(n)
                g.nop()
            with nc.Else():
                g.nop()
            g.nop()

        @block.tensor
        def _(pe):
            M = nc.tensor
            pe.wait_ge(weights, 16 * len(loads))
            pe.wait_ge(set_dve, 7 + 3 * TAPS)
            for k in range(TAPS):
                for t in range(3):
                    M.transpose(bank[k][:, 128 * t:128 * t + 128], scaled[:, 3 * k + t, :], ident)
            for t in range(2):
                M.transpose(bank[4][:, 128 * t:128 * t + 128], win[:, t, :], ident)
                M.transpose(bank[4][:, 256 + 128 * t:384 + 128 * t], wout[:, 128 * t:128 * t + 128], ident)
            M.transpose(bank[5][:, 0:HEADS], wdt[:], ident[0:HEADS, 0:HEADS]).then_inc(set_pe, 1)
            pe.wait_ge(set_dve, SETUP)

            def wait_past(sig, n):
                if not (isinstance(n, int) and n == 0):
                    pe.wait_ge(sig.sem, sig.at(n, 0))

            def tok(c, k=PAD):
                return xnT[:, k + CH * c:k + CH * c + CH]

            def xn_transposed(n):
                pe.wait_ge(s_ln.sem, s_ln.done(n))
                wait_past(s_kq, n)
                for c in range(NCH):
                    last = M.transpose(bank[0][:, CH * c:CH * c + CH], xn[:, c, :], ident)
                last.then_inc(t_T.sem, 1)

            def dt_products(n):
                pe.wait_ge(a_xnT.sem, a_xnT.at(n, 1))
                for c in range(NCH):
                    last = M.matmul(bank[1][:, HEADS * c:HEADS * c + HEADS], tok(c), DTW[:], start=True, stop=True)
                last.then_inc(t_dt.sem, 1)

            def lora1(n):
                pe.wait_ge(s_xl.sem, s_xl.done(n))
                M.matmul(bank[0][0:LORA, :], tw1[:], xnT[:, PAD:PAD + T], start=True, stop=True).then_inc(t_l1.sem, 1)

            def x_products(n):
                for c in range(NCH):
                    dst = bank[2 + c // 2][:, INNER * (c % 2):INNER * (c % 2) + INNER]
                    for k in range(TAPS):
                        M.matmul(dst, tok(c, k), XW[:, k, :], start=(k == 0), stop=False)
                    last = M.matmul(dst, ones[:], cb_row[:], start=False, stop=True)
                last.then_inc(t_x.sem, 1)

            def bc_products(n):
                pe.wait_ge(a_tanh.sem, a_tanh.at(n, 1))
                for k in range(TAPS):
                    last = M.matmul(bank[0][:], BCW[:, k, :], xnT[:, k:k + T], start=(k == 0), stop=(k == TAPS - 1))
                last.then_inc(t_bc.sem, 1)

            def z_products(n):
                pe.wait_ge(s_silu.sem, s_silu.at(n, 2))
                for c in range(NCH):
                    last = M.matmul(bank[2 + c // 2][:, INNER * (c % 2):INNER * (c % 2) + INNER], tok(c), ZW[:],
                                    start=True, stop=True)
                last.then_inc(t_z.sem, 1)

            def lora2(n):
                pe.wait_ge(s_dt.sem, s_dt.done(n))
                M.matmul(bank[1][:], tw2[:], th1[:], start=True, stop=True).then_inc(t_l2.sem, 1)

            def dt_spread(n):
                pe.wait_ge(a_tanh.sem, a_tanh.at(n, 5))
                for c in range(NCH):
                    last = M.matmul(bank[0][:, CH * c:CH * c + CH], dtb32[:, c, :, :].rearrange("p h k -> p (h k)"), ident,
                                    start=True, stop=True)
                last.then_inc(t_dtr.sem, 1)

            def b_at_ends(n):
                pe.wait_ge(s_silu.sem, s_silu.at(n, 3))
                pe.wait_ge(s_ph.sem, s_ph.at(n, 1))
                last_tokens = view(bc2, 0, 128, SUB - 1, [[SUB, NSUB]])
                M.matmul(bank[1][:, 0:NSUB], c_("bre"), last_tokens, start=True, stop=True)
                M.matmul(bank[1][:, NSUB:2 * NSUB], c_("bim"), last_tokens, start=True, stop=True).then_inc(t_be.sem, 1)

            def bc_columns(n):
                pe.wait_ge(s_silu.sem, s_silu.done(n))
                M.matmul(bank[2][:], c_("bcol"), bc2[:], start=True, stop=True)
                M.matmul(bank[3][:], c_("ccol"), bc2[:], start=True, stop=True).then_inc(t_bcc.sem, 1)

            def bc_spread(n):
                pe.wait_ge(s_bc.sem, s_bc.at(n, 2))
                M.matmul(bank[2][:], c_("cre"), bc2[:], start=True, stop=True)
                M.matmul(bank[3][:], c_("cim"), bc2[:], start=True, stop=True)
                pe.wait_ge(s_ph.sem, s_ph.done(n))
                M.matmul(bank[0][:], c_("cbre"), prod[:], start=True, stop=True)
                M.matmul(bank[1][:], c_("cbim"), prod[:], start=True, stop=True).then_inc(t_sel.sem, 1)

            def mlp0(n):
                for f in range(MT):
                    if f >= 2:
                        pe.wait_ge(s_h0l.sem, s_h0l.at(n, f - 1))
                    elif f == 0:
                        wait_past(a_gT, n)
                    w = W0[:, 128 * f:128 * f + 128]
                    M.matmul(bank[4 + f % 2][:], w, xh[:], start=True, stop=False)
                    M.matmul(bank[4 + f % 2][:], w, xl[:], start=False, stop=True).then_inc(t_h0.sem, 1)

            def mlp1(n):
                pe.wait_ge(s_h0l.sem, s_h0l.done(n))
                for f in range(MT):
                    if f >= 2:
                        pe.wait_ge(s_h1l.sem, s_h1l.at(n, f - 1))
                    for k in range(MT):
                        w = W1[:, k, 128 * f:128 * f + 128]
                        M.matmul(bank[4 + f % 2][:], w, h0h[:, k, :], start=(k == 0), stop=False)
                        last = M.matmul(bank[4 + f % 2][:], w, h0l[:, k, :], start=False, stop=(k == MT - 1))
                    last.then_inc(t_h1.sem, 1)

            def mlp_out(n):
                pe.wait_ge(s_h1l.sem, s_h1l.done(n))
                for c in range(NCH):
                    for k in range(MT):
                        for r, h in enumerate((h1h, h1l)):
                            last = M.matmul(bank[7][:, D * c:D * c + D], h[:, k, CH * c:CH * c + CH], W2[:, k, :],
                                            start=(k == 0 and r == 0), stop=(k == MT - 1 and r == 1))
                last.then_inc(t_mo.sem, 1)

            def g_products(n, fast, h, left, right, off, step_, n_blk, m, then=True):
                width = n_blk * m
                for c in range(NCH):
                    for r in range(2):
                        lt, rt = left[r], right[r]
                        rhs = view(rt[0], 32 * h, 32, rt[1] + CH * c + off, [[step_, n_blk], [1, m]])
                        last = M.matmul(bank[4 + h % 2][:, width * c:width * c + width],
                                        view(lt[0], 32 * h, 32, lt[1] + CH * c, [[1, CH]]), rhs,
                                        start=(r == 0), stop=(r == 1), skip_group_check=True)
                if then:
                    last.then_inc(t_g[fast].sem, 1)

            def g_across(n, h):
                for c in range(NCH):
                    for r, (k, q) in enumerate(((Bre, Qre), (Bim, Qim))):
                        last = M.matmul(bank[4 + h % 2][0:SUB, CH * c + SUB:CH * c + CH],
                                        view(k, 32 * h, 32, CH * c, [[1, SUB]]),
                                        view(q, 32 * h, 32, CH * c + SUB, [[1, SUB]]),
                                        start=(r == 0), stop=(r == 1), skip_group_check=True)
                last.then_inc(t_g[True].sem, 1)

            def k_transposed(n):
                pe.wait_ge(s_bk.sem, s_bk.done(n))
                pe.wait_ge(s_mo.sem, s_mo.done(n))
                wait_past(s_fin, n)
                for c in range(NCH):
                    for r, k in enumerate((Bre, Bim)):
                        q = 2 * c + r
                        last = M.transpose(bank[6 + q // 4][:, 128 * (q % 4):128 * (q % 4) + 128], k[:, CH * c:CH * c + CH], ident)
                    if c % 2:
                        last.then_inc(t_kt.sem, 1)

            def g_head(n, h):
                if h == 0:
                    pe.wait_ge(s_kq.sem, s_kq.done(n))
                    pe.wait_ge(s_bk.sem, s_bk.done(n))
                if h < 2:
                    pe.wait_ge(s_h1l.sem, s_h1l.done(n))
                else:
                    pe.wait_ge(s_g[True].sem, s_g[True].at(n, h - 1))
                g_products(n, True, h, ((Kre, 0), (Kim, 0)), ((Ure, 0), (Uim, 0)), 0, CH, 1, CH, then=False)
                g_across(n, h)

            def within(n, c):
                for h in range(HEADS):
                    last = M.matmul(bank[6 + c // 2][:, INNER * (c % 2) + HEAD * h:INNER * (c % 2) + HEAD * h + HEAD],
                                    GT[:, h, c, :], xd[:, c, HEAD * h:HEAD * h + HEAD],
                                    start=(c % 2 == 0 and h == 0), stop=True, skip_group_check=True)
                return last

            def new_state(n, fast, j):
                c, lo, size = (j, 0, CH) if fast else (j // 2, SUB * (j % 2), SUB)
                if j:
                    pe.wait_ge(s_st[fast].sem, s_st[fast].at(n, j if fast else 2 * j))
                for r in range(2):
                    last = M.matmul(bank[4][:, INNER * r:INNER * r + INNER], view(KT, lo, size, 256 * c + 128 * r, [[1, 128]]),
                                    view(xd, lo, size, INNER * c, [[1, INNER]]),
                                    start=(not fast or (j == 0 and r == 0)), stop=True, skip_group_check=True)
                last.then_inc(t_s[fast].sem, 1)

            def from_state(n, fast, j):
                c, lo, size = (j, 0, CH) if fast else (j // 2, SUB * (j % 2), SUB)
                pe.wait_ge(s_st[fast].sem, s_st[fast].at(n, j if fast else 2 * j))
                for r, q in enumerate((Qre, Qim)):
                    last = M.matmul(bank[6 + c // 2][lo:lo + size, INNER * (c % 2):INNER * (c % 2) + INNER],
                                    q[:, CH * c + lo:CH * c + lo + size], Sst[(j - 1) % 3][:, r, :],
                                    start=False, stop=True, skip_group_check=True)
                return last

            def y_wait(n, fast):
                pe.wait_ge(a_kt.sem, a_kt.done(n))
                pe.wait_ge(s_g[fast].sem, s_g[fast].done(n))
                pe.wait_ge(s_xd.sem, s_xd.done(n))

            def g_t(n):
                pe.wait_ge(s_gate.sem, s_gate.done(n))
                for h in range(2):
                    for c in range(NCH):
                        last = M.transpose(bank[4 + h][:, CH * c:CH * c + CH], g2[:, c, 128 * h:128 * h + 128], ident)
                last.then_inc(t_gT.sem, 1)

            def out_products(n):
                pe.wait_ge(a_gT.sem, a_gT.done(n))
                for c in range(NCH):
                    for h in range(2):
                        last = M.matmul(bank[6][:, D * c:D * c + D], gT[:, h, CH * c:CH * c + CH], OW[:, h, :],
                                        start=(h == 0), stop=(h == 1))
                last.then_inc(t_o.sem, 1)

            def pipelined(n, has_back, has_front):
                b = n - 1
                if has_back:
                    k_transposed(b)
                    g_head(b, 0)
                    g_head(b, 1)
                if has_front:
                    xn_transposed(n)
                    dt_products(n)
                if has_back:
                    g_head(b, 2)
                    g_head(b, 3)
                if has_front:
                    lora1(n)
                    x_products(n)
                if has_back:
                    y_wait(b, True)
                    new_state(b, True, 0)
                    within(b, 0)
                    within(b, 1)
                    new_state(b, True, 1)
                    from_state(b, True, 1).then_inc(t_y.sem, 1)
                if has_front:
                    bc_products(n)
                if has_back:
                    new_state(b, True, 2)
                    within(b, 2)
                    within(b, 3)
                    from_state(b, True, 2)
                    from_state(b, True, 3).then_inc(t_y.sem, 1)
                if has_front:
                    z_products(n)
                    lora2(n)
                    dt_spread(n)
                if has_back:
                    g_t(b)
                    out_products(b)
                if has_front:
                    b_at_ends(n)
                    bc_columns(n)
                    bc_spread(n)
                    mlp0(n)
                    mlp1(n)
                    mlp_out(n)

            pipelined(0, False, True)
            with pe.Fori(0, SEQS // 2 - 1) as i:
                pipelined(2 * i + 1, True, True)
                pipelined(2 * i + 2, True, True)
            pipelined(SEQS - 1, True, True)
            pipelined(SEQS, True, False)

            pe.wait_ge(s_most.sem, s_most.done(SEQS - 1) + 1)
            M.transpose(bank[0][0:1, 0:128], most[:], ident).then_inc(set_pe, 1)

            flag = general_needed(pe)
            with nc.If(flag > 0):
                with pe.Fori(0, SEQS // 2) as i:
                    for p in range(2):
                        n = SEQS + 2 * i + p
                        xn_transposed(n)
                        dt_products(n)
                        lora1(n)
                        x_products(n)
                        bc_products(n)
                        z_products(n)
                        lora2(n)
                        dt_spread(n)
                        b_at_ends(n)
                        bc_columns(n)
                        bc_spread(n)
                        mlp0(n)
                        mlp1(n)
                        mlp_out(n)
                        k_transposed(n)
                        for h in range(HEADS):
                            if h == 0:
                                pe.wait_ge(s_kq.sem, s_kq.done(n))
                            if h < 2:
                                pe.wait_ge(s_h1l.sem, s_h1l.done(n))
                            else:
                                pe.wait_ge(s_g[False].sem, s_g[False].at(n, h - 1))
                            g_products(n, False, h, ((Xre, 0), (Xim, 0)), ((Xre, T), (Xim, T)), 0, CH, 1, CH)
                        for k, m in enumerate(LEVELS):
                            pe.wait_ge(s_lvmul.sem, s_lvmul.at(n, 2 * k + 2))
                            for h in range(HEADS):
                                before = HEADS * k + h - 2
                                at = HEADS + 2 * (before + 1) if before >= 0 else h + 3
                                pe.wait_ge(s_g[False].sem, s_g[False].at(n, at))
                                g_products(n, False, h, ((Wre, 0), (Wim, 0)), ((Wre, 0), (Wim, 0)), m, 2 * m, CH // (2 * m), m)
                        y_wait(n, False)
                        for j in range(NSUB):
                            if j < NST[False]:
                                new_state(n, False, j)
                            if j % 2 == 0:
                                last = within(n, j // 2)
                            if j:
                                last = from_state(n, False, j)
                            if j % 4 == 3:
                                last.then_inc(t_y.sem, 1)
                        g_t(n)
                        out_products(n)
                pe.nop()
            with nc.Else():
                pe.nop()
            pe.nop()


_NAMES = ["x", "in_proj_w", "conv_w", "conv_b", "dt_bias", "lambda_base", "theta_base", "theta_w1", "theta_w2",
          "viscosity_eta", "D", "norm_w", "out_proj_w"]
_FFN = ["k0", "k1", "k2", "s0", "s1", "s2"]


def kernel(**inputs):
    import numpy as _np
    import concourse.bacc as _bacc
    from concourse import mybir as _mybir
    from concourse.bass_utils import run_bass_kernel_spmd as _run

    nc = _bacc.Bacc("TRN2", target_bir_lowering=False, num_devices=1)
    arrays, args = {}, {}
    for name in _NAMES + _FFN:
        full = ("L0_ffn_" if name in _FFN else "L0_attn_") + name
        arr = _np.ascontiguousarray(inputs[full])
        arr = arr.reshape(arr.shape or (1,))
        arrays[f"in_{name}"] = arr
        args[name] = nc.dram_tensor(f"in_{name}", arr.shape, _mybir.dt.from_np(arr.dtype), kind="ExternalInput").ap()
    arrays["constants"] = CONSTANTS
    consts = nc.dram_tensor("constants", CONSTANTS.shape, F32, kind="ExternalInput").ap()
    out = nc.dram_tensor("out", (SEQS, T, D), F32, kind="ExternalOutput").ap()
    build(nc, args, consts, out)
    r = _run(nc, [arrays], core_ids=[0])
    return r.results[0]["out"]
```

```python
import math
from contextlib import ExitStack

import numpy as np

import concourse.bass as bass
from concourse import mybir

ALU = mybir.AluOpType
ACT = mybir.ActivationFunctionType
AX_X = mybir.AxisListType.X
F32 = mybir.dt.float32
F16 = mybir.dt.float16
U8 = mybir.dt.uint8
I32 = mybir.dt.int32

SEQS, T, D = 8, 512, 128
INNER, HEADS, HEAD, BLK = 256, 4, 64, 32
STATE = 2 * BLK
TAPS = 4
LORA = 48
CH = 128
NCH = T // CH
MLP = 512
MT = MLP // 128
EPS = 1e-5
CLIP = math.pi / 2
XSCALE = 16.0
WSCALE = 256.0
BCSCALE = 16.0
PS = XSCALE * WSCALE
BIAS_SCALE = 64.0
SUB = 64
NSUB = T // SUB
LEVELS = [1, 2, 4, 8, 16, 32]
SAFE = 40.0
SPREAD = 0.999 * SAFE ** 2
MEAN = 1 / (2 * PS * math.sqrt(INNER))
ROUND = 1.5 * 2.0 ** 23
SETUP_PROJECTIONS = 45
SETUP = 65
TURN = 6.2831850
PHASE_STEPS = 10
LOG1P_TERMS = 9


def view(t, part, parts, offset, dims):
    pitch = t[:].ap[0][0]
    return bass.AP(t, part * pitch + offset, [[pitch, parts], *dims])


CONST_PARTS = {}


def constants():
    p = np.arange(128)
    parts = {}
    parts["ident"] = np.eye(128)
    s_, t_ = p[:, None], p[None, :]
    parts["causal"] = (s_ <= t_) * 1.0
    parts["restart"] = np.tile((np.arange(T) % SUB != 0) * 1.0, (128, 1))
    bre, bim, cre, cim = 0, 1, STATE, STATE + 1
    for name, row in (("bre", bre), ("bim", bim), ("cre", cre), ("cim", cim)):
        sel = np.zeros((128, 128))
        for col in range(128):
            sel[row + 2 * (col % BLK), col] = 0.5 / BCSCALE
        parts[name] = sel
    parts["heads"] = (p[:, None] // BLK == np.arange(INNER)[None, :] // HEAD) * 1.0
    for m in LEVELS:
        t = np.array([a + m + i for a in range(0, CH, 2 * m) for i in range(m)])
        parts[f"level{m}"] = ((p[:, None] // (2 * m) == t[None, :] // (2 * m)) & (p[:, None] % (2 * m) < m)) * 1.0
    at = 0
    for name, a in parts.items():
        CONST_PARTS[name] = (at, at + a.shape[1])
        at += a.shape[1]
    return np.concatenate(list(parts.values()), 1).astype(np.float32)


CONSTANTS = constants()


class Signal:

    def __init__(self, ctx, nc, name, steps):
        self.sem = ctx.enter_context(nc.semaphore(name))
        self.steps = steps

    def at(self, n, step):
        return n * self.steps + step

    def done(self, n):
        return n * self.steps + self.steps


class Level(Signal):

    def at(self, n, step):
        return (n - SEQS) * self.steps + step

    def done(self, n):
        return (n - SEQS) * self.steps + self.steps


def build(nc, a, consts, out):
    ctx = ExitStack()
    with ctx:
        def sb(name, shape, dt=F32):
            return ctx.enter_context(nc.sbuf_tensor(name, shape, dt))

        def sem(name):
            return ctx.enter_context(nc.semaphore(name))

        def signal(name, steps):
            return Signal(ctx, nc, name, steps)

        bank = [ctx.enter_context(nc.psum_tensor(f"bank{i}", [128, 512], F32)) for i in range(8)]

        gbank = [bank[4 + h % 2] for h in range(HEADS)]

        const = sb("const", [128, CONSTANTS.shape[1]])

        def c_(name):
            lo, hi = CONST_PARTS[name]
            return const[:, lo:hi]

        ident = c_("ident")
        sel_at = {name: 128 * k for k, name in enumerate(("bre", "bim", "cre", "cim"))}
        wdt = sb("wdt", [HEADS, D])
        wout = sb("wout", [128, INNER])
        cw = sb("cw", [128, 3, TAPS])
        cb_row = sb("cb_row", [1, INNER])
        cb_col = sb("cb_col", [128, 1])
        dtb = sb("dtb", [128, HEADS])
        skip = sb("skip", [128, HEADS])
        lam = sb("lam", [128, 1])
        base = sb("base", [128, 1])
        eta = sb("eta", [128, 1])
        normw = sb("normw", [128, 2])
        tw1 = sb("tw1", [128, LORA])
        tw2 = sb("tw2", [LORA, 128])
        k0u = sb("k0u", [128, 2, MLP], U8)
        k1u = sb("k1u", [128, MT, MLP], U8)
        k2u = sb("k2u", [128, MT, D], U8)
        s012 = sb("s012", [128, 3])
        XW = [sb(f"XW{k}", [128, TAPS, INNER], F16) for k in range(2)]
        BCW = [sb(f"BCW{k}", [128, TAPS, 128], F16) for k in range(2)]
        ZW = [sb(f"ZW{k}", [128, INNER], F16) for k in range(2)]
        TW1 = [sb(f"TW1{k}", [128, LORA], F16) for k in range(2)]
        DTW = [sb(f"DTW{k}", [128, HEADS], F16) for k in range(2)]
        CB = sb("CB", [BLK + 1, INNER], F16)
        OW = sb("OW", [128, 2, D])
        W0 = sb("W0", [128, MLP], F16)
        W1 = sb("W1", [128, MT, MLP], F16)
        W2 = sb("W2", [128, MT, D], F16)
        sign = sb("sign", [128, 3])
        negs = sb("negs", [128, 3])
        abss = sb("abss", [128, 3])
        w1s = sb("w1s", [128, 2])
        w0s = sb("w0s", [128, 1])
        sffn = sb("sffn", [128, 1])
        neglam = sb("neglam", [128, 1])
        negeta = sb("negeta", [128, 1])
        hcb = sb("hcb", [128, 1])
        hskip = sb("hskip", [128, HEADS])
        halfpi = sb("halfpi", [128, 1])
        minus_half = sb("minus_half", [128, NCH])
        eps4 = sb("eps4", [128, NCH])
        carrier = sb("carrier", [128, 2])
        biasrow = sb("biasrow", [BLK + 1, 128], F16)

        xtok = [sb(f"xtok{p}", [128, NCH, D]) for p in range(2)]
        osb = [sb(f"osb{p}", [128, NCH, D]) for p in range(2)]
        st6 = sb("st6", [128, NCH, 6])
        mv = sb("mv", [128, NCH, 2])
        vare = sb("vare", [128, NCH])
        rstd = sb("rstd", [128, NCH])
        xn = sb("xn", [128, NCH, D])
        PAD = TAPS - 1
        xh = sb("xh", [128, PAD + T], F16)
        xl = sb("xl", [128, PAD + T], F16)
        th1 = sb("th1", [LORA, T])
        x2 = sb("x2", [128, NCH, INNER])
        thx = sb("thx", [128, NCH, INNER])
        z2s = [sb(f"z2{p}", [128, NCH, INNER]) for p in range(2)]
        thz = sb("thz", [128, NCH, INNER])
        bcp = sb("bcp", [128, T])
        thb = sb("thb", [128, T])
        bc2 = sb("bc2", [128, T])
        bch = sb("bch", [128, T], F16)
        bcl = sb("bcl", [128, T], F16)
        sel = sb("sel", [128, 4 * 128], F16)
        dv = sb("dv", [128, NCH, HEADS])
        dneg = sb("dneg", [128, NCH, HEADS])
        de = sb("de", [128, NCH, HEADS])
        ds = sb("ds", [128, NCH, HEADS])
        dq = sb("dq", [128, NCH, HEADS])
        dacc = sb("dacc", [128, NCH, HEADS])
        dt = sb("dt", [128, NCH, HEADS])
        hdt = sb("hdt", [128, NCH, HEADS])
        dtb32 = sb("dtb32", [128, NCH, HEADS, BLK])
        xd = sb("xd", [128, NCH, INNER])
        theta = sb("theta", [128, T])
        sq = sb("sq", [128, T])
        nl = sb("nl", [128, T])
        lz = sb("lz", [128, T])
        ph = sb("ph", [128, T])
        cum3 = sb("cum3", [128, 3, T])
        phl = sb("phl", [128, T])
        pend = sb("pend", [128, NSUB])
        pint = sb("pint", [128, NSUB])
        poff = sb("poff", [128, NSUB])
        pabs = sb("pabs", [128, T])
        Xre = sb("Xre", [128, 2, T])
        Xim = sb("Xim", [128, 2, T])
        pcs, psn = Xre[:, 0, :], Xim[:, 0, :]
        bres = sb("bres", [128, T])
        bims = sb("bims", [128, T])
        cres, cims = thb, bcp
        cbre = sb("cbre", [128, T])
        cbim = bc2
        ec = sb("ec", [128, T])
        es = sb("es", [128, T])
        btmp = [sb(f"btmp{k}", [128, T]) for k in range(2)]
        tmpa = sb("tmpa", [128, T])
        tmpb = sb("tmpb", [128, T])
        E = sb("E", [128, T])
        E2 = sb("E2", [128, T])
        aend = sb("aend", [128, NSUB])
        Kre = sb("Kre", [128, T])
        Kim = sb("Kim", [128, T])
        Qre = sb("Qre", [128, T])
        Qim = sb("Qim", [128, T])
        Bre = sb("Bre", [128, T])
        Bim = sb("Bim", [128, T])
        Ure = sb("Ure", [128, T])
        Uim = sb("Uim", [128, T])
        GT = sb("GT", [128, HEADS, NCH, CH])
        scaled = GT[:].rearrange("p h c t -> p (h c) t")
        KT = sb("KT", [128, NCH, 2, 128])
        win = KT[:].rearrange("p c r n -> p (c r) n")[:, 0:5, :]
        w0d = E
        Sst = [sb(f"S{c}", [128, 2, INNER]) for c in range(3)]
        stmp = sb("stmp", [128, 2, INNER])
        tmpc, tmpd = stmp[:].rearrange("p r e -> p (r e)"), sb("tmpd", [128, T])[:]
        dx = sb("dx", [128, NCH, INNER])
        y1 = sb("y1", [128, NCH, INNER])
        g2 = sb("g2", [128, NCH, INNER])
        gsq = sb("gsq", [128, INNER])
        ssq = sb("ssq", [128, NCH])
        msq = sb("msq", [128, NCH])
        rms = sb("rms", [128, NCH])
        gT = sb("gT", [128, 2, T])
        o1 = sb("o1", [128, NCH, D])
        h0h = sb("h0h", [128, MT, T], F16)
        h0l = sb("h0l", [128, MT, T], F16)
        h1h = sb("h1h", [128, MT, T], F16)
        h1l = sb("h1l", [128, MT, T], F16)
        diff, arg = tmpa, tmpb
        Wre, Wim = Ure, Uim
        spread = sb("spread", [128, 1])
        beyond = sb("beyond", [128, 1])
        most = sb("most", [128, 1])
        top = sb("top", [1, 1])
        above = sb("above", [1, 1])
        again = sb("again", [1, 1], I32)

        tables = sem("tables_loaded")
        first_weights = sem("projection_weights_loaded")
        weights = sem("other_weights_loaded")
        x_in = [sem(f"x_loaded{p}") for p in range(2)]
        o_out = [sem(f"out_stored{p}") for p in range(2)]
        set_dve = sem("setup_vector")
        set_pe = sem("setup_transposes")
        flag_ready = sem("flag_ready")
        flag_top = sem("flag_top")
        NL = len(LEVELS)
        NST = {True: NCH - 1, False: NSUB - 1}
        s_ln = signal("layernorm", 3 * NCH + 2)
        s_xl = signal("xn_low_half", 1)
        s_dt = signal("dt_steps", 11 + LOG1P_TERMS)
        s_silu = signal("silu", 5)
        s_xd = signal("x_times_dt", 1)
        s_ph = signal("phases", 15)
        s_tail = Level(ctx, nc, "K_exponents", 1)
        s_kq = signal("decayed", 4 + 12)
        s_g = {True: signal("G_in_sbuf", HEADS), False: Level(ctx, nc, "G_in_sbuf_general", HEADS * (1 + 2 * NL))}
        s_lvarg = Level(ctx, nc, "level_exponents", NL)
        s_lvmul = Level(ctx, nc, "level_products", 2 * NL)
        s_st = {True: signal("states", NST[True]), False: Level(ctx, nc, "states_general", 2 * NST[False])}
        s_most = signal("largest_exponents", 1)
        s_gate = signal("gated", 4)
        s_fin = signal("final", NCH)
        s_h0l = signal("h0_low_half", MT)
        s_h1l = signal("h1_low_half", MT)
        s_rstd = signal("rstd", 1)
        s_dx = signal("skip_term", 1)
        s_rms = signal("rms", 1)
        s_msq = signal("mean_squares", 1)
        s_bk = signal("B_K", 6)
        a_xnT = signal("xn_high_half", 1)
        a_tanh = signal("tanhs", 7)
        a_dte = signal("dt_exp", 1)
        a_sq = signal("theta_squared", 1)
        a_trig = signal("sin_cos", 2)
        a_exp = signal("decay_exps", 4)
        a_lv = Level(ctx, nc, "level_exps", NL)
        a_bs = signal("B_copied", 2)
        a_cs = signal("C_copied", 2)
        s_cb = signal("B_times_C", 6)
        t_bs = signal("B_spread", 2)
        t_cs = signal("C_spread", 2)
        a_bch = signal("bc_high_half", 1)
        s_bcl = signal("bc_low_half", 1)
        a_kt = signal("KT_copied", 2)
        s_mo = signal("mlp_added", 1)
        a_ssq = signal("squares", NCH)
        a_gT = signal("gT_copied", 2)
        a_h0 = signal("h0_high_half", MT)
        a_h1 = signal("h1_high_half", MT)
        a_abs = signal("phase_abs", 1)
        t_T = signal("xn_transposed", 1)
        t_dt = signal("dt_projected", 1)
        t_l1 = signal("lora1", 1)
        t_x = signal("x_projected", 2)
        t_bc = signal("bc_projected", 1)
        t_z = signal("z_projected", 1)
        t_l2 = signal("lora2", 1)
        t_dtr = signal("dt_spread", 1)
        t_h0 = signal("mlp0", MT)
        t_h1 = signal("mlp1", MT)
        t_mo = signal("mlp_out", 1)
        t_g = {True: signal("G_products", HEADS), False: Level(ctx, nc, "G_products_general", HEADS * (1 + NL))}
        t_kt = signal("K_transposed", 2)
        t_s = {True: signal("state_products", NST[True]), False: Level(ctx, nc, "state_products_general", NST[False])}
        t_y = signal("y_products", 2)
        t_gT = signal("g_transposed", 1)
        t_o = signal("out_projected", 1)

        x_dram = a["x"].rearrange("b (c p) d -> b p c d", p=128)
        out_dram = out.rearrange("b (c p) d -> b p c d", p=128)

        def col(ap1d, n=128):
            return ap1d.rearrange("(p o) -> p o", o=1)

        def row_all(ap1d, n):
            return bass.AP(ap1d.tensor, ap1d.offset, [[0, 128], [1, n]])

        first_loads = [
            (win, a["in_proj_w"][0:640, :].rearrange("(t p) d -> p t d", p=128)),
            (cw[:], a["conv_w"].rearrange("(t p) k -> p t k", p=128)),
            (wdt[:], a["in_proj_w"][640:644, :]),
            (wout[:], a["out_proj_w"]),
            (cb_row[:], a["conv_b"][0:INNER].rearrange("(o c) -> o c", o=1)),
            (tw1[:], a["theta_w1"]),
        ]
        loads = [
            (cb_col[:], col(a["conv_b"][INNER:INNER + 128])),
            (dtb[:], row_all(a["dt_bias"], HEADS)),
            (skip[:], row_all(a["D"], HEADS)),
            (s012[:, 0:1], row_all(a["s0"], 1)),
            (s012[:, 1:2], row_all(a["s1"], 1)),
            (s012[:, 2:3], row_all(a["s2"], 1)),
            (k0u[:], a["k0"].rearrange("(t p) f -> p t f", p=128)),
            (k1u[:], a["k1"].rearrange("(t p) f -> p t f", p=128)),
            (k2u[:], a["k2"].rearrange("(t p) f -> p t f", p=128)),
            (lam[:], a["lambda_base"].rearrange("h (k o) -> (h k) o", o=1)),
            (base[:], a["theta_base"].rearrange("h (k o) -> (h k) o", o=1)),
            (eta[:], a["viscosity_eta"].rearrange("h (k o) -> (h k) o", o=1)),
            (normw[:], a["norm_w"].rearrange("(t p) -> p t", p=128)),
            (tw2[:], a["theta_w2"]),
        ]
        block = ctx.enter_context(nc.Block())

        tap_bank = [bank[k] for k in (0, 1, 7, 3)]

        def all_ones(n):
            return view(const, 0, 128, CONST_PARTS["causal"][1] - 1, [[0, n]])

        def general_needed(eng):
            eng.wait_ge(flag_ready, 1)
            return eng.value_load(again[0:1, 0:1], min_val=0, max_val=1)

        @block.sync
        def _(sp):
            def load(n, b, p):
                if not (isinstance(n, int) and n < 2):
                    sp.wait_ge(s_mo.sem, s_mo.done(n - 2))
                sp.dma_start(xtok[p][:], x_dram[b]).then_inc(x_in[p], 16)

            def store(n, b, p):
                sp.wait_ge(s_fin.sem, s_fin.done(n))
                sp.dma_start(out_dram[b], osb[p][:]).then_inc(o_out[p], 16)

            with nc.allow_non_contiguous_dma("small columns of weights"):
                load(0, 0, 0)
                sp.dma_start(const[:], consts).then_inc(tables, 16)
                for dst, src in first_loads:
                    sp.dma_start(dst, src).then_inc(first_weights, 16)
                load(1, 1, 1)
                with sp.Fori(0, SEQS // 2 - 1) as i:
                    for p in range(2):
                        load(2 * i + p + 2, 2 * i + p + 2, p)
                        store(2 * i + p, 2 * i + p, p)
                for p in range(2):
                    store(SEQS - 2 + p, SEQS - 2 + p, p)
                for p in range(2):
                    sp.wait_ge(o_out[p], 16 * (SEQS // 2) + 1)
                flag = general_needed(sp)
                with nc.If(flag > 0):
                    with sp.Fori(0, SEQS // 2) as i:
                        for p in range(2):
                            load(SEQS + 2 * i + p, 2 * i + p, p)
                            store(SEQS + 2 * i + p, 2 * i + p, p)
                    for p in range(2):
                        sp.wait_ge(o_out[p], 16 * SEQS + 1)
                    sp.nop()
                with nc.Else():
                    sp.nop()
                sp.nop()

        @block.vector
        def _(v):
            nd = [0]

            def setup(ins, linked=True):
                nd[0] += 1
                ins.then_inc(set_dve, 1)
                if linked:
                    v.wait_ge(set_dve, nd[0])

            V = nc.vector
            for p in range(2):
                V.memset(carrier[:, p:p + 1], 0.0).then_inc(o_out[p], 1)
            V.memset(most[:], 0.0).then_inc(s_most.sem, 1)
            def chain(signal_, n):
                count = [0]

                def step(ins, linked=True, by=1):
                    count[0] += by
                    ins.then_inc(signal_.sem, by)
                    assert count[0] <= signal_.steps
                    if linked:
                        v.wait_ge(signal_.sem, signal_.at(n, count[0]))

                def link(at=None):
                    v.wait_ge(signal_.sem, signal_.at(n, count[0] if at is None else at))

                step.count, step.link = count, link
                return step

            def layernorm(n, p, loaded):
                v.wait_ge(x_in[p], loaded)
                step = chain(s_ln, n)
                for c in range(NCH):
                    step(V.bn_stats(st6[:, c, :], xtok[p][:, c, :]), linked=False)
                step.link()
                step(V.memset(carrier[:, 0:1], 0.0), linked=False)
                for c in range(NCH):
                    step(V.bn_aggr(mv[:, c, :], st6[:, c, :]), linked=c == NCH - 1)
                step(V.tensor_scalar(vare[:], mv[:, :, 1], EPS, None, ALU.add), linked=False)

            def normalised(n, p):
                step = chain(s_ln, n)
                step.count[0] = 2 * NCH + 2
                v.wait_ge(s_rstd.sem, s_rstd.done(n))
                for c in range(NCH):
                    step(V.tensor_scalar(xn[:, c, :], xtok[p][:, c, :], mv[:, c, 0:1], rstd[:, c:c + 1],
                                         ALU.subtract, ALU.mult), linked=False)

            def xn_low(n):
                v.wait_ge(a_xnT.sem, a_xnT.done(n))
                step = chain(s_xl, n)
                step(V.scalar_tensor_tensor(xl[:, PAD:], bank[2][:], XSCALE, xh[:, PAD:], ALU.mult, ALU.subtract), linked=False)

            def dt_steps(n):
                v.wait_ge(t_dt.sem, t_dt.done(n))
                step = chain(s_dt, n)
                ps = bank[3][:, 0:NCH * HEADS].rearrange("p (c h) -> p c h", h=HEADS)
                bias = view(dtb, 0, 128, 0, [[0, NCH], [1, HEADS]])
                step(V.scalar_tensor_tensor(dv[:], ps, 1.0 / PS, bias, ALU.mult, ALU.add))
                step(V.scalar_tensor_tensor(dneg[:], dv[:], -1.0, dv[:], ALU.mult, ALU.min))
                v.wait_ge(a_dte.sem, a_dte.done(n))
                step(V.tensor_scalar(ds[:], de[:], 2.0, None, ALU.add))
                step(V.reciprocal(dq[:], ds[:]))
                step(V.tensor_tensor(ds[:], de[:], dq[:], ALU.mult))
                step(V.tensor_tensor(dq[:], ds[:], ds[:], ALU.mult))
                terms = LOG1P_TERMS
                step(V.tensor_scalar(dacc[:], dq[:], 1.0 / (2 * terms + 1), None, ALU.mult))
                for j in range(terms - 1, 0, -1):
                    step(V.scalar_tensor_tensor(dacc[:], dacc[:], 1.0 / (2 * j + 1), dq[:], ALU.add, ALU.mult))
                step(V.scalar_tensor_tensor(dacc[:], dacc[:], 1.0, ds[:], ALU.add, ALU.mult))
                step(V.tensor_scalar(dv[:], dv[:], 0.0, None, ALU.max))
                step(V.scalar_tensor_tensor(dt[:], dacc[:], 2.0, dv[:], ALU.mult, ALU.add))
                step(V.tensor_scalar(hdt[:], dt[:], 0.5 / PS, None, ALU.mult), linked=False)
                step(V.tensor_copy(dtb32[:], view(dt, 0, 128, 0, [[1, NCH * HEADS], [0, BLK]])))

            def silu_x(n, k):
                half = 1 - k
                v.wait_ge(a_tanh.sem, a_tanh.at(n, 1 + k))
                if k == 0:
                    wait_past(s_dx, n)
                V.scalar_tensor_tensor(x2[:, 2 * half:2 * half + 2, :], thx[:, 2 * half:2 * half + 2, :], 1.0,
                                       bank[6 + half][:], ALU.add, ALU.mult).then_inc(s_silu.sem, 1)

            def silu_bc(n):
                v.wait_ge(a_tanh.sem, a_tanh.at(n, 4))
                V.scalar_tensor_tensor(bc2[:], thb[:], 1.0, bcp[:], ALU.add, ALU.mult).then_inc(s_silu.sem, 1)

            def bc_low(n):
                v.wait_ge(a_bch.sem, a_bch.done(n))
                V.scalar_tensor_tensor(bcl[:], bc2[:], BCSCALE, bch[:], ALU.mult, ALU.subtract).then_inc(s_bcl.sem, 1)

            def silu_z(n, p):
                for half in range(2):
                    v.wait_ge(a_tanh.sem, a_tanh.at(n, 6 + half))
                    V.scalar_tensor_tensor(z2s[p][:, 2 * half:2 * half + 2, :], thz[:, 2 * half:2 * half + 2, :], 1.0,
                                           bank[6 + half][:], ALU.add, ALU.mult).then_inc(s_silu.sem, 1)

            def wait_past(sig, n):
                if not (isinstance(n, int) and n == 0):
                    v.wait_ge(sig.sem, sig.at(n, 0))

            def x_times_dt(n):
                v.wait_ge(s_silu.sem, s_silu.at(n, 2))
                V.tensor_tensor(xd[:].rearrange("p c (h e) -> p (c h) e", h=HEADS),
                                x2[:].rearrange("p c (h e) -> p (c h) e", h=HEADS),
                                view(hdt, 0, 128, 0, [[1, NCH * HEADS], [0, HEAD]]), ALU.mult).then_inc(s_xd.sem, 1)

            def thetas(n):
                step = chain(s_ph, n)
                v.wait_ge(t_l2.sem, t_l2.done(n))
                step(V.tensor_scalar(theta[:], bank[3][:], base[:, 0:1], -CLIP, ALU.add, ALU.max))
                step(V.tensor_scalar(theta[:], theta[:], CLIP, None, ALU.min))

            def phases(n, between=None):
                step = chain(s_ph, n)
                step.count[0] = 2
                v.wait_ge(t_dtr.sem, t_dtr.done(n))
                step(V.scalar_tensor_tensor(ph[:], theta[:], 1.0 / (2 * math.pi), bank[2][:], ALU.mult, ALU.mult))
                step(V.tensor_tensor_scan(phl[:], c_("restart"), ph[:], 0.0, ALU.mult, ALU.add), linked=False)
                if between:
                    between(0)
                step.link()
                ends = view(phl, 0, 128, SUB - 1, [[SUB, NSUB]])
                step(V.tensor_scalar(pint[:], ends, ROUND, -ROUND, ALU.add, ALU.add))
                step(V.tensor_tensor(pend[:], ends, pint[:], ALU.subtract))
                step(V.tensor_tensor_scan(poff[:, 1:NSUB], all_ones(NSUB - 1), pend[:, 0:NSUB - 1], 0.0, ALU.mult, ALU.add))
                step(V.tensor_tensor(phl[:].rearrange("p (c t) -> p c t", t=SUB), phl[:].rearrange("p (c t) -> p c t", t=SUB),
                                     view(poff, 0, 128, 0, [[1, NSUB], [0, SUB]]), ALU.add), linked=False)
                if between:
                    between(1)
                step.link()
                step(V.tensor_scalar(ph[:], phl[:], ROUND, -ROUND, ALU.add, ALU.add), linked=False)
                if between:
                    between(2)
                step.link()
                step(V.tensor_tensor(phl[:], phl[:], ph[:], ALU.subtract), linked=False)
                assert step.count[0] == PHASE_STEPS

            def exponents(n, fast, between=None):
                step = chain(s_ph, n)
                step.count[0] = PHASE_STEPS
                v.wait_ge(a_sq.sem, a_sq.done(n))
                step(V.tensor_scalar(nl[:], sq[:], negeta[:, 0:1], neglam[:, 0:1], ALU.mult, ALU.add))
                step(V.tensor_tensor(lz[:], nl[:], bank[2][:], ALU.mult), linked=False)
                if between:
                    between(3)
                step.link()
                if fast:
                    step(V.tensor_tensor_scan(cum3[:, 1, :], all_ones(T), lz[:], 0.0, ALU.mult, ALU.add))
                    step(V.tensor_scalar(cum3[:, 0, :], cum3[:, 1, :], SAFE, -SAFE, ALU.min, ALU.max), by=2)
                else:
                    step(V.tensor_tensor_scan(cum3[:, 0, :], c_("restart"), lz[:], 0.0, ALU.mult, ALU.add))
                    step(V.tensor_scalar(cum3[:, 1, :], cum3[:, 0, :], -1.0, None, ALU.mult))
                    step(V.tensor_copy(cum3[:, 2, :], cum3[:, 0, :]))
                assert step.count[0] == s_ph.steps, step.count

            def k_exponents(n):
                V.tensor_tensor(diff[:].rearrange("p (c t) -> p c t", t=SUB),
                                view(cum3, 0, 128, SUB - 1, [[SUB, NSUB], [0, SUB]]),
                                cum3[:, 1, :].rearrange("p (c t) -> p c t", t=SUB), ALU.add).then_inc(s_tail.sem, 1)

            def decayed(n, fast, part):
                step = chain(s_kq, n)
                ure, uim = (Ure[:], Uim[:]) if fast else (Xre[:, 1, :], Xim[:, 1, :])
                if part == 0:
                    v.wait_ge(a_trig.sem, a_trig.done(n))
                    v.wait_ge(a_exp.sem, a_exp.at(n, 1))
                    step(V.tensor_tensor(Kre[:], pcs, E[:], ALU.mult), linked=False)
                    step(V.tensor_tensor(Kim[:], psn, E[:], ALU.mult), linked=False)
                elif part == 1:
                    step.count[0] = 2
                    v.wait_ge(a_exp.sem, a_exp.done(n))
                    step(V.tensor_tensor(ec[:], pcs, E2[:], ALU.mult), linked=False)
                    step(V.tensor_tensor(es[:], psn, E2[:], ALU.mult))
                else:
                    step.count[0] = 3 * part - 2
                    if part == 2:
                        v.wait_ge(s_cb.sem, s_cb.done(n))
                    uc, us = (ec[:], es[:]) if fast else (pcs, psn)
                    dst, (p1, f1), (p2, f2), op = (
                        (ure, (cbre[:], uc), (cbim[:], us), ALU.subtract),
                        (uim, (cbre[:], us), (cbim[:], uc), ALU.add),
                        (Qre[:], (cres[:], ec[:]), (cims[:], es[:]), ALU.subtract),
                        (Qim[:], (cres[:], es[:]), (cims[:], ec[:]), ALU.add),
                    )[part - 2]
                    t1, t2 = (tmpa[:], tmpb[:]) if part % 2 else (tmpc, tmpd)
                    step(V.tensor_tensor(t1, p1, f1, ALU.mult), linked=False)
                    step(V.tensor_tensor(t2, p2, f2, ALU.mult))
                    step(V.tensor_tensor(dst, t1, t2, op), linked=part == 5)

            def largest(n):
                v.wait_ge(a_exp.sem, a_exp.done(n))
                v.wait_ge(s_most.sem, s_most.at(n, 1))
                V.tensor_tensor(most[:], most[:], beyond[:], ALU.max).then_inc(s_most.sem, 1)

            def g_base(n, fast, h):
                mask = CONST_PARTS["causal" if fast else "ident"][0]
                v.wait_ge(t_g[fast].sem, t_g[fast].at(n, h + 1))
                if h == 0:
                    wait_past(t_y, n)
                V.tensor_tensor(GT[:, h, :, :], gbank[h][:].rearrange("p (c t) -> p c t", t=CH),
                                view(const, 0, 128, mask, [[0, NCH], [1, CH]]), ALU.mult).then_inc(s_g[fast].sem, 1)

            def level_arg(n, k, m):
                nb = T // (2 * m)
                V.tensor_tensor(view(arg, 0, 128, 0, [[2 * m, nb], [m, 2], [1, m]]),
                                view(cum3, 0, 128, T, [[2 * m, nb], [T + m, 2], [1, m]]),
                                view(cum3, 0, 128, m - 1, [[2 * m, nb], [T, 2], [0, m]]), ALU.add).then_inc(s_lvarg.sem, 1)

            def level_mul(n, k, m):
                nb = T // (2 * m)
                v.wait_ge(a_lv.sem, a_lv.at(n, k + 1))
                e = view(E, 0, 128, 0, [[2 * m, nb], [m, 2], [1, m]])
                for dst, src in ((Wre, Xre), (Wim, Xim)):
                    V.tensor_tensor(view(dst, 0, 128, 0, [[2 * m, nb], [m, 2], [1, m]]),
                                    view(src, 0, 128, 0, [[2 * m, nb], [T + m, 2], [1, m]]), e, ALU.mult).then_inc(s_lvmul.sem, 1)

            def level_take(n, k, m, step):
                m0 = CONST_PARTS[f"level{m}"][0]
                nb = CH // (2 * m)
                for h in range(HEADS):
                    v.wait_ge(t_g[False].sem, t_g[False].at(n, HEADS * (1 + k) + h + 1))
                    step(V.memset(carrier[:, 1:2], 0.0), linked=False)
                    dst = view(GT, 0, 128, h * T + m, [[CH, NCH], [2 * m, nb], [1, m]])
                    mask = view(const, 0, 128, m0, [[0, NCH], [1, CH // 2]]).bitcast(I32)
                    src = gbank[h][:, 0:T // 2].rearrange("p (c t) -> p c t", t=CH // 2)
                    step(V.copy_predicated(dst, mask, src))

            def state(n, fast, c):
                step = chain(s_st[fast], n)
                heads = view(const, 0, 128, CONST_PARTS["heads"][0], [[0, 2], [1, INNER]])
                v.wait_ge(t_s[fast].sem, t_s[fast].at(n, c + 1))
                new, old = Sst[c % 3], Sst[(c - 1) % 3]
                ps = bank[4][:].rearrange("p (r e) -> p r e", r=2)
                if fast:
                    step.count[0] = c
                    step(V.tensor_tensor(new[:], ps, heads, ALU.mult), linked=False)
                    return
                step.count[0] = 2 * c
                if c:
                    step(V.tensor_tensor(stmp[:], ps, heads, ALU.mult))
                    step(V.scalar_tensor_tensor(new[:], old[:], aend[:, c:c + 1], stmp[:], ALU.mult, ALU.add))
                else:
                    step(V.tensor_tensor(new[:], ps, heads, ALU.mult), by=2)

            def gated(n, p):
                step = chain(s_gate, n)
                v.wait_ge(s_dx.sem, s_dx.done(n))
                for half in range(2):
                    v.wait_ge(t_y.sem, t_y.at(n, half + 1))
                    w = slice(2 * half, 2 * half + 2)
                    step(V.tensor_tensor(y1[:, w, :], dx[:, w, :], bank[6 + half][:].rearrange("p (c e) -> p c e", e=INNER), ALU.add))
                    step(V.tensor_tensor(g2[:, w, :], y1[:, w, :], z2s[p][:, w, :], ALU.mult), linked=False)

            def low_half(sig, high, lo, ready, n, f):
                v.wait_ge(ready.sem, ready.at(n, f + 1))
                V.scalar_tensor_tensor(lo[:, f, :], bank[4 + f % 2][:], 0.0, high[:, f, :], ALU.max, ALU.subtract).then_inc(sig.sem, 1)

            def add_mlp(n, p):
                v.wait_ge(t_mo.sem, t_mo.done(n))
                V.scalar_tensor_tensor(o1[:].rearrange("p c d -> p (c d)"), bank[4][:], sffn[:, 0:1],
                                       xtok[p][:].rearrange("p c d -> p (c d)"), ALU.mult, ALU.add).then_inc(s_mo.sem, 1)

            def final(n, p, stored):
                v.wait_ge(o_out[p], stored)
                v.wait_ge(t_o.sem, t_o.done(n))
                v.wait_ge(s_rms.sem, s_rms.done(n))
                v.wait_ge(s_mo.sem, s_mo.done(n))
                for c in range(NCH):
                    V.scalar_tensor_tensor(osb[p][:, c, :], bank[6][:, 128 * c:128 * c + 128], rms[:, c:c + 1],
                                           o1[:, c, :], ALU.mult, ALU.add).then_inc(s_fin.sem, 1)

            def h0_low(n, f):
                low_half(s_h0l, h0h, h0l, a_h0, n, f)

            def h1_low(n, f):
                low_half(s_h1l, h1h, h1l, a_h1, n, f)

            def pipelined(n, p, pq, stored, has_back, has_front, next_loaded):
                if has_front:
                    silu_x(n, 0)
                    silu_x(n, 1)
                    dt_steps(n)
                    silu_bc(n)
                if has_back:
                    g_base(n - 1, True, 0)
                    g_base(n - 1, True, 1)
                if has_front:
                    bc_low(n)
                    silu_z(n, p)
                    thetas(n)
                    phases(n)
                if has_back:
                    g_base(n - 1, True, 2)
                    g_base(n - 1, True, 3)
                    state(n - 1, True, 0)
                if has_front:
                    exponents(n, True)
                if next_loaded is not None:
                    layernorm(n + 1, 1 - p, next_loaded)
                if has_back:
                    state(n - 1, True, 1)
                if next_loaded is not None:
                    normalised(n + 1, 1 - p)
                if has_back:
                    state(n - 1, True, 2)
                    gated(n - 1, pq)
                if has_front:
                    h0_low(n, 0)
                    h0_low(n, 1)
                    x_times_dt(n)
                    decayed(n, True, 0)
                    h0_low(n, 2)
                    h0_low(n, 3)
                if next_loaded is not None:
                    xn_low(n + 1)
                if has_back:
                    final(n - 1, pq, stored)
                if has_front:
                    decayed(n, True, 1)
                    h1_low(n, 0)
                    decayed(n, True, 2)
                    h1_low(n, 1)
                    decayed(n, True, 3)
                    h1_low(n, 2)
                    decayed(n, True, 4)
                    h1_low(n, 3)
                    decayed(n, True, 5)
                    add_mlp(n, p)
                    largest(n)

            setup(V.memset(xh[:, 0:PAD], 0.0))
            setup(V.memset(xl[:, 0:PAD], 0.0))
            setup(V.memset(CB[:], 0.0))
            setup(V.memset(minus_half[:], -0.5))
            setup(V.memset(halfpi[:], math.pi / 2))
            setup(V.memset(biasrow[:], PS / BIAS_SCALE))
            setup(V.memset(eps4[:], EPS))
            setup(V.memset(spread[:], -SPREAD))
            setup(V.memset(poff[:], 0.0))
            v.wait_ge(tables, 16)
            layernorm(0, 0, 16)
            v.wait_ge(first_weights, 16 * len(first_loads))
            for k in range(TAPS):
                for t in range(3):
                    setup(V.tensor_scalar(scaled[:, 3 * k + t, :], win[:, 2 + t, :], cw[:, t, k:k + 1], None, ALU.mult), False)
            normalised(0, 0)

            def pair(high, low, src, scale=WSCALE):
                setup(V.tensor_scalar(high, src, scale, None, ALU.mult))
                setup(V.scalar_tensor_tensor(low, src, scale, high, ALU.mult, ALU.subtract), False)

            pair(CB[0:1, :], CB[BLK:BLK + 1, :], cb_row[:], BIAS_SCALE)
            pair(TW1[0][:], TW1[1][:], tw1[:])
            v.wait_ge(set_pe, 1)
            for k in range(TAPS):
                pair(XW[0][:, k, :], XW[1][:, k, :], tap_bank[k][:, 0:INNER])
                pair(BCW[0][:, k, :], BCW[1][:, k, :], tap_bank[k][:, INNER:INNER + 128])
            pair(ZW[0][:], ZW[1][:], bank[4][:, 0:INNER])
            pair(DTW[0][:], DTW[1][:], bank[5][:, 0:HEADS])
            assert nd[0] == SETUP_PROJECTIONS, nd
            xn_low(0)
            v.wait_ge(weights, 16 * len(loads))
            setup(V.tensor_scalar(sign[:], s012[:], 0.0, None, ALU.is_gt))
            setup(V.tensor_scalar(negs[:], s012[:], 0.0, None, ALU.is_lt))
            setup(V.tensor_tensor(sign[:], sign[:], negs[:], ALU.subtract))
            setup(V.tensor_tensor(abss[:], sign[:], s012[:], ALU.mult))
            setup(V.tensor_scalar(w0s[:], sign[:, 0:1], 2.0 / XSCALE, None, ALU.mult))
            setup(V.tensor_scalar(w1s[:, 0:1], sign[:, 1:2], 0.5, None, ALU.mult))
            setup(V.tensor_scalar(w1s[:, 1:2], sign[:, 1:2], -0.25, None, ALU.mult))
            setup(V.tensor_tensor(sffn[:], abss[:, 0:1], abss[:, 1:2], ALU.mult))
            setup(V.tensor_scalar(sffn[:], sffn[:], s012[:, 2:3], 16.0, ALU.mult, ALU.mult))
            setup(V.tensor_tensor(w0d[:], k0u[:, 0, :], k0u[:, 1, :], ALU.subtract))
            setup(V.tensor_scalar(W0[:], w0d[:], w0s[:, 0:1], None, ALU.mult))
            setup(V.tensor_scalar(W1[:], k1u[:], w1s[:, 0:1], w1s[:, 1:2], ALU.mult, ALU.add))
            setup(V.tensor_scalar(W2[:], k2u[:], 2.0, -1.0, ALU.mult, ALU.add))
            setup(V.tensor_scalar(neglam[:], lam[:], -1.0, None, ALU.mult))
            setup(V.tensor_scalar(negeta[:], eta[:], -1.0, None, ALU.mult))
            setup(V.tensor_scalar(hcb[:], cb_col[:], 0.5, None, ALU.mult))
            setup(V.tensor_scalar(hskip[:], skip[:], 0.5 / PS, None, ALU.mult))

            for h in range(2):
                setup(V.tensor_scalar(OW[:, h, :], bank[4][:, 256 + 128 * h:384 + 128 * h], normw[:, h:h + 1], 0.5 / PS,
                                      ALU.mult, ALU.mult))

            setup(V.tensor_copy(sel[:], const[:, CONST_PARTS["bre"][0]:CONST_PARTS["cim"][1]]))
            assert nd[0] == SETUP, nd
            v.wait_ge(set_dve, SETUP)
            pipelined(0, 0, 1, None, False, True, 16)
            with v.Fori(0, SEQS // 2 - 1) as i:
                pipelined(2 * i + 1, 1, 0, 16 * i + 1, True, True, 16 * i + 32)
                pipelined(2 * i + 2, 0, 1, 16 * i + 1, True, True, 16 * i + 32)
            last = SEQS // 2 - 1
            pipelined(SEQS - 1, 1, 0, 16 * last + 1, True, True, None)
            pipelined(SEQS, 0, 1, 16 * last + 1, True, False, None)

            v.wait_ge(set_pe, 2)
            V.tensor_reduce(top[:], bank[0][0:1, 0:128], AX_X, ALU.max).then_inc(flag_top, 1)
            v.wait_ge(flag_top, 1)
            V.tensor_scalar(above[:], top[:], 0.0, None, ALU.is_gt).then_inc(flag_top, 1)
            v.wait_ge(flag_top, 2)
            V.tensor_copy(again[:], above[:]).then_inc(flag_ready, 1)
            flag = general_needed(v)
            with nc.If(flag > 0):
                with v.Fori(0, SEQS // 2) as i:
                    for p in range(2):
                        n = SEQS + 2 * i + p
                        layernorm(n, p, 16 * i + 16 * (SEQS // 2) + 16)
                        normalised(n, p)
                        xn_low(n)
                        silu_x(n, 0)
                        silu_x(n, 1)
                        dt_steps(n)
                        silu_bc(n)
                        bc_low(n)
                        silu_z(n, p)
                        thetas(n)
                        x_times_dt(n)
                        phases(n)
                        for f in range(MT):
                            h0_low(n, f)
                        exponents(n, False)
                        k_exponents(n)
                        for f in range(MT):
                            h1_low(n, f)
                        for part in range(6):
                            decayed(n, False, part)
                        add_mlp(n, p)
                        for h in range(HEADS):
                            g_base(n, False, h)
                        step = chain(s_g[False], n)
                        step.count[0] = HEADS
                        step.link()
                        for k, m in enumerate(LEVELS):
                            level_arg(n, k, m)
                            level_mul(n, k, m)
                            level_take(n, k, m, step)
                        for c in range(NST[False]):
                            state(n, False, c)
                        gated(n, p)
                        final(n, p, 16 * i + 16 * (SEQS // 2) + 1)
                v.nop()
            with nc.Else():
                v.nop()
            v.nop()

        @block.scalar
        def _(act):
            A = nc.scalar
            with nc.allow_non_contiguous_dma("small columns of weights"):
                for dst, src in loads:
                    act.dma_start(dst, src).then_inc(weights, 16)
            act.wait_ge(weights, 16 * len(loads))
            act.wait_ge(set_dve, 9)

            def step(sig, ins, by=1):
                ins.then_inc(sig.sem, by)

            def xn_t(n):
                act.wait_ge(t_T.sem, t_T.done(n))
                step(a_xnT, A.activation(xh[:, PAD:], bank[2][:], ACT.Copy, scale=XSCALE))

            def dt_exp(n):
                act.wait_ge(s_dt.sem, s_dt.at(n, 2))
                step(a_dte, A.activation(de[:], dneg[:], ACT.Exp))

            def tanh_lora(n):
                act.wait_ge(t_l1.sem, t_l1.done(n))
                step(a_tanh, A.activation(th1[:], bank[3][0:LORA, :], ACT.Tanh, scale=1 / PS))

            def tanh_x(n, k):
                half = 1 - k
                act.wait_ge(t_x.sem, t_x.at(n, k + 1))
                step(a_tanh, A.activation(thx[:, 2 * half:2 * half + 2, :], bank[6 + half][:], ACT.Tanh, scale=0.5 / PS))

            def tanh_bc(n):
                if not (isinstance(n, int) and n == 0):
                    act.wait_ge(s_kq.sem, s_kq.at(n, 0))
                act.wait_ge(t_bc.sem, t_bc.done(n))
                step(a_tanh, A.activation(bcp[:], bank[2][:], ACT.Identity, bias=cb_col[:, 0:1], scale=1 / PS))
                step(a_tanh, A.activation(thb[:], bank[2][:], ACT.Tanh, bias=hcb[:, 0:1], scale=0.5 / PS))

            def bc_high(n):
                act.wait_ge(s_silu.sem, s_silu.at(n, 3))
                step(a_bch, A.activation(bch[:], bc2[:], ACT.Copy, scale=BCSCALE))

            def tanh_z(n):
                act.wait_ge(t_z.sem, t_z.done(n))
                for half in range(2):
                    step(a_tanh, A.activation(thz[:, 2 * half:2 * half + 2, :], bank[6 + half][:], ACT.Tanh, scale=0.5 / PS))

            def theta_square(n):
                act.wait_ge(s_ph.sem, s_ph.at(n, 2))
                step(a_sq, A.activation(sq[:], theta[:], ACT.Square))

            def b_copies(n):
                for k, dst in enumerate((bres, bims)):
                    act.wait_ge(t_bs.sem, t_bs.at(n, k + 1))
                    step(a_bs, A.copy(dst[:], bank[k][:]))

            def c_copies(n):
                for k, dst in enumerate((cres, cims)):
                    act.wait_ge(t_cs.sem, t_cs.at(n, k + 1))
                    step(a_cs, A.copy(dst[:], bank[k][:]))

            def trig(n):
                act.wait_ge(s_ph.sem, s_ph.at(n, PHASE_STEPS))
                step(a_abs, A.activation(pabs[:], phl[:], ACT.Abs))
                step(a_trig, A.activation(psn, phl[:], ACT.Sin, scale=TURN))
                act.wait_ge(a_abs.sem, a_abs.done(n))
                step(a_trig, A.activation(pcs, pabs[:], ACT.Sin, scale=-TURN, bias=halfpi[:, 0:1]))

            def decays(n, fast):
                if fast:
                    act.wait_ge(s_ph.sem, s_ph.done(n))
                    step(a_exp, A.activation(E[:], cum3[:, 0, :], ACT.Exp, scale=-1.0))
                else:
                    act.wait_ge(s_tail.sem, s_tail.done(n))
                    step(a_exp, A.activation(E[:], diff[:], ACT.Exp))
                step(a_exp, A.activation(E2[:], cum3[:, 0, :], ACT.Exp))
                if fast:
                    step(a_exp, A.activation(sq[:], cum3[:, 0, :], ACT.Square))
                    act.wait_ge(a_exp.sem, a_exp.at(n, 3))
                    step(a_exp, A.activation(sq[:], sq[:], ACT.Relu, bias=spread[:, 0:1], accum_out=beyond[:]))
                else:
                    step(a_exp, A.activation(aend[:], view(cum3, 0, 128, SUB - 1, [[SUB, NSUB]]), ACT.Exp), by=2)

            def level_exps(n):
                act.wait_ge(s_kq.sem, s_kq.done(n))
                for k in range(NL):
                    act.wait_ge(s_lvarg.sem, s_lvarg.at(n, k + 1))
                    step(a_lv, A.activation(E[:], arg[:], ACT.Exp))

            def mlp_high(sig, ready, hi, n, tiles=range(MT)):
                for f in tiles:
                    act.wait_ge(ready.sem, ready.at(n, f + 1))
                    step(sig, A.activation(hi[:, f, :], bank[4 + f % 2][:], ACT.Relu))

            def kt_copies(n):
                for half in range(2):
                    act.wait_ge(t_kt.sem, t_kt.at(n, half + 1))
                    step(a_kt, A.copy(KT[:, 2 * half:2 * half + 2, :, :], bank[half][:]))

            def squares(n):
                for c in range(NCH):
                    act.wait_ge(s_gate.sem, s_gate.at(n, 2 * (c // 2) + 2))
                    if c:
                        act.wait_ge(a_ssq.sem, a_ssq.at(n, c))
                    step(a_ssq, A.activation(gsq[:], g2[:, c, :], ACT.Square, scale=MEAN, accum_out=ssq[:, c:c + 1]))

            def g_transposed(n):
                act.wait_ge(t_gT.sem, t_gT.done(n))
                for h in range(2):
                    step(a_gT, A.copy(gT[:, h, :], bank[2 + h][:]))

            def pipelined(n, has_back, has_front, has_next):
                if has_front:
                    tanh_x(n, 0)
                    tanh_x(n, 1)
                    dt_exp(n)
                    tanh_bc(n)
                    tanh_lora(n)
                if has_back:
                    kt_copies(n - 1)
                if has_front:
                    bc_high(n)
                    tanh_z(n)
                    theta_square(n)
                    b_copies(n)
                    trig(n)
                    c_copies(n)
                    decays(n, True)
                    mlp_high(a_h0, t_h0, h0h, n, (0, 1))
                if has_back:
                    squares(n - 1)
                    g_transposed(n - 1)
                if has_front:
                    mlp_high(a_h0, t_h0, h0h, n, (2, 3))
                if has_next:
                    xn_t(n + 1)
                if has_front:
                    mlp_high(a_h1, t_h1, h1h, n)

            xn_t(0)
            pipelined(0, False, True, True)
            with act.Fori(0, SEQS // 2 - 1) as i:
                pipelined(2 * i + 1, True, True, True)
                pipelined(2 * i + 2, True, True, True)
            pipelined(SEQS - 1, True, True, False)
            pipelined(SEQS, True, False, False)

            flag = general_needed(act)
            with nc.If(flag > 0):
                with act.Fori(0, SEQS // 2) as i:
                    for p in range(2):
                        n = SEQS + 2 * i + p
                        xn_t(n)
                        tanh_x(n, 0)
                        tanh_x(n, 1)
                        dt_exp(n)
                        tanh_bc(n)
                        tanh_lora(n)
                        bc_high(n)
                        tanh_z(n)
                        b_copies(n)
                        c_copies(n)
                        theta_square(n)
                        trig(n)
                        mlp_high(a_h0, t_h0, h0h, n)
                        decays(n, False)
                        mlp_high(a_h1, t_h1, h1h, n)
                        kt_copies(n)
                        level_exps(n)
                        squares(n)
                        g_transposed(n)
                act.nop()
            with nc.Else():
                act.nop()
            act.nop()

        @block.gpsimd
        def _(g):
            P = nc.gpsimd
            g.wait_ge(set_dve, 9)

            def rstds(n):
                g.wait_ge(s_ln.sem, s_ln.at(n, 2 * NCH + 2))
                P.tensor_tensor(rstd[:], vare[:], minus_half[:], ALU.pow).then_inc(s_rstd.sem, 1)

            def skip_term(n):
                if not (isinstance(n, int) and n == 0):
                    g.wait_ge(s_gate.sem, s_gate.at(n, 0))
                g.wait_ge(s_silu.sem, s_silu.at(n, 2))
                P.tensor_tensor(dx[:].rearrange("p c (h e) -> p c h e", h=HEADS),
                                x2[:].rearrange("p c (h e) -> p c h e", h=HEADS),
                                view(hskip, 0, 128, 0, [[0, NCH], [1, HEADS], [0, HEAD]]), ALU.mult).then_inc(s_dx.sem, 1)

            def rms_of(n):
                g.wait_ge(a_ssq.sem, a_ssq.done(n))
                P.tensor_tensor(msq[:], ssq[:], eps4[:], ALU.add).then_inc(s_msq.sem, 1)
                g.wait_ge(s_msq.sem, s_msq.done(n))
                P.tensor_tensor(rms[:], msq[:], minus_half[:], ALU.pow).then_inc(s_rms.sem, 1)

            def b_times_c(n):
                g.wait_ge(a_cs.sem, a_cs.done(n))
                for k, (dst, first, second, op) in enumerate((
                    (cbre, (bres, cres), (bims, cims), ALU.subtract),
                    (cbim, (bres, cims), (bims, cres), ALU.add),
                )):
                    P.tensor_tensor(btmp[0][:], first[0][:], first[1][:], ALU.mult).then_inc(s_cb.sem, 1)
                    P.tensor_tensor(btmp[1][:], second[0][:], second[1][:], ALU.mult).then_inc(s_cb.sem, 1)
                    g.wait_ge(s_cb.sem, s_cb.at(n, 3 * k + 2))
                    P.tensor_tensor(dst[:], btmp[0][:], btmp[1][:], op).then_inc(s_cb.sem, 1)
                    g.wait_ge(s_cb.sem, s_cb.at(n, 3 * k + 3))

            def b_and_k(n):
                def subs(t):
                    return t[:].rearrange("p (c t) -> p c t", t=SUB)

                br, bi = (view(x, 0, 128, SUB - 1, [[SUB, NSUB], [0, SUB]]) for x in (bres, bims))
                g.wait_ge(s_kq.sem, s_kq.at(n, 2))
                for k, (dst, (p1, f1), (p2, f2), op) in enumerate((
                    (Bre, (Kre, br), (Kim, bi), ALU.add),
                    (Bim, (Kim, br), (Kre, bi), ALU.subtract),
                )):
                    P.tensor_tensor(subs(btmp[0]), subs(p1), f1, ALU.mult).then_inc(s_bk.sem, 1)
                    P.tensor_tensor(subs(btmp[1]), subs(p2), f2, ALU.mult).then_inc(s_bk.sem, 1)
                    g.wait_ge(s_bk.sem, s_bk.at(n, 3 * k + 2))
                    P.tensor_tensor(dst[:], btmp[0][:], btmp[1][:], op).then_inc(s_bk.sem, 1)
                    if k == 0:
                        g.wait_ge(s_bk.sem, s_bk.at(n, 3))

            def pipelined(n, has_back, has_front, has_next):
                if has_next:
                    rstds(n + 1)
                if has_front:
                    b_times_c(n)
                    skip_term(n)
                if has_back:
                    rms_of(n - 1)
                if has_front:
                    b_and_k(n)

            rstds(0)
            pipelined(0, False, True, True)
            with g.Fori(0, SEQS // 2 - 1) as i:
                pipelined(2 * i + 1, True, True, True)
                pipelined(2 * i + 2, True, True, True)
            pipelined(SEQS - 1, True, True, False)
            pipelined(SEQS, True, False, False)

            flag = general_needed(g)
            with nc.If(flag > 0):
                with g.Fori(0, SEQS // 2) as i:
                    for p in range(2):
                        n = SEQS + 2 * i + p
                        rstds(n)
                        b_times_c(n)
                        skip_term(n)
                        b_and_k(n)
                        rms_of(n)
                g.nop()
            with nc.Else():
                g.nop()
            g.nop()

        @block.tensor
        def _(pe):
            M = nc.tensor
            pe.wait_ge(tables, 16)
            pe.wait_ge(first_weights, 16 * len(first_loads))
            pe.wait_ge(set_dve, 9 + 3 * TAPS)
            for k in range(TAPS):
                for t in range(3):
                    M.transpose(tap_bank[k][:, 128 * t:128 * t + 128], scaled[:, 3 * k + t, :], ident)
            for t in range(2):
                M.transpose(bank[4][:, 128 * t:128 * t + 128], win[:, t, :], ident)
                M.transpose(bank[4][:, 256 + 128 * t:384 + 128 * t], wout[:, 128 * t:128 * t + 128], ident)
            M.transpose(bank[5][:, 0:HEADS], wdt[:], ident[0:HEADS, 0:HEADS]).then_inc(set_pe, 1)

            def wait_past(sig, n):
                if not (isinstance(n, int) and n == 0):
                    pe.wait_ge(sig.sem, sig.at(n, 0))

            def pairs(w):
                return ((xh, w[0]), (xl, w[0]), (xh, w[1]))

            def tok(x, c, k=PAD):
                return x[:, k + CH * c:k + CH * c + CH]

            def xn_transposed(n):
                pe.wait_ge(s_ln.sem, s_ln.done(n))
                wait_past(s_ph, n)
                if not (isinstance(n, int) and n < 2):
                    pe.wait_ge(a_gT.sem, a_gT.at(n - 1, 0))
                for c in range(NCH):
                    last = M.transpose(bank[2][:, CH * c:CH * c + CH], xn[:, c, :], ident)
                last.then_inc(t_T.sem, 1)

            def dt_products(n):
                if not (isinstance(n, int) and n == 0):
                    pe.wait_ge(s_ph.sem, s_ph.at(n, 0))
                for c in range(NCH):
                    for k, (x, w) in enumerate(pairs(DTW)):
                        last = M.matmul(bank[3][:, HEADS * c:HEADS * c + HEADS], tok(x, c), w[:], start=(k == 0), stop=(k == 2))
                last.then_inc(t_dt.sem, 1)

            def lora1(n):
                pe.wait_ge(s_dt.sem, s_dt.at(n, 1))
                for k, (x, w) in enumerate(pairs(TW1)):
                    last = M.matmul(bank[3][0:LORA, :], w[:], x[:, PAD:], start=(k == 0), stop=(k == 2))
                last.then_inc(t_l1.sem, 1)

            def x_part(n, half, part):
                if part == 0:
                    pe.wait_ge(s_xl.sem, s_xl.done(n))
                    if half == 0 and not (isinstance(n, int) and n < 2):
                        pe.wait_ge(s_fin.sem, s_fin.at(n - 1, 0))
                c, k = 2 * half + part // TAPS, part % TAPS
                dst = bank[6 + half][:, INNER * (c % 2):INNER * (c % 2) + INNER]
                if k == 0:
                    M.matmul(dst, biasrow[:], CB[:], start=True, stop=False)
                for q, (x, w) in enumerate(pairs(XW)):
                    last = M.matmul(dst, tok(x, c, k), w[:, k, :], start=False, stop=(k == TAPS - 1 and q == 2))
                if part == 2 * TAPS - 1:
                    last.then_inc(t_x.sem, 1)

            def x_products(n, half):
                for part in range(2 * TAPS):
                    x_part(n, half, part)

            def bc_products(n):
                for k in range(TAPS):
                    for q, (x, w) in enumerate(pairs(BCW)):
                        last = M.matmul(bank[2][:], w[:, k, :], x[:, k:k + T], start=(k == 0 and q == 0),
                                        stop=(k == TAPS - 1 and q == 2))
                last.then_inc(t_bc.sem, 1)

            def z_part(n, c):
                if c == 0:
                    pe.wait_ge(s_silu.sem, s_silu.at(n, 2))
                for q, (x, w) in enumerate(pairs(ZW)):
                    last = M.matmul(bank[6 + c // 2][:, INNER * (c % 2):INNER * (c % 2) + INNER], tok(x, c), w[:],
                                    start=(q == 0), stop=(q == 2))
                if c == NCH - 1:
                    last.then_inc(t_z.sem, 1)

            def lora2(n):
                pe.wait_ge(a_tanh.sem, a_tanh.at(n, 5))
                M.matmul(bank[3][:], tw2[:], th1[:], start=True, stop=True).then_inc(t_l2.sem, 1)

            def dt_spread(n):
                pe.wait_ge(a_tanh.sem, a_tanh.at(n, 4))
                pe.wait_ge(s_dt.sem, s_dt.done(n))
                for c in range(NCH):
                    last = M.matmul(bank[2][:, CH * c:CH * c + CH], dtb32[:, c, :, :].rearrange("p h k -> p (h k)"), ident,
                                    start=True, stop=True)
                last.then_inc(t_dtr.sem, 1)

            def spread_bc(dst, name):
                w = sel[:, sel_at[name]:sel_at[name] + 128]
                for k, x in enumerate((bch, bcl)):
                    last = M.matmul(dst, w, x[:], start=(k == 0), stop=(k == 1))
                return last

            def b_spread(n, k):
                if k == 0:
                    pe.wait_ge(s_bcl.sem, s_bcl.done(n))
                    wait_past(a_kt, n)
                spread_bc(bank[k][:], ("bre", "bim")[k]).then_inc(t_bs.sem, 1)

            def c_spread(n, k):
                pe.wait_ge(a_bs.sem, a_bs.at(n, k + 1))
                spread_bc(bank[k][:], ("cre", "cim")[k]).then_inc(t_cs.sem, 1)

            def mlp0(n, tiles):
                for f in tiles:
                    if f >= 2:
                        pe.wait_ge(s_h0l.sem, s_h0l.at(n, f - 1))
                    w = W0[:, 128 * f:128 * f + 128]
                    M.matmul(bank[4 + f % 2][:], w, xh[:, PAD:], start=True, stop=False)
                    M.matmul(bank[4 + f % 2][:], w, xl[:, PAD:], start=False, stop=True).then_inc(t_h0.sem, 1)

            def mlp1(n, tiles):
                pe.wait_ge(s_h0l.sem, s_h0l.done(n))
                for f in tiles:
                    if f >= 2:
                        pe.wait_ge(s_h1l.sem, s_h1l.at(n, f - 1))
                    for k in range(MT):
                        w = W1[:, k, 128 * f:128 * f + 128]
                        M.matmul(bank[4 + f % 2][:], w, h0h[:, k, :], start=(k == 0), stop=False)
                        last = M.matmul(bank[4 + f % 2][:], w, h0l[:, k, :], start=False, stop=(k == MT - 1))
                    last.then_inc(t_h1.sem, 1)

            def mlp_out(n):
                pe.wait_ge(s_h1l.sem, s_h1l.done(n))
                for c in range(NCH):
                    for k in range(MT):
                        for r, h in enumerate((h1h, h1l)):
                            last = M.matmul(bank[4][:, D * c:D * c + D], h[:, k, CH * c:CH * c + CH], W2[:, k, :],
                                            start=(k == 0 and r == 0), stop=(k == MT - 1 and r == 1))
                last.then_inc(t_mo.sem, 1)

            def g_products(heads, c, r, left, right, off, step_, n_blk, m, signal_=None):
                width = n_blk * m
                for h in heads:
                    rhs = view(right[0], 32 * h, 32, right[1] + CH * c + off, [[step_, n_blk], [1, m]])
                    last = M.matmul(gbank[h][:, width * c:width * c + width],
                                    view(left[0], 32 * h, 32, left[1] + CH * c, [[1, CH]]), rhs,
                                    start=(r == 0), stop=(r == 1), skip_group_check=True)
                    if signal_ is not None:
                        last.then_inc(signal_.sem, 1)

            def g_across(n, heads, c, r):
                k, q = ((Bre, Qre), (Bim, Qim))[r]
                for h in heads:
                    last = M.matmul(gbank[h][0:SUB, CH * c + SUB:CH * c + CH],
                                    view(k, 32 * h, 32, CH * c, [[1, SUB]]),
                                    view(q, 32 * h, 32, CH * c + SUB, [[1, SUB]]),
                                    start=(r == 0), stop=(r == 1), skip_group_check=True)
                    if c == NCH - 1 and r == 1:
                        last.then_inc(t_g[True].sem, 1)

            def k_transposed(n, c, r):
                if c == 0 and r == 0:
                    pe.wait_ge(s_bk.sem, s_bk.done(n))
                    pe.wait_ge(s_kq.sem, s_kq.done(n))
                q = 2 * c + r
                last = M.transpose(bank[q // 4][:, 128 * (q % 4):128 * (q % 4) + 128],
                                   (Bre, Bim)[r][:, CH * c:CH * c + CH], ident)
                if c % 2 and r:
                    last.then_inc(t_kt.sem, 1)

            def within(n, c):
                for h in range(HEADS):
                    last = M.matmul(bank[6 + c // 2][:, INNER * (c % 2) + HEAD * h:INNER * (c % 2) + HEAD * h + HEAD],
                                    GT[:, h, c, :], xd[:, c, HEAD * h:HEAD * h + HEAD],
                                    start=(c % 2 == 0 and h == 0), stop=True, skip_group_check=True)
                return last

            def new_state(n, fast, j):
                c, lo, size = (j, 0, CH) if fast else (j // 2, SUB * (j % 2), SUB)
                if j:
                    pe.wait_ge(s_st[fast].sem, s_st[fast].at(n, j if fast else 2 * j))
                for r in range(2):
                    last = M.matmul(bank[4][:, INNER * r:INNER * r + INNER], view(KT, lo, size, 256 * c + 128 * r, [[1, 128]]),
                                    view(xd, lo, size, INNER * c, [[1, INNER]]),
                                    start=(not fast or (j == 0 and r == 0)), stop=True, skip_group_check=True)
                last.then_inc(t_s[fast].sem, 1)

            def from_state(n, fast, j):
                c, lo, size = (j, 0, CH) if fast else (j // 2, SUB * (j % 2), SUB)
                pe.wait_ge(s_st[fast].sem, s_st[fast].at(n, j if fast else 2 * j))
                for r, q in enumerate((Qre, Qim)):
                    last = M.matmul(bank[6 + c // 2][lo:lo + size, INNER * (c % 2):INNER * (c % 2) + INNER],
                                    q[:, CH * c + lo:CH * c + lo + size], Sst[(j - 1) % 3][:, r, :],
                                    start=False, stop=True, skip_group_check=True)
                return last

            def y_wait(n, fast, newest):
                pe.wait_ge(s_silu.sem, s_silu.done(newest))
                pe.wait_ge(a_kt.sem, a_kt.done(n))
                pe.wait_ge(s_g[fast].sem, s_g[fast].done(n))
                pe.wait_ge(s_xd.sem, s_xd.done(n))

            def g_t(n, newest):
                pe.wait_ge(s_gate.sem, s_gate.done(n))
                pe.wait_ge(s_ph.sem, s_ph.done(newest))
                for h in range(2):
                    for c in range(NCH):
                        last = M.transpose(bank[2 + h][:, CH * c:CH * c + CH], g2[:, c, 128 * h:128 * h + 128], ident)
                last.then_inc(t_gT.sem, 1)

            def out_products(n):
                pe.wait_ge(a_gT.sem, a_gT.done(n))
                for c in range(NCH):
                    for h in range(2):
                        last = M.matmul(bank[6][:, D * c:D * c + D], gT[:, h, CH * c:CH * c + CH], OW[:, h, :],
                                        start=(h == 0), stop=(h == 1))
                last.then_inc(t_o.sem, 1)

            def pipelined(n, has_back, has_front, has_next):
                b = n - 1
                if has_front:
                    lora1(n)
                for pair_ in ((0, 1), (2, 3)):
                    if has_back:
                        if pair_[0] == 0:
                            pe.wait_ge(s_mo.sem, s_mo.done(b))
                            pe.wait_ge(s_kq.sem, s_kq.done(b))
                        else:
                            pe.wait_ge(s_g[True].sem, s_g[True].at(b, 2))
                        for q in range(2 * NCH):
                            c, r = q // 2, q % 2
                            g_products(pair_, c, r, ((Kre, 0), (Kim, 0))[r], ((Ure, 0), (Uim, 0))[r], 0, CH, 1, CH)
                            if pair_[0] == 0:
                                k_transposed(b, c, r)
                            elif has_front and q == 3:
                                b_spread(n, 0)
                            elif has_front and q == 6:
                                b_spread(n, 1)
                    for q in range(2 * NCH):
                        if has_back:
                            g_across(b, pair_, q // 2, q % 2)
                        if has_front and pair_[0] == 0 and q % 2:
                            z_part(n, q // 2)
                    if has_front and pair_[0] == 0:
                        lora2(n)
                        dt_spread(n)
                if has_front and not has_back:
                    b_spread(n, 0)
                    b_spread(n, 1)
                if has_back:
                    pe.wait_ge(a_kt.sem, a_kt.done(b))
                    pe.wait_ge(s_xd.sem, s_xd.done(b))
                    pe.wait_ge(s_g[True].sem, s_g[True].at(b, 3))
                    new_state(b, True, 0)
                if has_front:
                    c_spread(n, 0)
                if has_back:
                    y_wait(b, True, n if has_front else b)
                    within(b, 0)
                    within(b, 1)
                    new_state(b, True, 1)
                if has_front:
                    c_spread(n, 1)
                if has_back:
                    from_state(b, True, 1).then_inc(t_y.sem, 1)
                    within(b, 2)
                    new_state(b, True, 2)
                    within(b, 3)
                    from_state(b, True, 2)
                    from_state(b, True, 3).then_inc(t_y.sem, 1)
                if has_front:
                    mlp0(n, (0, 1))
                if has_back:
                    g_t(b, n if has_front else b)
                if has_front:
                    mlp0(n, (2, 3))
                if has_back:
                    out_products(b)
                if has_front:
                    if has_next:
                        xn_transposed(n + 1)
                    mlp1(n, (0, 1))
                    if has_next:
                        x_products(n + 1, 1)
                    mlp1(n, (2, 3))
                    if has_next:
                        x_products(n + 1, 0)
                    mlp_out(n)
                    if has_next:
                        dt_products(n + 1)
                        bc_products(n + 1)

            xn_transposed(0)
            pe.wait_ge(set_dve, SETUP_PROJECTIONS)
            x_products(0, 1)
            x_products(0, 0)
            dt_products(0)
            bc_products(0)
            pe.wait_ge(weights, 16 * len(loads))
            pe.wait_ge(set_dve, SETUP)
            pipelined(0, False, True, True)
            with pe.Fori(0, SEQS // 2 - 1) as i:
                pipelined(2 * i + 1, True, True, True)
                pipelined(2 * i + 2, True, True, True)
            pipelined(SEQS - 1, True, True, False)
            pipelined(SEQS, True, False, False)

            pe.wait_ge(s_most.sem, s_most.done(SEQS - 1) + 1)
            M.transpose(bank[0][0:1, 0:128], most[:], ident).then_inc(set_pe, 1)

            flag = general_needed(pe)
            with nc.If(flag > 0):
                with pe.Fori(0, SEQS // 2) as i:
                    for p in range(2):
                        n = SEQS + 2 * i + p
                        xn_transposed(n)
                        x_products(n, 1)
                        x_products(n, 0)
                        dt_products(n)
                        lora1(n)
                        bc_products(n)
                        for c in range(NCH):
                            z_part(n, c)
                        lora2(n)
                        dt_spread(n)
                        for k in range(2):
                            b_spread(n, k)
                        for k in range(2):
                            c_spread(n, k)
                        mlp0(n, range(MT))
                        mlp1(n, range(MT))
                        mlp_out(n)
                        for q in range(2 * NCH):
                            k_transposed(n, q // 2, q % 2)
                        pe.wait_ge(s_mo.sem, s_mo.done(n))
                        made, taken = t_g[False], s_g[False]
                        for pair_ in ((0, 1), (2, 3)):
                            if pair_[0]:
                                pe.wait_ge(taken.sem, taken.at(n, 2))
                            for q in range(2 * NCH):
                                x_ = (Xre, Xim)[q % 2]
                                g_products(pair_, q // 2, q % 2, (x_, 0), (x_, T), 0, CH, 1, CH,
                                           made if q == 2 * NCH - 1 else None)
                        for k, m in enumerate(LEVELS):
                            pe.wait_ge(s_lvmul.sem, s_lvmul.at(n, 2 * k + 2))
                            for pair_ in ((0, 1), (2, 3)):
                                pe.wait_ge(taken.sem, taken.at(n, HEADS * (1 + 2 * k) + 2 * pair_[0]))
                                for q in range(2 * NCH):
                                    w = (Wre, Wim)[q % 2]
                                    g_products(pair_, q // 2, q % 2, (w, 0), (w, 0), m, 2 * m, CH // (2 * m), m,
                                               made if q == 2 * NCH - 1 else None)
                        y_wait(n, False, n)
                        for j in range(NSUB):
                            if j < NST[False]:
                                new_state(n, False, j)
                            if j % 2 == 0:
                                last = within(n, j // 2)
                            if j:
                                last = from_state(n, False, j)
                            if j % 4 == 3:
                                last.then_inc(t_y.sem, 1)
                        g_t(n, n)
                        out_products(n)
                pe.nop()
            with nc.Else():
                pe.nop()
            pe.nop()


_NAMES = ["x", "in_proj_w", "conv_w", "conv_b", "dt_bias", "lambda_base", "theta_base", "theta_w1", "theta_w2",
          "viscosity_eta", "D", "norm_w", "out_proj_w"]
_FFN = ["k0", "k1", "k2", "s0", "s1", "s2"]


def kernel(**inputs):
    import numpy as _np
    import concourse.bacc as _bacc
    from concourse import mybir as _mybir
    from concourse.bass_utils import run_bass_kernel_spmd as _run

    nc = _bacc.Bacc("TRN2", target_bir_lowering=False, num_devices=1)
    arrays, args = {}, {}
    for name in _NAMES + _FFN:
        full = ("L0_ffn_" if name in _FFN else "L0_attn_") + name
        arr = _np.ascontiguousarray(inputs[full])
        arr = arr.reshape(arr.shape or (1,))
        arrays[f"in_{name}"] = arr
        args[name] = nc.dram_tensor(f"in_{name}", arr.shape, _mybir.dt.from_np(arr.dtype), kind="ExternalInput").ap()
    arrays["constants"] = CONSTANTS
    consts = nc.dram_tensor("constants", CONSTANTS.shape, F32, kind="ExternalInput").ap()
    out = nc.dram_tensor("out", (SEQS, T, D), F32, kind="ExternalOutput").ap()
    build(nc, args, consts, out)
    r = _run(nc, [arrays], core_ids=[0])
    return r.results[0]["out"]
```
